# Optimizing a Trainium2 kernel written in Bass

```python
import numpy as np
import jax
import jax.numpy as jnp

def _softmax(x, axis=-1):
    return jax.nn.softmax(x, axis=axis)

def _gelu(x):
    return jax.nn.gelu(x, approximate=True)

def _silu(x):
    return jax.nn.silu(x)

def _sigmoid(x):
    return jax.nn.sigmoid(x)

def _layernorm(x, axis=-1, eps=1e-05):
    m = jnp.mean(x, axis=axis, keepdims=True)
    v = jnp.var(x, axis=axis, keepdims=True)
    return (x - m) / jnp.sqrt(v + eps)

def _scatter_add(tgt, idx, src, axis=0):
    return tgt.at[idx].add(src)

def _segment_sum(src, seg, n):
    return jax.ops.segment_sum(src, seg, n)
kernel_name = 'mk_cond_seq_d2_seqx_r8_354294'

def setup_inputs(seed: int=0):
    np.random.seed(seed)
    _w = jnp.asarray

    def _rec_inputs():
        import jax
        import jax.numpy as jnp
        _rk = jax.random.key(seed)
        x = -0.0002928 + 1 * jax.random.normal(jax.random.fold_in(_rk, 1), (16, 128, 128), jnp.float32)
        _lenS = 128 - jax.random.randint(jax.random.fold_in(_rk, 7), (16,), 0, max(1, 128 // 4) + 1, jnp.int32)
        _lenS2 = 128 - jax.random.randint(jax.random.fold_in(_rk, 8), (16,), 0, max(1, 128 // 4) + 1, jnp.int32)
        cond_1024 = 0.000887014 + 1.03683 * jax.random.normal(jax.random.fold_in(_rk, 11), (16, 128), jnp.float32)
        fside_BxSx3_0 = jax.random.uniform(jax.random.fold_in(_rk, 12), (16, 128, 3), jnp.float32, 0.0, 0.999943)
        return (x, cond_1024, fside_BxSx3_0)
    x, cond_1024, fside_BxSx3_0 = _rec_inputs()

    def _L0_cond_setup():
        import jax, jax.numpy as jnp
        import numpy as np
        HID = 128
        HEADS = 16
        HEAD_DIM = HID // HEADS
        ROPE_DIM = HEAD_DIM // 6 * 6
        HALF = ROPE_DIM // 3 // 2
        SWIGLU_HID = int(2 * (HID * 4) / 3)
        EPS = 1e-06
        THETA = 10000.0

        def rmsnorm(x, w, eps=EPS):
            xf = x.astype(jnp.float32)
            v = jnp.mean(xf * xf, axis=-1, keepdims=True)
            return w * (xf * jax.lax.rsqrt(v + eps)).astype(x.dtype)

        def modulate(x, shift, scale):
            return x * (1.0 + scale) + shift

        def rope_freqs():
            return 1.0 / THETA ** (jnp.arange(HALF, dtype=jnp.float32) / HALF)

        def apply_rope3d(q, k, positions):
            freqs = rope_freqs()
            ang = positions[..., :, None] * freqs
            ang = ang.reshape(ang.shape[0], ang.shape[1], -1)
            cos = jnp.cos(ang)[:, :, None, :]
            sin = jnp.sin(ang)[:, :, None, :]

            def rot(t):
                B, N, H, D = t.shape
                tr = t.reshape(B, N, H, D // 2, 2)
                t0, t1 = (tr[..., 0], tr[..., 1])
                out = jnp.stack([t0 * cos - t1 * sin, t0 * sin + t1 * cos], axis=-1)
                return out.reshape(B, N, H, D)
            return (rot(q), rot(k))
        key = jax.random.key(seed)
        ks = jax.random.split(key, 12)
        B, N = (2, 256)
        s = 0.02
        return {'x': jax.random.normal(ks[0], (B, N, HID), jnp.float32), 'c': jax.random.normal(ks[1], (B, HID), jnp.float32), 'positions': jax.random.uniform(ks[2], (B, N, 3), jnp.float32), 'norm1_w': jnp.ones((HID,), jnp.float32), 'qkv_w': jax.random.normal(ks[3], (3 * HID, HID), jnp.float32) * s, 'q_norm_w': jnp.ones((HEAD_DIM,), jnp.float32), 'k_norm_w': jnp.ones((HEAD_DIM,), jnp.float32), 'proj_w': jax.random.normal(ks[4], (HID, HID), jnp.float32) * s, 'proj_b': jnp.zeros((HID,), jnp.float32), 'norm2_w': jnp.ones((HID,), jnp.float32), 'w1': jax.random.normal(ks[5], (SWIGLU_HID, HID), jnp.float32) * s, 'w3': jax.random.normal(ks[6], (SWIGLU_HID, HID), jnp.float32) * s, 'w2': jax.random.normal(ks[7], (HID, SWIGLU_HID), jnp.float32) * s, 'ada_w': jax.random.normal(ks[8], (6 * HID, HID), jnp.float32) * s, 'ada_b': jnp.zeros((6 * HID,), jnp.float32)}
    _L0_cond_all = _L0_cond_setup()
    _L0_cond_in = {k: v for k, v in _L0_cond_all.items() if k in ('norm1_w', 'qkv_w', 'q_norm_w', 'k_norm_w', 'proj_w', 'proj_b', 'norm2_w', 'w1', 'w3', 'w2', 'ada_w', 'ada_b')}
    del _L0_cond_all

    def _L1_cond_setup():
        import jax, jax.numpy as jnp
        import numpy as np
        H = 16
        EPS = 1e-05

        def layer_norm(x, g, b):
            mu = jnp.mean(x, axis=-1, keepdims=True)
            var = jnp.var(x, axis=-1, keepdims=True)
            return (x - mu) * jax.lax.rsqrt(var + EPS) * g + b
        key = jax.random.key(seed)
        ks = jax.random.split(key, 8)
        B, T, D, TE = (4, 512, 128, 128)
        s = 0.02
        return {'x': jax.random.normal(ks[0], (B, T, D), jnp.float32), 'emb': jax.random.normal(ks[1], (B, 1, TE), jnp.float32), 'gate_msa': jax.random.normal(ks[2], (B, 1, D), jnp.float32), 'norm_g': jnp.ones((D,), jnp.float32), 'norm_b': jnp.zeros((D,), jnp.float32), 'Wq': jax.random.normal(ks[3], (D, D), jnp.float32) * s, 'bq': jnp.zeros((D,), jnp.float32), 'Wk': jax.random.normal(ks[4], (D, D), jnp.float32) * s, 'bk': jnp.zeros((D,), jnp.float32), 'Wv': jax.random.normal(ks[5], (D, D), jnp.float32) * s, 'bv': jnp.zeros((D,), jnp.float32), 'emb_W': jax.random.normal(ks[6], (TE, 2 * D), jnp.float32) * s, 'emb_b': jnp.zeros((2 * D,), jnp.float32), 'sn_g': jnp.ones((D,), jnp.float32), 'sn_b': jnp.zeros((D,), jnp.float32), 'out_W': jax.random.normal(ks[7], (D, D), jnp.float32) * s, 'out_b': jnp.zeros((D,), jnp.float32)}
    _L1_cond_all = _L1_cond_setup()
    _L1_cond_in = {k: v for k, v in _L1_cond_all.items() if k in ('norm_g', 'norm_b', 'Wq', 'bq', 'Wk', 'bk', 'Wv', 'bv', 'emb_W', 'emb_b', 'sn_g', 'sn_b', 'out_W', 'out_b')}
    del _L1_cond_all
    return {'x': x, 'cond_1024': cond_1024, 'fside_BxSx3_0': fside_BxSx3_0, 'L0_cond_norm1_w': _L0_cond_in['norm1_w'], 'L0_cond_qkv_w': _L0_cond_in['qkv_w'], 'L0_cond_q_norm_w': _L0_cond_in['q_norm_w'], 'L0_cond_k_norm_w': _L0_cond_in['k_norm_w'], 'L0_cond_proj_w': _L0_cond_in['proj_w'], 'L0_cond_proj_b': _L0_cond_in['proj_b'], 'L0_cond_norm2_w': _L0_cond_in['norm2_w'], 'L0_cond_w1': _L0_cond_in['w1'], 'L0_cond_w3': _L0_cond_in['w3'], 'L0_cond_w2': _L0_cond_in['w2'], 'L0_cond_ada_w': _L0_cond_in['ada_w'], 'L0_cond_ada_b': _L0_cond_in['ada_b'], 'L1_cond_norm_g': _L1_cond_in['norm_g'], 'L1_cond_norm_b': _L1_cond_in['norm_b'], 'L1_cond_Wq': _L1_cond_in['Wq'], 'L1_cond_bq': _L1_cond_in['bq'], 'L1_cond_Wk': _L1_cond_in['Wk'], 'L1_cond_bk': _L1_cond_in['bk'], 'L1_cond_Wv': _L1_cond_in['Wv'], 'L1_cond_bv': _L1_cond_in['bv'], 'L1_cond_emb_W': _L1_cond_in['emb_W'], 'L1_cond_emb_b': _L1_cond_in['emb_b'], 'L1_cond_sn_g': _L1_cond_in['sn_g'], 'L1_cond_sn_b': _L1_cond_in['sn_b'], 'L1_cond_out_W': _L1_cond_in['out_W'], 'L1_cond_out_b': _L1_cond_in['out_b']}

def reference(x, cond_1024, fside_BxSx3_0, L0_cond_norm1_w, L0_cond_qkv_w, L0_cond_q_norm_w, L0_cond_k_norm_w, L0_cond_proj_w, L0_cond_proj_b, L0_cond_norm2_w, L0_cond_w1, L0_cond_w3, L0_cond_w2, L0_cond_ada_w, L0_cond_ada_b, L1_cond_norm_g, L1_cond_norm_b, L1_cond_Wq, L1_cond_bq, L1_cond_Wk, L1_cond_bk, L1_cond_Wv, L1_cond_bv, L1_cond_emb_W, L1_cond_emb_b, L1_cond_sn_g, L1_cond_sn_b, L1_cond_out_W, L1_cond_out_b):
    import jax
    import jax.numpy as jnp

    def _L0_cond_ref(x, c, positions, norm1_w, qkv_w, q_norm_w, k_norm_w, proj_w, proj_b, norm2_w, w1, w3, w2, ada_w, ada_b):
        import jax, jax.numpy as jnp
        import numpy as np
        HID = 128
        HEADS = 16
        HEAD_DIM = HID // HEADS
        ROPE_DIM = HEAD_DIM // 6 * 6
        HALF = ROPE_DIM // 3 // 2
        SWIGLU_HID = int(2 * (HID * 4) / 3)
        EPS = 1e-06
        THETA = 10000.0

        def rmsnorm(x, w, eps=EPS):
            xf = x.astype(jnp.float32)
            v = jnp.mean(xf * xf, axis=-1, keepdims=True)
            return w * (xf * jax.lax.rsqrt(v + eps)).astype(x.dtype)

        def modulate(x, shift, scale):
            return x * (1.0 + scale) + shift

        def rope_freqs():
            return 1.0 / THETA ** (jnp.arange(HALF, dtype=jnp.float32) / HALF)

        def apply_rope3d(q, k, positions):
            freqs = rope_freqs()
            ang = positions[..., :, None] * freqs
            ang = ang.reshape(ang.shape[0], ang.shape[1], -1)
            cos = jnp.cos(ang)[:, :, None, :]
            sin = jnp.sin(ang)[:, :, None, :]

            def rot(t):
                B, N, H, D = t.shape
                tr = t.reshape(B, N, H, D // 2, 2)
                t0, t1 = (tr[..., 0], tr[..., 1])
                out = jnp.stack([t0 * cos - t1 * sin, t0 * sin + t1 * cos], axis=-1)
                return out.reshape(B, N, H, D)
            return (rot(q), rot(k))
        B, N, C = x.shape
        H, D = (HEADS, HEAD_DIM)
        mod = (c @ ada_w.T + ada_b)[:, None, :]
        sh_msa, sc_msa, g_msa, sh_mlp, sc_mlp, g_mlp = jnp.split(mod, 6, axis=-1)
        h = modulate(rmsnorm(x, norm1_w), sh_msa, sc_msa)
        qkv = (h @ qkv_w.T).reshape(B, N, 3, H, D)
        q, k, v = (qkv[:, :, 0], qkv[:, :, 1], qkv[:, :, 2])
        q = rmsnorm(q, q_norm_w)
        k = rmsnorm(k, k_norm_w)
        q_r, k_r = apply_rope3d(q[..., :ROPE_DIM], k[..., :ROPE_DIM], positions)
        q = jnp.concatenate([q_r, q[..., ROPE_DIM:]], axis=-1)
        k = jnp.concatenate([k_r, k[..., ROPE_DIM:]], axis=-1)
        scale = D ** (-0.5)
        attn = jnp.einsum('bnhd,bmhd->bhnm', q, k) * scale
        attn = jax.nn.softmax(attn, axis=-1)
        o = jnp.einsum('bhnm,bmhd->bnhd', attn, v).reshape(B, N, C)
        o = o @ proj_w.T + proj_b
        x = x + g_msa * o
        h2 = modulate(rmsnorm(x, norm2_w), sh_mlp, sc_mlp)
        ff = jax.nn.silu(h2 @ w1.T) * (h2 @ w3.T) @ w2.T
        x = x + g_mlp * ff
        return x

    def _L1_cond_ref(x, emb, gate_msa, norm_g, norm_b, Wq, bq, Wk, bk, Wv, bv, emb_W, emb_b, sn_g, sn_b, out_W, out_b):
        import jax, jax.numpy as jnp
        import numpy as np
        H = 16
        EPS = 1e-05

        def layer_norm(x, g, b):
            mu = jnp.mean(x, axis=-1, keepdims=True)
            var = jnp.var(x, axis=-1, keepdims=True)
            return (x - mu) * jax.lax.rsqrt(var + EPS) * g + b
        B, T, D = x.shape
        dh = D // H
        xn = layer_norm(x, norm_g, norm_b)
        q = (xn @ Wq + bq).reshape(B, T, H, dh)
        k = (xn @ Wk + bk).reshape(B, T, H, dh)
        v = (xn @ Wv + bv).reshape(B, T, H, dh)
        q = jax.nn.softmax(q, axis=-1)
        k = jax.nn.softmax(k, axis=1)
        ctx = jnp.einsum('bnhd,bnhl->bhdl', k, v)
        y = jnp.einsum('bnhd,bhdl->bnhl', q, ctx).reshape(B, T, D)
        emb_out = jax.nn.silu(emb) @ emb_W + emb_b
        scale, shift = jnp.split(emb_out, 2, axis=-1)
        h = layer_norm(y, sn_g, sn_b) * (1.0 + scale) + shift
        h = jax.nn.silu(h) @ out_W + out_b
        return x + gate_msa * h
    x = _L0_cond_ref(x, cond_1024, fside_BxSx3_0, L0_cond_norm1_w, L0_cond_qkv_w, L0_cond_q_norm_w, L0_cond_k_norm_w, L0_cond_proj_w, L0_cond_proj_b, L0_cond_norm2_w, L0_cond_w1, L0_cond_w3, L0_cond_w2, L0_cond_ada_w, L0_cond_ada_b)
    x = _L1_cond_ref(x, cond_1024[:, None, :], cond_1024[:, None, :], L1_cond_norm_g, L1_cond_norm_b, L1_cond_Wq, L1_cond_bq, L1_cond_Wk, L1_cond_bk, L1_cond_Wv, L1_cond_bv, L1_cond_emb_W, L1_cond_emb_b, L1_cond_sn_g, L1_cond_sn_b, L1_cond_out_W, L1_cond_out_b)
    return x

_drawn_inputs = setup_inputs


def setup_inputs(seed=0):
    import zlib

    import numpy as np

    out = dict(_drawn_inputs(seed))
    spreads = {'L0_cond_norm1_w': (1.0, 0.6),
     'L0_cond_q_norm_w': (1.0, 0.6),
     'L0_cond_k_norm_w': (1.0, 0.6),
     'L0_cond_proj_b': (0.0, 0.295),
     'L0_cond_norm2_w': (1.0, 0.6),
     'L0_cond_ada_b': (0.0, 0.714),
     'L1_cond_norm_g': (1.0, 0.6),
     'L1_cond_norm_b': (0.0, 0.8),
     'L1_cond_bq': (0.0, 2.0),
     'L1_cond_bk': (0.0, 2.0),
     'L1_cond_bv': (0.0, 0.8),
     'L1_cond_emb_b': (0.0, 2.0),
     'L1_cond_sn_g': (1.0, 0.6),
     'L1_cond_sn_b': (0.0, 2.0),
     'L1_cond_out_b': (0.0, 2.0)}
    factors = {'fside_BxSx3_0': 8.0,
     'L0_cond_qkv_w': 8.0,
     'L0_cond_proj_w': 8.0,
     'L0_cond_w1': 8.0,
     'L0_cond_w3': 8.0,
     'L0_cond_w2': 8.0,
     'L1_cond_Wq': 64.0,
     'L1_cond_Wk': 64.0,
     'L1_cond_Wv': 8.0,
     'L1_cond_emb_W': 8.0,
     'L1_cond_out_W': 5.228}
    for name, (base, spread) in spreads.items():
        noise = np.random.default_rng([zlib.crc32(name.encode()), seed]).standard_normal(out[name].shape)
        drawn = base * np.exp(spread * noise) if base else spread * noise
        out[name] = jnp.asarray(drawn.astype(out[name].dtype))
    for name, factor in factors.items():
        out[name] = (out[name] * factor).astype(out[name].dtype)
    return out
```

```python
import math

import numpy as np
import concourse.bass as bass
from concourse import mybir
from concourse.alu_op_type import AluOpType as ALU
from contextlib import ExitStack

F32 = mybir.dt.float32
BF16 = mybir.dt.bfloat16
I32 = mybir.dt.int32
ACT = mybir.ActivationFunctionType
X_AXIS = mybir.AxisListType.X

B, T, D = 16, 128, 128
H = 16
DH = D // H
ROPE = DH // 6 * 6
AXES = ROPE // 2
FFN = int(2 * (4 * D) / 3)
FC = -(-FFN // 128)
LAST = FFN - (FC - 1) * 128
GRP = 4
NG = B // GRP
SLOT = 64
HPC = 4
NC = H // HPC
PAIRS = H // 2
VW = 32
EPS0, EPS1 = 1e-6, 1e-5
SCALE = DH ** -0.5
MAGIC = 0x5F3759DF
ROUND = 1.5 * 2.0 ** 23
TWO_PI_A = 6.28125
TWO_PI_B = float(np.float32(round((2 * math.pi - TWO_PI_A) * 2 ** 21) / 2 ** 21))
TWO_PI_C = 2 * math.pi - TWO_PI_A - TWO_PI_B
PI_BELOW = 3.1415925

A1, S1, G1, GB1, A2, S2, G2, A3, S3, GATE, GO, NMOD = range(12)
R_ADA, R_N1, R_PB, R_N2, R_NG, R_NB, R_BK, R_EB, R_SG, R_SB, R_OB, NROW = 0, 6, 7, 8, 9, 10, 11, 12, 14, 15, 16, 17
TBL = 4 * DH

LEAD = 4


def is_seq(b):
    return not isinstance(b, int) or 0 <= b < B


def wait(eng, sem, value):
    if not isinstance(value, int) or value > 0:
        eng.wait_ge(sem, value)


def steps(eng, body):
    first, last = LEAD, B - LEAD
    for t in range(-LEAD, first):
        body(t, t % 2)
    with eng.Fori(0, (last - first) // 2) as i:
        body(i * 2 + first, first % 2)
        body(i * 2 + (first + 1), (first + 1) % 2)
    for t in range(last, B + 1):
        body(t, t % 2)


def groups(eng, body):
    body(0)
    with eng.Fori(1, NG - 1) as g:
        body(g)
    body(NG - 1)


def ahead(g, front):
    if not isinstance(g, int) or g + 1 < NG:
        front(g + 1)


def dit_then_linear_attention(nc, x, cond, pos, norm1_w, qkv_w, q_norm_w, k_norm_w, proj_w, proj_b,
                              norm2_w, w1, w3, w2, ada_w, ada_b, norm_g, norm_b, Wq, bq, Wk, bk, Wv,
                              bv, emb_W, emb_b, sn_g, sn_b, out_W, out_b, out):
    ctx = ExitStack()
    with ctx:
        def sb(name, shape, dt=F32):
            return ctx.enter_context(nc.sbuf_tensor(name, shape, dt))

        def sem(name):
            return ctx.enter_context(nc.semaphore(name))

        ident = sb("ident", [128, 128])
        identb = sb("identb", [128, 128], BF16)
        ones = sb("ones", [1, 128])
        blocks = sb("blocks", [128, 128])
        sel = sb("sel", [128, H, 128], BF16)
        xin = sb("xin", [128, B, D])
        cond_n = sb("cond_n", [B, D])
        params_n = sb("params_n", [NROW, D])
        bqv = sb("bqv", [1, 2 * D])
        posn = sb("posn", [128, B * AXES])
        qkw = sb("qkw", [128, 2, DH])
        qkv_n = sb("qkv_n", [128, 3, D])
        proj_n = sb("proj_n", [128, D])
        w1_n = sb("w1_n", [128, FC, D])
        w3_n = sb("w3_n", [128, FC, D])
        w2_n = sb("w2_n", [128, FC * 128])
        ada_n = sb("ada_n", [128, 6, D])
        emb_n = sb("emb_n", [128, 2 * D])
        lin_n = sb("lin_n", [128, 3, D])
        outw_n = sb("outw_n", [128, D])
        adaT = sb("adaT", [128, 6 * D])
        qkvT = sb("qkvT", [128, 3 * D])
        projT = sb("projT", [128, D])
        w1T = sb("w1T", [128, FC * 128])
        w3T = sb("w3T", [128, FC * 128])
        w2T = sb("w2T", [128, FC, D])
        lin = sb("lin", [128, 3, D])
        outw = sb("outw", [128, D])
        nbb = sb("nbb", [128, 128])
        bias_qv = sb("bias_qv", [128, 2 * D])
        bias_k = sb("bias_k", [128, 1])
        par = sb("par", [128, NROW])
        condT = sb("condT", [128, B])
        csilu = sb("csilu", [128, B])
        ctanh = sb("ctanh", [128, B])
        modr = sb("modr", [128, 6, B])
        embr = sb("embr", [128, 2, B])
        mods = sb("mods", [128, B, NMOD])
        ang = sb("ang", [128, 2, B * AXES])
        sincos = sb("sincos", [128, 2, B, AXES])
        nsin = sb("nsin", [128, B, AXES])
        turns = sb("turns", [128, B * AXES])
        rope = sb("rope", [128, B, TBL])
        big = sb("big", [128, B, D])
        ms = sb("ms", [128, B])
        ry = sb("ry", [128, B])
        rt = sb("rt", [128, B])
        rstd_x = sb("rstd_x", [128, B])
        fac = [sb(f"fac{p}", [128, TBL + 2]) for p in range(2)]
        gfac = [sb(f"gfac{p}", [128, 2]) for p in range(2)]
        xs = [sb(f"xs{p}", [128, D]) for p in range(2)]
        hT = [sb(f"hT{p}", [128, T]) for p in range(2)]
        qk = [sb(f"qk{p}", [128, 2 * H, DH]) for p in range(2)]
        qk2 = [sb(f"qk2{p}", [128, 2 * H, DH]) for p in range(2)]
        qv_ms = [sb(f"qv_ms{p}", [128, 2 * H]) for p in range(2)]
        qv_s = [sb(f"qv_s{p}", [128, 2 * H]) for p in range(2)]
        qv_y = [sb(f"qv_y{p}", [128, 2 * H]) for p in range(2)]
        qv_t = sb("qv_t", [128, 2 * H])
        three_halves = sb("three_halves", [128, 2 * H])
        qn = sb("qn", [128, 2 * H, DH])
        partner = sb("partner", [128, 2 * H, ROPE])
        rot = [sb(f"rot{p}", [128, 2 * H, DH]) for p in range(2)]
        rest = sb("rest", [128, 2 * H, DH])
        parts = [sb(f"parts{p}", [128, 2, H, SLOT], BF16) for p in range(2)]
        qT = [sb(f"qT{p}", [128, PAIRS, T], BF16) for p in range(2)]
        kT = [sb(f"kT{p}", [128, PAIRS, 2, T], BF16) for p in range(2)]
        nmax = [sb(f"nmax{p}", [128, H]) for p in range(2)]
        mparts = sb("mparts", [128, 128], BF16)
        mT = [sb(f"mT{p}", [128, T], BF16) for p in range(2)]
        probs = [sb(f"probs{c}", [128, HPC, T]) for c in range(NC)]
        vall = sb("vall", [128, B, D])
        vpad = [sb(f"vpad{p}", [128, H, VW]) for p in range(2)]
        oT4 = sb("oT4", [128, NC * T])
        rsum = sb("rsum", [128, H])
        o = sb("o", [128, H, DH])
        oT = sb("oT", [128, T])
        pr = sb("pr", [128, T])
        x1 = sb("x1", [128, B, D])
        gm = sb("gm", [128, GRP, 2])
        gg = sb("gg", [128, GRP, 2])
        rstd1 = sb("rstd1", [128, B])
        xs4 = sb("xs4", [128, GRP, D])
        hT4 = [sb(f"hT4{p}", [128, GRP, T]) for p in range(2)]
        th = [sb(f"th{c}", [128, GRP * T]) for c in range(FC)]
        yg = [sb(f"yg{c}", [128, GRP * T]) for c in range(FC)]
        ff = [sb(f"ff{c}", [128, GRP * T]) for c in range(FC)]
        fg = sb("fg", [128, GRP, T])
        x2 = sb("x2", [128, B, D])
        bn = sb("bn", [128, B, 6])
        mean2 = sb("mean2", [128, B])
        rstd2 = sb("rstd2", [128, B])
        kmax = sb("kmax", [128, GRP])
        ke = sb("ke", [128, GRP, T])
        kx = sb("kx", [128, GRP, T])
        kxT = sb("kxT", [128, GRP, D])
        qvb = sb("qvb", [128, GRP, 2 * D + 2])
        qmax = sb("qmax", [128, GRP * H])
        qs = sb("qs", [128, GRP * H, DH])
        qe = sb("qe", [128, GRP * H, DH])
        qsum = sb("qsum", [128, GRP * H])
        qrec = sb("qrec", [128, GRP * H])
        qx = sb("qx", [128, GRP * H, DH])
        qxT = sb("qxT", [128, GRP, T])
        krec = sb("krec", [128, GRP])
        cx = sb("cx", [128, GRP, D])
        y = sb("y", [128, B, D])
        mean3 = sb("mean3", [128, B])
        rstd3 = sb("rstd3", [128, B])
        hs = sb("hs", [128, GRP * T])
        hg = sb("hg", [128, GRP, T])
        res = sb("res", [128, B, D])

        bank = [ctx.enter_context(nc.psum_tensor(f"bank{i}", [128, 512], F32)) for i in range(8)]
        S_BANK, E_BANK, Q_BANK, K_BANK, O_BANK, W_BANK = (0, 1), (2, 3), 4, 5, 6, 7

        ld_x = sem("ld_x")
        ld_small = sem("ld_small")
        ld_ada = sem("ld_ada")
        ld_qkv = sem("ld_qkv")
        ld_pos = sem("ld_pos")
        ld_rest = sem("ld_rest")
        consts = sem("consts")
        padded = sem("padded")
        seeded = sem("seeded")
        stored = sem("stored")
        pt = sem("pt")
        pv_v = sem("pv_v")
        pv_a = sem("pv_a")
        pv_g = sem("pv_g")
        s_fac = sem("s_fac")
        s_xs = sem("s_xs")
        s_xsT = sem("s_xsT")
        s_hT = sem("s_hT")
        s_qkv = sem("s_qkv")
        s_sq = sem("s_sq")
        s_qk = sem("s_qk")
        s_vall = sem("s_vall")
        s_ss = sem("s_ss")
        s_newton = sem("s_newton")
        s_rot = sem("s_rot")
        s_parts = sem("s_parts")
        s_qTp = sem("s_qTp")
        s_kTp = sem("s_kTp")
        s_qT = sem("s_qT")
        s_kT = sem("s_kT")
        s_s = sem("s_s")
        s_max = sem("s_max")
        s_mh = sem("s_mh")
        s_mp = sem("s_mp")
        s_mTp = sem("s_mTp")
        s_mT = sem("s_mT")
        s_e = sem("s_e")
        s_p = sem("s_p")
        s_vpad = sem("s_vpad")
        s_o = sem("s_o")
        s_oT4 = sem("s_oT4")
        s_oq = sem("s_oq")
        s_rec = sem("s_rec")
        s_on = sem("s_on")
        s_oTp = sem("s_oTp")
        s_oT = sem("s_oT")
        s_proj = sem("s_proj")
        s_gfac = sem("s_gfac")
        s_pr = sem("s_pr")
        s_prT = sem("s_prT")
        s_x1 = sem("s_x1")
        s_res = sem("s_res")

        b_bn = sem("b_bn")
        b_ff = sem("b_ff")
        b_fg = sem("b_fg")
        b_fgT = sem("b_fgT")
        b_fm = sem("b_fm")
        b_g = sem("b_g")
        b_gm = sem("b_gm")
        b_hT = sem("b_hT")
        b_rstd = sem("b_rstd")
        b_sq = sem("b_sq")
        b_th = sem("b_th")
        b_u = sem("b_u")
        b_x2 = sem("b_x2")
        b_xs = sem("b_xs")
        b_xsT = sem("b_xsT")
        b_y = sem("b_y")
        c_bn = sem("c_bn")
        c_ctx = sem("c_ctx")
        c_cx = sem("c_cx")
        c_hT = sem("c_hT")
        c_k = sem("c_k")
        c_ke = sem("c_ke")
        c_km = sem("c_km")
        c_krec = sem("c_krec")
        c_kx = sem("c_kx")
        c_kxT = sem("c_kxT")
        c_kxTp = sem("c_kxTp")
        c_qe = sem("c_qe")
        c_qmax = sem("c_qmax")
        c_qrec = sem("c_qrec")
        c_qs = sem("c_qs")
        c_qsum = sem("c_qsum")
        c_qv = sem("c_qv")
        c_qvb = sem("c_qvb")
        c_qx = sem("c_qx")
        c_qxT = sem("c_qxT")
        c_qxTp = sem("c_qxTp")
        c_rstd = sem("c_rstd")
        c_xc = sem("c_xc")
        c_xs = sem("c_xs")
        c_xsT = sem("c_xsT")
        c_y = sem("c_y")
        c_yp = sem("c_yp")
        d_gg = sem("d_gg")
        d_gm = sem("d_gm")
        d_hT = sem("d_hT")
        d_hg = sem("d_hg")
        d_hgT = sem("d_hgT")
        d_hs = sem("d_hs")
        d_op = sem("d_op")
        d_rstd = sem("d_rstd")
        d_th = sem("d_th")
        d_xc = sem("d_xc")
        d_xs = sem("d_xs")
        d_xsT = sem("d_xsT")

        N_CSILU, N_NBB, N_DONE = 10 + 2 + 11 + 1 + 10 + 2, 10 + 2 + 11 + 1 + 10 + 3, 10 + 2 + 11 + 1 + 10 + 3 + 7
        NEWT, ROT, PARTS, SEED = 12, 5, 9, 4
        RSTEPS, LSTEPS = 13, 14
        N_SIN = 1
        N_SMALL, N_REST = 16 * 12, 16 * 12
        P_COND, P_ADA, P_QKV, P_MOD, P_W1, P_W3, P_W2, P_BIAS, P_EMB = range(1, 10)
        V_ANG, V_COND = 8, 10

        block = ctx.enter_context(nc.Block())

        def rsqrt(v, sm, base, y_, s_, t_):
            n = base

            def did(ins):
                nonlocal n
                n += 1
                ins.then_inc(sm, 1)
                v.wait_ge(sm, n)
            did(nc.vector.tensor_scalar(t_.bitcast(I32), s_.bitcast(I32), 1, None, ALU.logical_shift_right))
            did(nc.vector.tensor_scalar(y_.bitcast(I32), t_.bitcast(I32), -1.0, float(MAGIC), ALU.mult, ALU.add))
            for _ in range(3):
                did(nc.vector.tensor_tensor(t_, y_, y_, ALU.mult))
                did(nc.vector.scalar_tensor_tensor(t_, t_, -0.5, s_, ALU.mult, ALU.mult))
                did(nc.vector.scalar_tensor_tensor(y_, t_, 1.5, y_, ALU.add, ALU.mult))
            return n

        def blocks_gpsimd(g):
            q = nc.gpsimd

            def normed(src, mean, rstd, centred, made, used):
                def group(i):
                    wait(g, used, i)
                    rows = bass.ds(i * GRP, GRP)
                    x_ = src[:, rows, :]
                    if mean is not None:
                        q.tensor_tensor(xs4[:, :, :], x_, mean[:, rows].unsqueeze(2).to_broadcast([128, GRP, D]),
                                        ALU.subtract).then_inc(centred, 1)
                        g.wait_ge(centred, i + 1)
                        x_ = xs4[:, :, :]
                    q.tensor_tensor(xs4[:, :, :], x_, rstd[:, rows].unsqueeze(2).to_broadcast([128, GRP, D]),
                                    ALU.mult).then_inc(made, 1)
                return group

            g.wait_ge(b_rstd, RSTEPS)
            groups(g, normed(x1, None, rstd1, None, b_xs, b_xsT))

            def query(i):
                def bc(v_):
                    return v_[:, :].unsqueeze(2).to_broadcast([128, GRP * H, DH])
                g.wait_ge(c_qmax, i + 1)
                for j in range(GRP):
                    last = q.tensor_tensor(qs[:, j * H:(j + 1) * H, :], qvb[:, j, 0:D].rearrange("p (h d) -> p h d", d=DH),
                                           qmax[:, j * H:(j + 1) * H].unsqueeze(2).to_broadcast([128, H, DH]), ALU.subtract)
                last.then_inc(c_qs, 1)
                ahead(i, c_front)
                g.wait_ge(c_qrec, i + 1)
                wait(g, c_qxT, i)
                q.tensor_tensor(qx[:, :, :], qe[:, :, :], bc(qrec), ALU.mult).then_inc(c_qx, 1)

            g.wait_ge(c_rstd, LSTEPS)
            c_front = normed(x2, mean2, rstd2, c_xc, c_xs, c_xsT)
            c_front(0)
            groups(g, query)
            g.wait_ge(d_rstd, LSTEPS)
            groups(g, normed(y, mean3, rstd3, d_xc, d_xs, d_xsT))

        def blocks_scalar(a):
            q = nc.scalar

            def flat(t_):
                return t_[:, :, :].rearrange("p g t -> p (g t)")

            a.wait_ge(s_x1, B)
            q.activation(big[:, :, :], x1[:, :, :], ACT.Square).then_inc(b_sq, 1)

            def b_front(g):
                a.wait_ge(b_xsT, g + 1)
                a.wait_ge(b_gm, g + 1)
                for j in range(GRP):
                    last = q.activation(hT4[0][:, j, :], bank[0][:, j * T:(j + 1) * T], ACT.Identity,
                                        bias=gm[:, j, 1:2], scale=gm[:, j, 0:1])
                last.then_inc(b_hT, 1)

            def b_body(g):
                for c in range(FC):
                    a.wait_ge(b_g, FC * g + c + 1)
                    wait(a, b_y, FC * (g - 1) + c + 1)
                    q.activation(th[c][:, :], bank[1 + c][:, :], ACT.Tanh, scale=0.5).then_inc(b_th, 1)
                ahead(g, b_front)
            b_front(0)
            groups(a, b_body)

            def c_front(g):
                a.wait_ge(c_xsT, g + 1)
                q.activation(flat(hT4[1]), bank[0][:, :], ACT.Copy).then_inc(c_hT, 1)

            def c_body(g):
                a.wait_ge(c_ke, g + 1)
                wait(a, c_kxTp, g)
                q.activation(flat(kx), flat(ke), ACT.Exp).then_inc(c_kx, 1)
                ahead(g, c_front)
                a.wait_ge(c_kxTp, g + 1)
                wait(a, c_ctx, g)
                q.activation(flat(kxT), bank[4][:, :], ACT.Copy).then_inc(c_kxT, 1)
                a.wait_ge(c_qs, g + 1)
                wait(a, c_qx, g)
                q.activation(flat(qe), flat(qs), ACT.Exp).then_inc(c_qe, 1)
                a.wait_ge(c_qxTp, g + 1)
                wait(a, c_yp, g)
                q.activation(flat(qxT), bank[1][:, :], ACT.Copy).then_inc(c_qxT, 1)
            c_front(0)
            groups(a, c_body)

            def d_front(g):
                a.wait_ge(d_xsT, g + 1)
                a.wait_ge(d_gm, g + 1)
                wait(a, d_hs, g)
                for j in range(GRP):
                    last = q.activation(hT4[0][:, j, :], bank[0][:, j * T:(j + 1) * T], ACT.Identity,
                                        bias=gm[:, j, 1:2], scale=gm[:, j, 0:1])
                last.then_inc(d_hT, 1)
                a.wait_ge(d_hT, g + 1)
                q.activation(th[0][:, :], flat(hT4[0]), ACT.Tanh, scale=0.5).then_inc(d_th, 1)

            def d_body(g):
                a.wait_ge(d_op, g + 1)
                a.wait_ge(d_gg, g + 1)
                wait(a, d_hgT, g)
                for j in range(GRP):
                    last = q.activation(hg[:, j, :], bank[1][:, j * T:(j + 1) * T], ACT.Identity,
                                        bias=gg[:, j, 1:2], scale=gg[:, j, 0:1])
                last.then_inc(d_hg, 1)
                ahead(g, d_front)
            d_front(0)
            groups(a, d_body)

        def blocks_vector(v):
            q = nc.vector

            def stage(dst, col, n, g, sm):
                q.tensor_scalar(dst[:, :, :], mods[:, bass.ds(g * GRP, GRP), col:col + n], 1.0, None, ALU.mult).then_inc(sm, 1)

            v.wait_ge(b_sq, 1)
            q.tensor_reduce(ms[:, :], big[:, :, :], X_AXIS, ALU.add).then_inc(b_rstd, 1)
            v.wait_ge(b_rstd, 1)
            q.tensor_scalar(ms[:, :], ms[:, :], 1.0 / D, EPS0, ALU.mult, ALU.add).then_inc(b_rstd, 1)
            v.wait_ge(b_rstd, 2)
            assert rsqrt(v, b_rstd, 2, rstd1[:, :], ms[:, :], rt[:, :]) == RSTEPS

            def b_body(g):
                for c in range(FC):
                    v.wait_ge(b_th, FC * g + c + 1)
                    if c == 0:
                        wait(v, b_x2, g)
                    q.scalar_tensor_tensor(yg[c][:, :], th[c][:, :], 1.0, bank[1 + c][:, :], ALU.add, ALU.mult).then_inc(b_y, 1)
                    if c == 0 and not (isinstance(g, int) and g == 0):
                        moments(g - 1, lambda j: x2[:, bass.ds((g - 1) * GRP + j, 1), :].rearrange("p a f -> p (a f)")).then_inc(b_bn, 1)
                    v.wait_ge(b_y, FC * g + c + 1)
                    v.wait_ge(b_u, FC * g + c + 1)
                    if c == 0:
                        wait(v, b_fm, g)
                    q.tensor_tensor(ff[c][:, :], bank[4 + c][:, :], yg[c][:, :], ALU.mult).then_inc(b_ff, 1)

                def next_gm(i):
                    v.wait_ge(b_hT, i)
                    stage(gm, A2, 2, i, b_gm)
                ahead(g, next_gm)
                rows = bass.ds(g * GRP, GRP)
                v.wait_ge(b_fm, g + 1)
                wait(v, b_fgT, g)
                b7 = bank[7][:, :].rearrange("p (g t) -> p g t", t=T)
                q.tensor_tensor(fg[:, :, :], b7, mods[:, rows, G2:G2 + 1].to_broadcast([128, GRP, T]), ALU.mult).then_inc(b_fg, 1)
                v.wait_ge(b_fgT, g + 1)
                q.tensor_tensor(x2[:, rows, :], b7, x1[:, rows, :], ALU.add).then_inc(b_x2, 1)

            def moments(g, src):
                for j in range(GRP):
                    last = q.bn_stats(bn[:, bass.ds(g * GRP + j, 1), :].rearrange("p a s -> p (a s)"), src(j))
                return last

            def std(mean, rstd, sm):
                me, mo, de, do = bn[:, :, 1], bn[:, :, 4], bn[:, :, 2], bn[:, :, 5]
                q.tensor_tensor(mean[:, :], me, mo, ALU.add)
                q.tensor_tensor(rt[:, :], me, mo, ALU.subtract)
                q.tensor_tensor(ms[:, :], de, do, ALU.add).then_inc(sm, 1)
                v.wait_ge(sm, 1)
                q.tensor_scalar(mean[:, :], mean[:, :], 0.5, None, ALU.mult)
                q.tensor_scalar(ms[:, :], ms[:, :], 1.0 / D, EPS1, ALU.mult, ALU.add)
                q.scalar_tensor_tensor(rt[:, :], rt[:, :], 0.25, rt[:, :], ALU.mult, ALU.mult).then_inc(sm, 1)
                v.wait_ge(sm, 2)
                q.tensor_tensor(ms[:, :], ms[:, :], rt[:, :], ALU.add).then_inc(sm, 1)
                v.wait_ge(sm, 3)
                assert rsqrt(v, sm, 3, rstd[:, :], ms[:, :], rt[:, :]) == LSTEPS

            stage(gm, A2, 2, 0, b_gm)
            groups(v, b_body)

            v.wait_ge(b_x2, NG)
            moments(NG - 1, lambda j: x2[:, (NG - 1) * GRP + j, :]).then_inc(b_bn, 1)
            v.wait_ge(b_bn, NG)
            std(mean2, rstd2, c_rstd)

            def c_body(g):
                b1 = bank[1][:, :].rearrange("p (g t) -> p g t", t=T)
                v.wait_ge(c_k, g + 1)
                q.tensor_reduce(kmax[:, :], b1, X_AXIS, ALU.max).then_inc(c_km, 1)
                v.wait_ge(c_km, 2 * g + 1)
                q.tensor_scalar(kmax[:, :], kmax[:, :], bias_k[:, 0:1], None, ALU.add).then_inc(c_km, 1)
                v.wait_ge(c_km, 2 * g + 2)
                wait(v, c_kx, g)
                q.scalar_tensor_tensor(ke[:, :, :], b1, bias_k[:, 0:1], kmax[:, :].unsqueeze(2).to_broadcast([128, GRP, T]),
                                       ALU.add, ALU.subtract).then_inc(c_ke, 1)
                v.wait_ge(c_qv, g + 1)
                wait(v, c_ctx, g)
                wait(v, c_qs, g)
                for k in range(2):
                    last = q.tensor_tensor(qvb[:, 2 * k:2 * k + 2, 0:2 * D],
                                           bank[2 + k][:, :].rearrange("p (g f) -> p g f", f=2 * D),
                                           bias_qv[:, :].unsqueeze(1).to_broadcast([128, 2, 2 * D]), ALU.add)
                last.then_inc(c_qvb, 1)
                v.wait_ge(c_qvb, g + 1)
                for j in range(GRP):
                    last = q.tensor_reduce(qmax[:, j * H:(j + 1) * H], qvb[:, j, 0:D].rearrange("p (h d) -> p h d", d=DH),
                                           X_AXIS, ALU.max)
                last.then_inc(c_qmax, 1)
                v.wait_ge(c_qe, g + 1)
                q.tensor_reduce(qsum[:, :], qe[:, :, :], X_AXIS, ALU.add).then_inc(c_qsum, 1)
                v.wait_ge(c_qsum, g + 1)
                wait(v, c_qx, g)
                q.reciprocal(qrec[:, :], qsum[:, :]).then_inc(c_qrec, 1)
                v.wait_ge(c_ctx, g + 1)
                for k in range(2):
                    last = q.reciprocal(krec[:, 2 * k:2 * k + 2],
                                        bank[5 + k][:, 0:2 * (D + 1)].rearrange("p (g f) -> p g f", f=D + 1)[:, :, D])
                last.then_inc(c_krec, 1)
                v.wait_ge(c_krec, g + 1)
                wait(v, c_yp, g)
                for j in range(GRP):
                    at = j % 2 * (D + 1)
                    last = q.scalar_tensor_tensor(cx[:, j, :], bank[5 + j // 2][:, at:at + D], krec[:, j:j + 1],
                                                  blocks[:, :], ALU.mult, ALU.mult)
                last.then_inc(c_cx, 1)
                v.wait_ge(c_yp, g + 1)
                q.tensor_scalar(y[:, bass.ds(g * GRP, GRP), :], bank[7][:, :].rearrange("p (g f) -> p g f", f=D),
                                1.0, None, ALU.mult).then_inc(c_y, 1)
                moments(g, lambda j: bank[7][:, j * D:(j + 1) * D]).then_inc(c_bn, 1)
            groups(v, c_body)

            v.wait_ge(c_bn, NG)
            std(mean3, rstd3, d_rstd)

            def d_body(g):
                v.wait_ge(d_th, g + 1)
                wait(v, d_op, g)
                q.scalar_tensor_tensor(hs[:, :], th[0][:, :], 1.0, hT4[0][:, :, :].rearrange("p g t -> p (g t)"),
                                       ALU.add, ALU.mult).then_inc(d_hs, 1)
                wait(v, d_hg, g)
                stage(gg, GATE, 2, g, d_gg)

                def next_gm(i):
                    v.wait_ge(d_hT, i)
                    stage(gm, A3, 2, i, d_gm)
                ahead(g, next_gm)
                rows = bass.ds(g * GRP, GRP)
                v.wait_ge(d_hgT, g + 1)
                q.tensor_tensor(res[:, rows, :], bank[2][:, :].rearrange("p (g f) -> p g f", f=D), x2[:, rows, :],
                                ALU.add).then_inc(s_res, 1)
            stage(gm, A3, 2, 0, d_gm)
            groups(v, d_body)

        def blocks_tensor(e):
            q = nc.tensor

            def four(dst, src, sm):
                for j in range(GRP):
                    last = q.transpose(dst[:, j * 128:(j + 1) * 128], src(j), ident[:, :])
                last.then_inc(sm, 1)

            def b_front(g):
                e.wait_ge(b_xs, g + 1)
                wait(e, b_hT, g)
                four(bank[0], lambda j: xs4[:, j, :], b_xsT)

            def b_body(g):
                h = hT4[0][:, :, :].rearrange("p g t -> p (g t)")
                e.wait_ge(b_hT, g + 1)
                for c in range(FC):
                    wait(e, b_y, FC * (g - 1) + c + 1)
                    q.matmul(bank[1 + c][:, :], w1T[:, c * 128:c * 128 + 128], h, start=True, stop=True).then_inc(b_g, 1)
                    wait(e, b_ff, FC * (g - 1) + c + 1)
                    q.matmul(bank[4 + c][:, :], w3T[:, c * 128:c * 128 + 128], h, start=True, stop=True).then_inc(b_u, 1)
                ahead(g, b_front)
                wait(e, b_x2, g)
                for c in range(FC):
                    e.wait_ge(b_ff, FC * g + c + 1)
                    last = q.matmul(bank[7][:, :], w2T[:, c, :], ff[c][:, :], start=c == 0, stop=c == FC - 1)
                last.then_inc(b_fm, 1)
                e.wait_ge(b_fg, g + 1)
                four(bank[7], lambda j: fg[:, j, :], b_fgT)
            e.wait_ge(s_x1, B)
            b_front(0)
            groups(e, b_body)

            def c_front(g):
                e.wait_ge(c_xs, g + 1)
                wait(e, c_hT, g)
                four(bank[0], lambda j: xs4[:, j, :], c_xsT)

            def c_body(g):
                e.wait_ge(c_hT, g + 1)
                wait(e, c_qxT, g)
                q.matmul(bank[1][:, :], lin[:, 2, :], hT4[1][:, :, :].rearrange("p g t -> p (g t)"), start=True, stop=True).then_inc(c_k, 1)
                wait(e, c_qvb, g)
                for j in range(GRP):
                    last = q.matmul(bank[2 + j // 2][:, j % 2 * 2 * D:(j % 2 + 1) * 2 * D], hT4[1][:, j, :],
                                    lin[:, 0:2, :].rearrange("p c f -> p (c f)"), start=True, stop=True)
                last.then_inc(c_qv, 1)
                ahead(g, c_front)
                e.wait_ge(c_kx, g + 1)
                wait(e, c_kxT, g)
                four(bank[4], lambda j: kx[:, j, :], c_kxTp)
                e.wait_ge(c_kxT, g + 1)
                e.wait_ge(c_qvb, g + 1)
                wait(e, c_cx, g)
                for j in range(GRP):
                    at = j % 2 * (D + 1)
                    last = q.matmul(bank[5 + j // 2][:, at:at + D + 1], kxT[:, j, :], qvb[:, j, D:2 * D + 1], start=True, stop=True)
                last.then_inc(c_ctx, 1)
                e.wait_ge(c_qx, g + 1)
                four(bank[1], lambda j: qx[:, j * H:(j + 1) * H, :].rearrange("p h d -> p (h d)"), c_qxTp)
                e.wait_ge(c_qxT, g + 1)
                e.wait_ge(c_cx, g + 1)
                wait(e, c_bn, g)
                for j in range(GRP):
                    last = q.matmul(bank[7][:, j * D:(j + 1) * D], qxT[:, j, :], cx[:, j, :], start=True, stop=True)
                last.then_inc(c_yp, 1)
            e.wait_ge(b_x2, NG)
            c_front(0)
            groups(e, c_body)

            def d_front(g):
                e.wait_ge(d_xs, g + 1)
                wait(e, d_hT, g)
                four(bank[0], lambda j: xs4[:, j, :], d_xsT)

            def d_body(g):
                e.wait_ge(d_hs, g + 1)
                wait(e, d_hg, g)
                q.matmul(bank[1][:, :], outw[:, :], hs[:, :], start=True, stop=True).then_inc(d_op, 1)
                ahead(g, d_front)
                e.wait_ge(d_hg, g + 1)
                wait(e, s_res, g)
                four(bank[2], lambda j: hg[:, j, :], d_hgT)
            e.wait_ge(c_y, NG)
            d_front(0)
            groups(e, d_body)

        @block.sync
        def _(sp):
            sp.dma_start(cond_n[:, :], cond).then_inc(ld_small, 16)
            for row, v, n in ((R_ADA, ada_b, 6), (R_N1, norm1_w, 1), (R_PB, proj_b, 1), (R_N2, norm2_w, 1),
                              (R_NG, norm_g, 1), (R_NB, norm_b, 1), (R_BK, bk, 1), (R_EB, emb_b, 2),
                              (R_SG, sn_g, 1), (R_SB, sn_b, 1), (R_OB, out_b, 1)):
                sp.dma_start(params_n[row:row + n, :], v.rearrange("(a n) -> a n", a=n)).then_inc(ld_small, 16)
            sp.dma_start(qkv_n[:, :, :], qkv_w.rearrange("(c p) f -> p c f", p=128)).then_inc(ld_qkv, 16)
            wait(sp, padded, 3)
            for w, wn in ((w1, w1_n), (w3, w3_n)):
                sp.dma_start(wn[:, 0:FC - 1, :], w[0:(FC - 1) * 128, :].rearrange("(c p) f -> p c f", p=128)).then_inc(ld_rest, 16)
                sp.dma_start(wn[0:LAST, FC - 1, :], w[(FC - 1) * 128:FFN, :]).then_inc(ld_rest, 16)
            sp.dma_start(w2_n[:, 0:FFN], w2).then_inc(ld_rest, 16)
            sp.dma_start(emb_n[:, :], emb_W).then_inc(ld_rest, 16)
            for i, w in enumerate((Wq, Wv, Wk)):
                sp.dma_start(lin_n[:, i, :], w).then_inc(ld_rest, 16)
            sp.dma_start(outw_n[:, :], out_W).then_inc(ld_rest, 16)
            sp.dma_start(bqv[:, 0:D], bq.rearrange("(a n) -> a n", a=1)).then_inc(ld_rest, 16)
            sp.dma_start(bqv[:, D:2 * D], bv.rearrange("(a n) -> a n", a=1)).then_inc(ld_rest, 16)
            with sp.Fori(0, NG) as g:
                sp.wait_ge(s_res, g + 1)
                sp.dma_start(out[bass.ds(g * GRP, GRP), :, :].rearrange("b t f -> t b f"),
                             res[:, bass.ds(g * GRP, GRP), :]).then_inc(stored, 16)
            sp.wait_ge(stored, 16 * NG)


        @block.gpsimd
        def _(g):
            q = nc.gpsimd
            q.memset(w1_n[:, FC - 1, :], 0.0).then_inc(padded, 1)
            q.memset(w3_n[:, FC - 1, :], 0.0).then_inc(padded, 1)
            q.memset(w2_n[:, FFN:], 0.0).then_inc(padded, 1)
            q.memset(ident[:, :], 0.0).then_inc(consts, 1)
            q.memset(identb[:, :], 0.0).then_inc(consts, 1)
            q.memset(sel[:, :, :], 0.0).then_inc(consts, 1)
            q.memset(blocks[:, :], 1.0).then_inc(consts, 1)
            q.memset(ones[:, :], 1.0)
            q.memset(three_halves[:, :], 1.5).then_inc(consts, 1)
            g.wait_ge(consts, 5)
            for m in (ident, identb):
                q.affine_select(out=m[:, :], in_=m[:, :], compare_op=ALU.not_equal, fill=1.0, base=0,
                                pattern=[[-1, 128]], channel_multiplier=1).then_inc(consts, 1)
            for k in (0, 1):
                q.affine_select(out=sel[:, :, :], in_=sel[:, :, :], compare_op=ALU.not_equal, fill=1.0,
                                base=-H * k, pattern=[[-1, H], [0, 128]], channel_multiplier=1).then_inc(consts, 1)
                g.wait_ge(consts, 8 + k)
            bl = blocks[:, :].rearrange("p (a b) -> p a b", b=DH)
            q.affine_select(out=bl, in_=bl, compare_op=ALU.is_ge, fill=0.0, base=0,
                            pattern=[[-DH, H], [0, DH]], channel_multiplier=1).then_inc(consts, 1)
            g.wait_ge(consts, 10)
            q.affine_select(out=bl, in_=bl, compare_op=ALU.is_ge, fill=0.0, base=DH - 1,
                            pattern=[[DH, H], [0, DH]], channel_multiplier=-1).then_inc(consts, 1)
            g.wait_ge(pv_a, N_SIN)
            g.wait_ge(ld_pos, 48)
            q.tensor_scalar(nsin[:, :, :], sincos[:, 0, :, :], -1.0, 1.0, ALU.mult, ALU.mult).then_inc(pv_g, 1)
            g.wait_ge(pv_g, 1)
            for s in range(2):
                for e in range(2):
                    own, other = s * DH, 2 * DH + s * DH
                    w_e = qkw[:, s:s + 1, e:ROPE:2].to_broadcast([128, B, AXES])
                    w_o = qkw[:, s:s + 1, 1 - e:ROPE:2].to_broadcast([128, B, AXES])
                    q.tensor_tensor(rope[:, :, own + e:own + ROPE:2], sincos[:, 1, :, :], w_e, ALU.mult).then_inc(pv_g, 1)
                    sn = sincos[:, 0, :, :] if e else nsin[:, :, :]
                    q.tensor_tensor(rope[:, :, other + e:other + ROPE:2], sn, w_o, ALU.mult).then_inc(pv_g, 1)
                q.tensor_copy(rope[:, :, own + ROPE:own + DH],
                              qkw[:, s:s + 1, ROPE:DH].to_broadcast([128, B, DH - ROPE])).then_inc(pv_g, 1)
                q.memset(rope[:, :, other + ROPE:other + DH], 0.0).then_inc(pv_g, 1)

            def step(t, p):
                b, p = t + LEAD, (p + LEAD) % 2
                if not is_seq(b):
                    return
                g.wait_ge(s_ss, SEED * b + SEED)
                y_, s_, t_ = qv_y[p][:, :], qv_s[p][:, :], qv_t[:, :]
                for k in range(3):
                    q.tensor_tensor(t_, y_, y_, ALU.mult).then_inc(s_newton, 1)
                    g.wait_ge(s_newton, NEWT * b + 4 * k + 1)
                    q.tensor_tensor(t_, t_, s_, ALU.mult).then_inc(s_newton, 1)
                    g.wait_ge(s_newton, NEWT * b + 4 * k + 2)
                    q.tensor_tensor(t_, three_halves[:, :], t_, ALU.subtract).then_inc(s_newton, 1)
                    g.wait_ge(s_newton, NEWT * b + 4 * k + 3)
                    q.tensor_tensor(y_, y_, t_, ALU.mult).then_inc(s_newton, 1)
                    g.wait_ge(s_newton, NEWT * b + 4 * k + 4)
                g.wait_ge(s_qk, b + 1)
                q.tensor_tensor(qn[:, :, :], qk[p][:, :, :],
                                qv_y[p][:, :].unsqueeze(2).to_broadcast([128, 2 * H, DH]), ALU.mult).then_inc(s_rot, 1)
                g.wait_ge(s_rot, ROT * b + 1)
                g.wait_ge(s_fac, b + 1)
                wait(g, s_parts, PARTS * (b - 2) + PARTS)
                f4 = fac[p][:, 0:TBL].rearrange("p (u s d) -> p u s d", u=2, s=2)
                qn4 = qn[:, :, :].rearrange("p (s h) d -> p s h d", s=2)
                rot4 = rot[p][:, :, :].rearrange("p (s h) d -> p s h d", s=2)
                pa4 = partner[:, :, :].rearrange("p (s h) d -> p s h d", s=2)
                for s in range(2):
                    q.tensor_tensor(rot4[:, s, :, :], qn4[:, s, :, :],
                                    f4[:, 0, s:s + 1, :].to_broadcast([128, H, DH]), ALU.mult)
                    for e in range(2):
                        last = q.tensor_tensor(pa4[:, s, :, e::2], qn4[:, s, :, 1 - e:ROPE:2],
                                               f4[:, 1, s:s + 1, e:ROPE:2].to_broadcast([128, H, AXES]), ALU.mult)
                    last.then_inc(s_rot, 1)
                g.wait_ge(s_rot, ROT * b + 3)
                q.tensor_tensor(rot[p][:, :, 0:ROPE], rot[p][:, :, 0:ROPE], partner[:, :, :], ALU.add).then_inc(s_rot, 2)

            steps(g, step)
            blocks_gpsimd(g)


        @block.scalar
        def _(a):
            q = nc.scalar
            for i in range(4):
                a.dma_start(xin[:, 4 * i:4 * i + 4, :], x[4 * i:4 * i + 4, :, :].rearrange("b t f -> t b f")).then_inc(ld_x, 16)
            a.dma_start(ada_n[:, :, :], ada_w.rearrange("(c p) f -> p c f", p=128)).then_inc(ld_ada, 16)
            a.dma_start(posn[:, :].rearrange("p (b c) -> p b c", c=AXES), pos.rearrange("b t c -> t b c")).then_inc(ld_pos, 16)
            for s, w in enumerate((q_norm_w, k_norm_w)):
                a.dma_start(qkw[:, s, :], w.partition_broadcast(128)).then_inc(ld_pos, 16)
            a.dma_start(proj_n[:, :], proj_w).then_inc(ld_ada, 16)
            a.wait_ge(pv_v, V_ANG)
            q.activation(sincos[:, :, :, :].rearrange("p s b c -> p (s b c)"),
                         ang[:, :, :].rearrange("p s n -> p (s n)"), ACT.Sin).then_inc(pv_a, 1)
            a.wait_ge(ld_x, 64)
            q.activation(big[:, :, :], xin[:, :, :], ACT.Square).then_inc(pv_a, 1)
            a.wait_ge(pt, P_ADA)
            q.activation(adaT[:, 0:512], bank[1][:, :], ACT.Copy).then_inc(pv_a, 1)
            q.activation(adaT[:, 512:768], bank[2][:, 0:256], ACT.Copy).then_inc(pv_a, 1)
            q.activation(projT[:, :], bank[2][:, 256:384], ACT.Copy).then_inc(pv_a, 1)
            a.wait_ge(pv_v, V_COND)
            q.activation(ctanh[:, :], condT[:, :], ACT.Tanh, scale=0.5).then_inc(pv_a, 1)
            a.wait_ge(pt, P_W1)
            q.activation(w1T[:, :], bank[5][:, 0:FC * 128], ACT.Copy).then_inc(pv_a, 1)
            a.wait_ge(pt, P_W3)
            q.activation(w3T[:, :], bank[6][:, 0:FC * 128], ACT.Copy).then_inc(pv_a, 1)
            a.wait_ge(pt, P_W2)
            q.activation(w2T[:, :, :].rearrange("p c f -> p (c f)"), bank[7][:, 0:FC * 128], ACT.Copy, scale=0.5).then_inc(pv_a, 1)
            q.activation(outw[:, :], outw_n[:, :], ACT.Copy, scale=0.5).then_inc(pv_a, 1)
            a.wait_ge(seeded, 6)

            def step(t, p):
                q1, q0 = (p + 1) % 2, p
                if is_seq(t - 1):
                    b = t - 1
                    a.wait_ge(s_o, NC * b + NC)
                    wait(a, s_oq, b)
                    q.activation(oT4[:, :], bank[O_BANK][:, :], ACT.Copy).then_inc(s_oT4, 1)

                def exp(c):
                    if is_seq(t):
                        a.wait_ge(s_e, NC * t + c + 1)
                        wait(a, s_o, NC * (t - 1) + c + 1)
                        q.activation(probs[c][:, :, :].rearrange("p h t -> p (h t)"), bank[E_BANK[c % 2]][:, :],
                                     ACT.Exp, scale=SCALE).then_inc(s_p, 1)
                exp(0)
                if is_seq(t + 4):
                    b = t + 4
                    a.wait_ge(s_xsT, b + 1)
                    a.wait_ge(s_fac, b + 1)
                    wait(a, s_qkv, b - 1)
                    q.activation(hT[q0][:, :], bank[W_BANK][:, 0:T], ACT.Identity,
                                 bias=fac[q0][:, TBL + 1:TBL + 2], scale=fac[q0][:, TBL:TBL + 1]).then_inc(s_hT, 1)
                exp(1)
                exp(2)
                if is_seq(t + 2):
                    b = t + 2
                    a.wait_ge(s_kTp, b + 1)
                    wait(a, s_e, NC * (b - 2) + NC)
                    kb = bank[K_BANK][:, :].bitcast(BF16).rearrange("p (j t) -> p j t", t=T)
                    q.activation(kT[q0][0:64, :, 0, :], kb[0:64], ACT.Copy)
                    q.activation(kT[q0][64:128, :, 1, :], kb[64:128], ACT.Copy).then_inc(s_kT, 1)
                if is_seq(t + 4):
                    b = t + 4
                    a.wait_ge(s_qkv, b + 1)
                    wait(a, s_ss, SEED * (b - 2) + 1)
                    qkp = bank[W_BANK][:, 0:2 * D]
                    q.activation(qk2[q0][:, :, :].rearrange("p h d -> p (h d)"), qkp, ACT.Square).then_inc(s_sq, 1)
                    wait(a, s_rot, ROT * (b - 2) + 1)
                    q.activation(qk[q0][:, :, :].rearrange("p h d -> p (h d)"), qkp, ACT.Copy).then_inc(s_qk, 1)
                exp(3)
                if is_seq(t - 1):
                    b = t - 1
                    a.wait_ge(s_oTp, b + 1)
                    wait(a, s_proj, b)
                    q.activation(oT[:, :], bank[W_BANK][:, 0:T], ACT.Copy).then_inc(s_oT, 1)
                    a.wait_ge(s_proj, b + 1)
                    a.wait_ge(s_gfac, b + 1)
                    wait(a, s_prT, b)
                    q.activation(pr[:, :], bank[W_BANK][:, 0:T], ACT.Identity, bias=gfac[q1][:, 1:2],
                                 scale=gfac[q1][:, 0:1]).then_inc(s_pr, 1)
                if is_seq(t + 1):
                    b = t + 1
                    a.wait_ge(s_mTp, b + 1)
                    wait(a, s_e, NC * (b - 2) + NC)
                    q.activation(mT[q1][:, :], bank[E_BANK[0]][:, 0:T // 2].bitcast(BF16), ACT.Copy).then_inc(s_mT, 1)

            steps(a, step)
            blocks_scalar(a)


        @block.vector
        def _(v):
            q = nc.vector
            n = 0

            def did(ins):
                nonlocal n
                n += 1
                ins.then_inc(pv_v, 1)
                v.wait_ge(pv_v, n)

            for p in range(2):
                q.memset(parts[p][:, :, :, :].rearrange("p s h d -> p (s h d)").bitcast(F32), 0.0)
                q.memset(kT[p][:, :, :, :].rearrange("p j s t -> p (j s t)").bitcast(F32), 0.0)
                q.memset(vpad[p][:, :, :], 0.0).then_inc(seeded, 1)
            q.memset(mparts[:, :].bitcast(F32), 0.0).then_inc(seeded, 1)
            v.wait_ge(seeded, 3)
            for p in range(2):
                q.memset(vpad[p][:, :, DH:DH + 1], 1.0).then_inc(seeded, 1)
            q.memset(qvb[:, :, 2 * D:], 1.0).then_inc(seeded, 1)
            v.wait_ge(ld_pos, 48)
            r0, r1 = ang[:, 0, :], ang[:, 1, :]
            did(q.tensor_scalar(turns[:, :], posn[:, :], 1.0 / (2 * math.pi), ROUND, ALU.mult, ALU.add))
            did(q.tensor_scalar(turns[:, :], turns[:, :], -ROUND, None, ALU.add))
            did(q.scalar_tensor_tensor(r0, turns[:, :], -TWO_PI_A, posn[:, :], ALU.mult, ALU.add))
            did(q.scalar_tensor_tensor(r0, turns[:, :], -TWO_PI_B, r0, ALU.mult, ALU.add))
            did(q.scalar_tensor_tensor(r0, turns[:, :], -TWO_PI_C, r0, ALU.mult, ALU.add))
            did(q.scalar_tensor_tensor(r1, r0, -1.0, r0, ALU.mult, ALU.max))
            did(q.tensor_scalar(r1, r1, -1.0, math.pi / 2, ALU.mult, ALU.add))
            did(q.tensor_scalar(r0, r0, PI_BELOW, -PI_BELOW, ALU.min, ALU.max))
            assert n == V_ANG
            v.wait_ge(pt, P_COND)
            did(q.tensor_copy(par[:, :], bank[0][:, 0:NROW]))
            did(q.tensor_copy(condT[:, :], bank[0][:, 32:32 + B]))
            assert n == V_COND
            v.wait_ge(pv_a, 2)
            did(q.tensor_reduce(ms[:, :], big[:, :, :], X_AXIS, ALU.add))
            did(q.tensor_scalar(ms[:, :], ms[:, :], 1.0 / D, EPS0, ALU.mult, ALU.add))
            n = rsqrt(v, pv_v, n, rstd_x[:, :], ms[:, :], rt[:, :])
            v.wait_ge(pt, P_QKV)
            did(q.tensor_copy(qkvT[:, :], bank[3][:, 0:3 * D]))
            v.wait_ge(pt, P_MOD)
            did(q.tensor_tensor(modr[:, :, :], bank[4][:, 0:6 * B].rearrange("p (c b) -> p c b", b=B),
                                par[:, R_ADA:R_ADA + 6].unsqueeze(2).to_broadcast([128, 6, B]), ALU.add))
            did(q.tensor_scalar(mods[:, :, A1], modr[:, 1, :], 1.0, par[:, R_N1:R_N1 + 1], ALU.add, ALU.mult))
            did(q.tensor_copy(mods[:, :, S1], modr[:, 0, :]))
            did(q.tensor_copy(mods[:, :, G1], modr[:, 2, :]))
            did(q.tensor_scalar(mods[:, :, GB1], modr[:, 2, :], par[:, R_PB:R_PB + 1], None, ALU.mult))
            did(q.tensor_scalar(mods[:, :, A2], modr[:, 4, :], 1.0, par[:, R_N2:R_N2 + 1], ALU.add, ALU.mult))
            did(q.tensor_copy(mods[:, :, S2], modr[:, 3, :]))
            did(q.tensor_copy(mods[:, :, G2], modr[:, 5, :]))
            did(q.tensor_copy(mods[:, :, GATE], condT[:, :]))
            did(q.tensor_scalar(mods[:, :, GO], condT[:, :], par[:, R_OB:R_OB + 1], None, ALU.mult))
            v.wait_ge(pv_a, 6)
            did(q.scalar_tensor_tensor(csilu[:, :], ctanh[:, :], 1.0, condT[:, :], ALU.add, ALU.mult))
            did(q.tensor_scalar(csilu[:, :], csilu[:, :], 0.5, None, ALU.mult))
            assert n == N_CSILU
            did(q.tensor_scalar(nbb[:, :], par[:, R_NB:R_NB + 1].to_broadcast([128, 128]), 1.0, None, ALU.mult))
            assert n == N_NBB
            v.wait_ge(ld_rest, N_REST)
            did(q.tensor_scalar(lin[:, :, :], lin_n[:, :, :], par[:, R_NG:R_NG + 1], None, ALU.mult))
            v.wait_ge(pt, P_BIAS)
            did(q.tensor_copy(bias_qv[:, :], bank[3][:, 0:2 * D]))
            did(q.tensor_tensor(bias_k[:, :], bank[3][:, 2 * D:2 * D + 1], par[:, R_BK:R_BK + 1], ALU.add))
            v.wait_ge(pt, P_EMB)
            did(q.tensor_tensor(embr[:, :, :], bank[4][:, 0:2 * B].rearrange("p (c b) -> p c b", b=B),
                                par[:, R_EB:R_EB + 2].unsqueeze(2).to_broadcast([128, 2, B]), ALU.add))
            did(q.tensor_scalar(mods[:, :, A3], embr[:, 0, :], 1.0, par[:, R_SG:R_SG + 1], ALU.add, ALU.mult))
            did(q.tensor_scalar(mods[:, :, S3], embr[:, 0, :], 1.0, par[:, R_SB:R_SB + 1], ALU.add, ALU.mult))
            did(q.tensor_tensor(mods[:, :, S3], mods[:, :, S3], embr[:, 1, :], ALU.add))
            assert n == N_DONE
            v.wait_ge(pv_g, 13)

            def step(t, p):
                q0, q1 = p, (p + 1) % 2
                if is_seq(t + 4):
                    b = t + 4
                    wait(v, s_xsT, b - 1)
                    q.tensor_scalar(xs[q0][:, :], xin[:, bass.ds(b, 1), :].rearrange("p a f -> p (a f)"),
                                    rstd_x[:, bass.ds(b, 1)], None, ALU.mult).then_inc(s_xs, 1)
                    wait(v, s_rot, ROT * (b - 2) + ROT)
                    wait(v, s_hT, b - 1)
                    q.tensor_scalar(fac[q0][:, 0:TBL], rope[:, bass.ds(b, 1), :].rearrange("p a f -> p (a f)"), 1.0, None, ALU.mult)
                    q.tensor_scalar(fac[q0][:, TBL:TBL + 2], mods[:, bass.ds(b, 1), A1:A1 + 2].rearrange("p a f -> p (a f)"),
                                    1.0, None, ALU.mult).then_inc(s_fac, 1)
                if is_seq(t - 1):
                    b = t - 1
                    v.wait_ge(s_oq, b + 1)
                    oq = bank[O_BANK][:, :].rearrange("p (h w) -> p h w", w=VW)
                    q.reciprocal(rsum[:, :], oq[:, :, DH:DH + 1].rearrange("p h a -> p (h a)")).then_inc(s_rec, 1)
                    v.wait_ge(s_rec, b + 1)
                    wait(v, s_oTp, b)
                    q.tensor_tensor(o[:, :, :], oq[:, :, 0:DH],
                                    rsum[:, :].unsqueeze(2).to_broadcast([128, H, DH]), ALU.mult).then_inc(s_on, 1)
                    wait(v, s_pr, b - 1)
                    q.tensor_scalar(gfac[q1][:, :], mods[:, bass.ds(b, 1), G1:G1 + 2].rearrange("p a f -> p (a f)"),
                                    1.0, None, ALU.mult).then_inc(s_gfac, 1)

                def rowmax(c):
                    if is_seq(t + 1):
                        b = t + 1
                        v.wait_ge(s_s, NC * b + c + 1)
                        if c == 0:
                            wait(v, s_mp, b - 1)
                        q.tensor_reduce(nmax[q1][:, c * HPC:(c + 1) * HPC],
                                        bank[S_BANK[c % 2]][:, :].rearrange("p (h t) -> p h t", t=T),
                                        X_AXIS, ALU.max, negate=True).then_inc(s_max, 1)
                rowmax(0)
                if is_seq(t + 1):
                    b = t + 1
                    v.wait_ge(s_vall, b + 1)
                    wait(v, s_o, NC * (b - 2) + NC)
                    q.tensor_scalar(vpad[q1][:, :, 0:DH], vall[:, bass.ds(b, 1), :].rearrange("p a (h d) -> p (a h) d", d=DH),
                                    1.0, None, ALU.mult).then_inc(s_vpad, 1)
                rowmax(1)
                if is_seq(t + 2):
                    b = t + 2
                    v.wait_ge(s_qTp, b + 1)
                    wait(v, s_e, NC * (b - 2) + NC)
                    q.tensor_copy(qT[q0][:, :, :].rearrange("p j t -> p (j t)"), bank[Q_BANK][:, :].bitcast(BF16)).then_inc(s_qT, 1)
                rowmax(2)
                if is_seq(t + 4):
                    b = t + 4
                    v.wait_ge(s_qk, b + 1)
                    q.tensor_scalar(vall[:, bass.ds(b, 1), :].rearrange("p a f -> p (a f)"), bank[W_BANK][:, 2 * D:3 * D],
                                    1.0, None, ALU.mult).then_inc(s_vall, 1)
                rowmax(3)
                if is_seq(t + 1):
                    b = t + 1
                    v.wait_ge(s_max, NC * b + NC)
                    wait(v, s_mTp, b)
                    q.tensor_copy(mparts[:, 0:H], nmax[q1][:, :]).then_inc(s_mh, 1)
                    v.wait_ge(s_mh, b + 1)
                    q.tensor_tensor(mparts[:, H:2 * H], nmax[q1][:, :], mparts[:, 0:H], ALU.subtract).then_inc(s_mp, 1)
                if is_seq(t + 4):
                    b = t + 4
                    v.wait_ge(s_sq, b + 1)
                    wait(v, s_newton, NEWT * (b - 2) + NEWT)
                    q.tensor_reduce(qv_ms[q0][:, :], qk2[q0][:, :, :], X_AXIS, ALU.add).then_inc(s_ss, 1)
                    v.wait_ge(s_ss, SEED * b + 1)
                    q.tensor_scalar(qv_s[q0][:, :], qv_ms[q0][:, :], 0.5 / DH, 0.5 * EPS0, ALU.mult, ALU.add).then_inc(s_ss, 1)
                    v.wait_ge(s_ss, SEED * b + 2)
                    q.tensor_scalar(qv_ms[q0][:, :].bitcast(I32), qv_s[q0][:, :].bitcast(I32), 1, None,
                                    ALU.logical_shift_right).then_inc(s_ss, 1)
                    v.wait_ge(s_ss, SEED * b + 3)
                    wait(v, s_rot, ROT * (b - 2) + 1)
                    q.tensor_scalar(qv_y[q0][:, :].bitcast(I32), qv_ms[q0][:, :].bitcast(I32), -1.0, float(MAGIC - 2 ** 22),
                                    ALU.mult, ALU.add).then_inc(s_ss, 1)
                if is_seq(t + 3):
                    b = t + 3
                    pp = parts[q1]
                    both = pp[:, :, :, :].rearrange("p s h (k d) -> p (s h) k d", d=DH)
                    pq = pp[:, 0, :, :].rearrange("p h (k d) -> p h k d", d=DH)
                    pk = pp[:, 1, :, :].rearrange("p h (k d) -> p h k d", d=DH)
                    rq = rot[q1]
                    v.wait_ge(s_rot, ROT * b + ROT)
                    wait(v, s_kTp, b - 1)
                    base = PARTS * b
                    q.tensor_copy(both[:, :, 2, :], rq[:, :, :]).then_inc(s_parts, 1)
                    v.wait_ge(s_parts, base + 1)
                    q.tensor_tensor(rest[:, :, :], rq[:, :, :], both[:, :, 2, :], ALU.subtract).then_inc(s_parts, 1)
                    v.wait_ge(s_parts, base + 2)
                    q.tensor_copy(both[:, :, 5, :], rest[:, :, :]).then_inc(s_parts, 1)
                    v.wait_ge(s_parts, base + 3)
                    q.tensor_tensor(pq[:, :, 4, :], rest[:, 0:H, :], pq[:, :, 5, :], ALU.subtract).then_inc(s_parts, 1)
                    q.tensor_tensor(pk[:, :, 1, :], rest[:, H:, :], pk[:, :, 5, :], ALU.subtract).then_inc(s_parts, 1)
                    q.tensor_copy(pq[:, :, 0:2, :], pq[:, :, 2:3, :].to_broadcast([128, H, 2, DH])).then_inc(s_parts, 1)
                    q.tensor_copy(pk[:, :, 3:5, :], pk[:, :, 2:3, :].to_broadcast([128, H, 2, DH])).then_inc(s_parts, 1)
                    q.tensor_copy(pq[:, :, 3, :], pq[:, :, 5, :]).then_inc(s_parts, 1)
                    q.tensor_copy(pk[:, :, 0, :], pk[:, :, 5, :]).then_inc(s_parts, 1)
                if is_seq(t - 1):
                    b = t - 1
                    v.wait_ge(s_prT, b + 1)
                    q.tensor_tensor(x1[:, bass.ds(b, 1), :].rearrange("p a f -> p (a f)"), bank[W_BANK][:, 0:D],
                                    xin[:, bass.ds(b, 1), :].rearrange("p a f -> p (a f)"), ALU.add).then_inc(s_x1, 1)

            steps(v, step)
            blocks_vector(v)

        @block.tensor
        def _(e):
            q = nc.tensor
            e.wait_ge(consts, 11)
            e.wait_ge(ld_small, N_SMALL)
            q.transpose(bank[0][:, 0:NROW], params_n[:, :], ident[0:NROW, 0:NROW])
            q.transpose(bank[0][:, 32:32 + B], cond_n[:, :], ident[0:B, 0:B]).then_inc(pt, 1)
            e.wait_ge(ld_ada, 32)
            for c in range(6):
                q.transpose(bank[1 + c // 4][:, c % 4 * 128:c % 4 * 128 + 128], ada_n[:, c, :], ident[:, :])
            q.transpose(bank[2][:, 256:384], proj_n[:, :], ident[:, :]).then_inc(pt, 1)
            e.wait_ge(ld_qkv, 16)
            for c in range(3):
                last = q.transpose(bank[3][:, c * 128:c * 128 + 128], qkv_n[:, c, :], ident[:, :])
            last.then_inc(pt, 1)
            e.wait_ge(pv_v, V_COND)
            e.wait_ge(pv_a, 4)
            for c in range(6):
                last = q.matmul(bank[4][:, c * B:(c + 1) * B], adaT[:, c * 128:c * 128 + 128], condT[:, :], start=True, stop=True)
            last.then_inc(pt, 1)
            e.wait_ge(ld_rest, N_REST)
            for k, src in ((5, w1_n), (6, w3_n)):
                for c in range(FC):
                    last = q.transpose(bank[k][:, c * 128:c * 128 + 128], src[:, c, :], ident[:, :])
                last.then_inc(pt, 1)
            for c in range(FC):
                last = q.transpose(bank[7][:, c * 128:c * 128 + 128], w2_n[:, c * 128:c * 128 + 128], ident[:, :])
            last.then_inc(pt, 1)
            e.wait_ge(pv_v, N_NBB)
            q.matmul(bank[3][:, 0:2 * D], nbb[:, :], lin_n[:, 0:2, :].rearrange("p c f -> p (c f)"), start=True, stop=False)
            q.matmul(bank[3][:, 0:2 * D], ones[:, :], bqv[:, :], start=False, stop=True)
            q.matmul(bank[3][:, 2 * D:2 * D + 1], lin_n[:, 2, :], nbb[:, 0:1], start=True, stop=True).then_inc(pt, 1)
            for c in range(2):
                last = q.matmul(bank[4][:, c * B:(c + 1) * B], emb_n[:, c * 128:c * 128 + 128], csilu[:, :], start=True, stop=True)
            last.then_inc(pt, 1)
            e.wait_ge(pv_v, N_DONE)
            e.wait_ge(pv_a, 10)
            e.wait_ge(seeded, 6)

            def step(t, p):
                q0, q1 = p, (p + 1) % 2

                def weighted(c):
                    if not is_seq(t):
                        return
                    if c == 0:
                        e.wait_ge(s_mT, t + 1)
                    wait(e, s_p, NC * t + c - 1)
                    for i in range(HPC):
                        h = c * HPC + i
                        dst = bank[E_BANK[c % 2]][:, i * T:(i + 1) * T]
                        q.matmul(dst, kT[q0][:, h // 2, h % 2, :], qT[q0][:, h // 2, :], start=True, stop=False)
                        last = q.matmul(dst, sel[:, h, :], mT[q0][:, :], start=False, stop=True)
                    last.then_inc(s_e, 1)

                def scores(c):
                    if not is_seq(t + 1):
                        return
                    b = t + 1
                    if c == 0:
                        e.wait_ge(s_qT, b + 1)
                        e.wait_ge(s_kT, b + 1)
                    wait(e, s_max, NC * b + c - 1)
                    for i in range(HPC // 2):
                        j = c * (HPC // 2) + i
                        last = q.matmul(bank[S_BANK[c % 2]][:, i * 2 * T:(i + 1) * 2 * T], qT[q1][:, j, :],
                                        kT[q1][:, j, :, :].rearrange("p s t -> p (s t)"), start=True, stop=True)
                    last.then_inc(s_s, 1)

                def values(c):
                    if not is_seq(t):
                        return
                    if c == 0:
                        e.wait_ge(s_vpad, t + 1)
                        wait(e, s_on, t)
                    e.wait_ge(s_p, NC * t + c + 1)
                    for i in range(HPC):
                        last = q.matmul(bank[O_BANK][VW * i:VW * (i + 1), c * T:(c + 1) * T], vpad[q0][:, c * HPC + i, :],
                                        probs[c][:, i, :], start=True, stop=True)
                    last.then_inc(s_o, 1)

                def stack(s, sm, bk_, freed):
                    b = t + 2
                    for j in range(PAIRS):
                        last = q.transpose(bank[bk_][:, j * T // 2:(j + 1) * T // 2].bitcast(BF16),
                                           parts[q0][:, s, 2 * j:2 * j + 2, :].rearrange("p h k -> p (h k)"), identb[:, :])
                    last.then_inc(sm, 1)

                weighted(0)
                if is_seq(t - 1):
                    b = t - 1
                    e.wait_ge(s_oT4, b + 1)
                    for i in range(NC):
                        last = q.transpose(bank[O_BANK][:, i * T:(i + 1) * T], oT4[:, i * T:(i + 1) * T], ident[:, :])
                    last.then_inc(s_oq, 1)
                scores(0)
                weighted(1)
                if is_seq(t + 4):
                    b = t + 4
                    e.wait_ge(s_xs, b + 1)
                    wait(e, s_x1, t - 1)
                    wait(e, s_vall, b)
                    q.transpose(bank[W_BANK][:, 0:T], xs[q0][:, :], ident[:, :]).then_inc(s_xsT, 1)
                values(0)
                scores(1)
                if is_seq(t + 2):
                    e.wait_ge(s_parts, PARTS * (t + 2) + PARTS)
                    wait(e, s_qT, t + 2)
                    stack(0, s_qTp, Q_BANK, s_qT)
                weighted(2)
                values(1)
                scores(2)
                if is_seq(t + 2):
                    wait(e, s_kT, t + 2)
                    stack(1, s_kTp, K_BANK, s_kT)
                if is_seq(t + 4):
                    b = t + 4
                    e.wait_ge(s_hT, b + 1)
                    q.matmul(bank[W_BANK][:, 0:3 * D], hT[q0][:, :], qkvT[:, :], start=True, stop=True).then_inc(s_qkv, 1)
                weighted(3)
                values(2)
                scores(3)
                if is_seq(t - 1):
                    b = t - 1
                    e.wait_ge(s_on, b + 1)
                    if is_seq(t + 4):
                        e.wait_ge(s_vall, t + 4 + 1)
                    else:
                        wait(e, s_x1, b)
                        e.wait_ge(s_vall, B)
                    q.transpose(bank[W_BANK][:, 0:T], o[:, :, :].rearrange("p h d -> p (h d)"), ident[:, :]).then_inc(s_oTp, 1)
                values(3)
                if is_seq(t - 1):
                    b = t - 1
                    e.wait_ge(s_oT, b + 1)
                    q.matmul(bank[W_BANK][:, 0:T], projT[:, :], oT[:, :], start=True, stop=True).then_inc(s_proj, 1)
                    e.wait_ge(s_pr, b + 1)
                    q.transpose(bank[W_BANK][:, 0:D], pr[:, :], ident[:, :]).then_inc(s_prT, 1)
                if is_seq(t + 1):
                    b = t + 1
                    e.wait_ge(s_mp, b + 1)
                    wait(e, s_p, NC * t + NC - 1)
                    q.transpose(bank[E_BANK[0]][:, 0:T // 2].bitcast(BF16), mparts[:, :], identb[:, :]).then_inc(s_mTp, 1)

            steps(e, step)
            blocks_tensor(e)


_INS = ['x', 'cond_1024', 'fside_BxSx3_0', 'L0_cond_norm1_w', 'L0_cond_qkv_w', 'L0_cond_q_norm_w', 'L0_cond_k_norm_w',
        'L0_cond_proj_w', 'L0_cond_proj_b', 'L0_cond_norm2_w', 'L0_cond_w1', 'L0_cond_w3', 'L0_cond_w2', 'L0_cond_ada_w',
        'L0_cond_ada_b', 'L1_cond_norm_g', 'L1_cond_norm_b', 'L1_cond_Wq', 'L1_cond_bq', 'L1_cond_Wk', 'L1_cond_bk',
        'L1_cond_Wv', 'L1_cond_bv', 'L1_cond_emb_W', 'L1_cond_emb_b', 'L1_cond_sn_g', 'L1_cond_sn_b', 'L1_cond_out_W',
        'L1_cond_out_b']


def kernel(**inputs):
    import numpy as _np
    import concourse.bacc as _bacc
    from concourse import mybir as _mybir
    from concourse.bass_utils import run_bass_kernel_spmd as _run

    nc = _bacc.Bacc("TRN2", target_bir_lowering=False, num_devices=1)
    arrays, args = {}, []
    for name in _INS:
        a = _np.ascontiguousarray(inputs[name])
        arrays[f"in_{name}_dram"] = a
        args.append(nc.dram_tensor(f"in_{name}_dram", a.shape, _mybir.dt.from_np(a.dtype), kind="ExternalInput").ap())
    args.append(nc.dram_tensor("out_0_dram", (B, T, D), _mybir.dt.float32, kind="ExternalOutput").ap())
    dit_then_linear_attention(nc, *args)
    r = _run(nc, [arrays], core_ids=[0])
    return r.results[0]["out_0_dram"]
```

```python
import math

import numpy as np
import concourse.bass as bass
from concourse import mybir
from concourse.alu_op_type import AluOpType as ALU
from contextlib import ExitStack

F32 = mybir.dt.float32
BF16 = mybir.dt.bfloat16
I32 = mybir.dt.int32
ACT = mybir.ActivationFunctionType
X_AXIS = mybir.AxisListType.X

B, T, D = 16, 128, 128
H = 16
DH = D // H
ROPE = DH // 6 * 6
AXES = ROPE // 2
FFN = int(2 * (4 * D) / 3)
FC = -(-FFN // 128)
LAST = FFN - (FC - 1) * 128
UNIT = 2
U = B // UNIT
NG = 4
GRP = B // NG
SLOT = 64
HPC = 4
NC = H // HPC
PAIRS = H // 2
VW = 32
EPS0, EPS1 = 1e-6, 1e-5
SCALE = DH ** -0.5
MAGIC = 0x5F3759DF
ROUND = 1.5 * 2.0 ** 23
TWO_PI_A = 6.28125
TWO_PI_B = float(np.float32(round((2 * math.pi - TWO_PI_A) * 2 ** 21) / 2 ** 21))
TWO_PI_C = 2 * math.pi - TWO_PI_A - TWO_PI_B
PI_BELOW = 3.1415925

A1, S1, G1, GB1, A2, S2, G2, A3, S3, GATE, GO, NMOD = range(12)
R_ADA, R_N1, R_PB, R_N2, R_NG, R_NB, R_BK, R_EB, R_SG, R_SB, R_OB, NROW = 0, 6, 7, 8, 9, 10, 11, 12, 14, 15, 16, 17
TBL = 4 * DH

LEAD = 5


def is_seq(b):
    return not isinstance(b, int) or 0 <= b < B


def wait(eng, sem, value):
    if not isinstance(value, int) or value > 0:
        eng.wait_ge(sem, value)


def pipeline(eng, body, first, last, end, start):
    last = first + (last - first) // 2 * 2
    for t in range(start, first):
        body(t, t % 2)
    with eng.Fori(0, (last - first) // 2) as i:
        body(i * 2 + first, first % 2)
        body(i * 2 + (first + 1), (first + 1) % 2)
    for t in range(last, end):
        body(t, t % 2)


def steps(eng, body):
    pipeline(eng, body, 3, B - LEAD, B + 1, -LEAD)


def is_unit(u):
    return not isinstance(u, int) or 0 <= u < U


def units(eng, body, lead):
    pipeline(eng, body, 2, U - lead, U, -lead)


def dit_then_linear_attention(nc, x, cond, pos, norm1_w, qkv_w, q_norm_w, k_norm_w, proj_w, proj_b,
                              norm2_w, w1, w3, w2, ada_w, ada_b, norm_g, norm_b, Wq, bq, Wk, bk, Wv,
                              bv, emb_W, emb_b, sn_g, sn_b, out_W, out_b, out):
    ctx = ExitStack()
    with ctx:
        def sb(name, shape, dt=F32):
            return ctx.enter_context(nc.sbuf_tensor(name, shape, dt))

        def sem(name):
            return ctx.enter_context(nc.semaphore(name))

        ident = sb("ident", [128, 128])
        identb = sb("identb", [128, 128], BF16)
        ones = sb("ones", [1, 128])
        blocks = sb("blocks", [128, 128])
        sel = sb("sel", [128, H, 128], BF16)
        xin = sb("xin", [128, B, D])
        cond_n = sb("cond_n", [B, D])
        params_n = sb("params_n", [NROW, D])
        bqv = sb("bqv", [1, 2 * D])
        posn = sb("posn", [128, B * AXES])
        qkw = sb("qkw", [128, 2, DH])
        qkv_n = sb("qkv_n", [128, 3, D])
        proj_n = sb("proj_n", [128, D])
        w1_n = sb("w1_n", [128, FC, D])
        w3_n = sb("w3_n", [128, FC, D])
        w2_n = sb("w2_n", [128, FC * 128])
        ada_n = sb("ada_n", [128, 6, D])
        emb_n = sb("emb_n", [128, 2 * D])
        lin_n = sb("lin_n", [128, 3, D])
        outw_n = sb("outw_n", [128, D])
        adaT = sb("adaT", [128, 6 * D])
        qkvT = sb("qkvT", [128, 3 * D])
        projT = sb("projT", [128, D])
        w1T = sb("w1T", [128, FC * 128])
        w3T = sb("w3T", [128, FC * 128])
        w2T = sb("w2T", [128, FC, D])
        lin = sb("lin", [128, 3, D])
        outw = sb("outw", [128, D])
        nbb = sb("nbb", [128, 128])
        bias_qv = sb("bias_qv", [128, 2 * D])
        bias_k = sb("bias_k", [128, 1])
        par = sb("par", [128, NROW])
        condT = sb("condT", [128, B])
        csilu = sb("csilu", [128, B])
        ctanh = sb("ctanh", [128, B])
        modr = sb("modr", [128, 6, B])
        embr = sb("embr", [128, 2, B])
        mods = sb("mods", [128, B, NMOD])
        ang = sb("ang", [128, 2, B * AXES])
        sincos = sb("sincos", [128, 2, B, AXES])
        nsin = sb("nsin", [128, B, AXES])
        turns = sb("turns", [128, B * AXES])
        rope = sb("rope", [128, B, TBL])
        big = sb("big", [128, B, D])
        ms = sb("ms", [128, B])
        ry = sb("ry", [128, B])
        rt = sb("rt", [128, B])
        rstd_x = sb("rstd_x", [128, B])
        xs = [sb(f"xs{p}", [128, D]) for p in range(2)]
        hT = [sb(f"hT{p}", [128, T]) for p in range(2)]
        qk = [sb(f"qk{p}", [128, 2 * H, DH]) for p in range(2)]
        qk2 = [sb(f"qk2{p}", [128, 2 * H, DH]) for p in range(2)]
        qv_ms = [sb(f"qv_ms{p}", [128, 2 * H]) for p in range(2)]
        qv_s = [sb(f"qv_s{p}", [128, 2 * H]) for p in range(2)]
        qv_y = [sb(f"qv_y{p}", [128, 2 * H]) for p in range(2)]
        qv_t = sb("qv_t", [128, 2 * H])
        three_halves = sb("three_halves", [128, 2 * H])
        partner = sb("partner", [128, 2 * H, ROPE])
        rot = [sb(f"rot{p}", [128, 2 * H, DH]) for p in range(2)]
        rest = sb("rest", [128, 2 * H, DH])
        parts = [sb(f"parts{p}", [128, 2, H, SLOT], BF16) for p in range(2)]
        qT = [sb(f"qT{p}", [128, PAIRS, T], BF16) for p in range(2)]
        kT = [sb(f"kT{p}", [128, PAIRS, 2, T], BF16) for p in range(2)]
        nmax = [sb(f"nmax{p}", [128, H]) for p in range(2)]
        mparts = sb("mparts", [128, 128], BF16)
        mT = [sb(f"mT{p}", [128, T], BF16) for p in range(2)]
        probs = [sb(f"probs{c}", [128, HPC, T]) for c in range(NC)]
        vall = sb("vall", [128, B, D])
        vpad = [sb(f"vpad{p}", [128, H, VW]) for p in range(2)]
        oT4 = sb("oT4", [128, NC * T])
        rsum = sb("rsum", [128, H])
        o = sb("o", [128, H, DH])
        oT = sb("oT", [128, T])
        pr = sb("pr", [128, T])
        x1 = sb("x1", [128, B, D])
        def two(name, *shape):
            return [sb(f"{name}{p}", [128, *shape]) for p in range(2)]
        rstd1 = sb("rstd1", [128, B])
        xs2 = two("xs2", UNIT, D)
        hT2 = two("hT2", UNIT, T)
        th = [sb(f"th{c}", [128, UNIT * T]) for c in range(FC)]
        yg = [sb(f"yg{c}", [128, UNIT * T]) for c in range(FC)]
        ff = [sb(f"ff{c}", [128, UNIT * T]) for c in range(FC)]
        fg = sb("fg", [128, UNIT, T])
        x2 = sb("x2", [128, B, D])
        bn = sb("bn", [128, B, 6])
        mean2 = sb("mean2", [128, B])
        rstd2 = sb("rstd2", [128, B])
        kmax = sb("kmax", [128, UNIT])
        knb = two("knb", UNIT)
        kx = two("kx", UNIT, T)
        ksum = two("ksum", UNIT)
        krec = two("krec", UNIT)
        kxT = two("kxT", UNIT, D)
        qvb = two("qvb", UNIT, 2 * D)
        qmax = two("qmax", UNIT, H)
        qs = two("qs", UNIT, H, DH)
        qe = two("qe", UNIT, H, DH)
        qsum = sb("qsum", [128, UNIT, H])
        qrec = two("qrec", UNIT, H)
        qx = two("qx", UNIT, H, DH)
        qxT = two("qxT", UNIT, T)
        cx = two("cx", UNIT, D)
        y = sb("y", [128, B, D])
        mean3 = sb("mean3", [128, B])
        rstd3 = sb("rstd3", [128, B])
        hs = two("hs", UNIT * T)
        hg = two("hg", UNIT, T)
        res = sb("res", [128, B, D])

        bank = [ctx.enter_context(nc.psum_tensor(f"bank{i}", [128, 512], F32)) for i in range(8)]
        S_BANK, E_BANK, STACK_BANK, P_BANK, O_BANK, W_BANK = (0, 1), (2, 3), 4, 5, 6, 7

        ld_x = sem("ld_x")
        ld_small = sem("ld_small")
        ld_ada = sem("ld_ada")
        ld_qkv = sem("ld_qkv")
        ld_pos = sem("ld_pos")
        ld_rest = sem("ld_rest")
        consts = sem("consts")
        padded = sem("padded")
        seeded = sem("seeded")
        stored = sem("stored")
        pt = sem("pt")
        pv_v = sem("pv_v")
        pv_a = sem("pv_a")
        pv_g = sem("pv_g")
        s_xs = sem("s_xs")
        s_xsT = sem("s_xsT")
        s_hT = sem("s_hT")
        s_qkv = sem("s_qkv")
        s_sq = sem("s_sq")
        s_qk = sem("s_qk")
        s_vall = sem("s_vall")
        s_ss = sem("s_ss")
        s_newton = sem("s_newton")
        s_rot = sem("s_rot")
        s_hi = sem("s_hi")
        s_parts = sem("s_parts")
        s_st = sem("s_st")
        s_st0 = sem("s_st0")
        s_st1 = sem("s_st1")
        s_s = sem("s_s")
        s_max = sem("s_max")
        s_mh = sem("s_mh")
        s_mp = sem("s_mp")
        s_mTp = sem("s_mTp")
        s_mT = sem("s_mT")
        s_e = sem("s_e")
        s_p = sem("s_p")
        s_vpad = sem("s_vpad")
        s_o = sem("s_o")
        s_oT4 = sem("s_oT4")
        s_oq = sem("s_oq")
        s_rec = sem("s_rec")
        s_on = sem("s_on")
        s_oTp = sem("s_oTp")
        s_oT = sem("s_oT")
        s_proj = sem("s_proj")
        s_pr = sem("s_pr")
        s_prT = sem("s_prT")
        s_x1 = sem("s_x1")
        s_bn = sem("s_bn")
        s_res = sem("s_res")

        b_bn = sem("b_bn")
        b_ff = sem("b_ff")
        b_fg = sem("b_fg")
        b_fgT = sem("b_fgT")
        b_fm = sem("b_fm")
        b_gu = sem("b_gu")
        b_hT = sem("b_hT")
        b_rstd = sem("b_rstd")
        b_th = sem("b_th")
        b_x2 = sem("b_x2")
        b_xs = sem("b_xs")
        b_xsT = sem("b_xsT")
        b_y = sem("b_y")
        c_bn = sem("c_bn")
        c_ctx = sem("c_ctx")
        c_cx = sem("c_cx")
        c_hT = sem("c_hT")
        c_k = sem("c_k")
        c_km = sem("c_km")
        c_krec = sem("c_krec")
        c_kx = sem("c_kx")
        c_kxT = sem("c_kxT")
        c_kxTp = sem("c_kxTp")
        c_nb = sem("c_nb")
        c_qe = sem("c_qe")
        c_qmax = sem("c_qmax")
        c_qrec = sem("c_qrec")
        c_qs = sem("c_qs")
        c_qsum = sem("c_qsum")
        c_qv = sem("c_qv")
        c_qvb = sem("c_qvb")
        c_qx = sem("c_qx")
        c_qxT = sem("c_qxT")
        c_qxTp = sem("c_qxTp")
        c_rstd = sem("c_rstd")
        c_xc = sem("c_xc")
        c_xs = sem("c_xs")
        c_xsT = sem("c_xsT")
        c_y = sem("c_y")
        c_yp = sem("c_yp")
        d_hT = sem("d_hT")
        d_hg = sem("d_hg")
        d_hgT = sem("d_hgT")
        d_hs = sem("d_hs")
        d_op = sem("d_op")
        d_rstd = sem("d_rstd")
        d_th = sem("d_th")
        d_xc = sem("d_xc")
        d_xs = sem("d_xs")
        d_xsT = sem("d_xsT")

        N_CSILU, N_NBB, N_DONE = 10 + 2 + 11 + 1 + 10 + 2, 10 + 2 + 11 + 1 + 10 + 3, 10 + 2 + 11 + 1 + 10 + 3 + 7
        NEWT, ROT, PARTS, SEED = 12, 3, 6, 4
        RSTEPS, LSTEPS = 14, 14
        N_SIN = 1
        N_SMALL, N_REST = 16 * 12, 16 * 12
        P_COND, P_ADA, P_QKV, P_MOD, P_W1, P_W3, P_W2, P_BIAS, P_EMB = range(1, 10)
        V_ANG, V_COND = 8, 10

        block = ctx.enter_context(nc.Block())

        def rsqrt(v, sm, base, y_, s_, t_):
            n = base

            def did(ins):
                nonlocal n
                n += 1
                ins.then_inc(sm, 1)
                v.wait_ge(sm, n)
            did(nc.vector.tensor_scalar(t_.bitcast(I32), s_.bitcast(I32), 1, None, ALU.logical_shift_right))
            did(nc.vector.tensor_scalar(y_.bitcast(I32), t_.bitcast(I32), -1.0, float(MAGIC), ALU.mult, ALU.add))
            for _ in range(3):
                did(nc.vector.tensor_tensor(t_, y_, y_, ALU.mult))
                did(nc.vector.scalar_tensor_tensor(t_, t_, -0.5, s_, ALU.mult, ALU.mult))
                did(nc.vector.scalar_tensor_tensor(y_, t_, 1.5, y_, ALU.add, ALU.mult))
            return n

        def pair(u):
            return bass.ds(u * UNIT, UNIT)

        def flat(t_):
            return t_[:, :, :].rearrange("p u t -> p (u t)")

        def column(u, j, col):
            return mods[:, bass.ds(u * UNIT + j, 1), col:col + 1].rearrange("p a f -> p (a f)")

        def blocks_gpsimd(g):
            q = nc.gpsimd

            def normed(src, mean, rstd, centred, made, used):
                def step(t, p):
                    u, xs_ = t, xs2[p]
                    if not is_unit(u):
                        return
                    wait(g, used, u - 1)
                    x_ = src[:, pair(u), :]
                    if mean is not None:
                        q.tensor_tensor(xs_[:, :, :], x_, mean[:, pair(u)].unsqueeze(2).to_broadcast([128, UNIT, D]),
                                        ALU.subtract).then_inc(centred, 1)
                        g.wait_ge(centred, u + 1)
                        x_ = xs_[:, :, :]
                    q.tensor_tensor(xs_[:, :, :], x_, rstd[:, pair(u)].unsqueeze(2).to_broadcast([128, UNIT, D]),
                                    ALU.mult).then_inc(made, 1)
                return step

            g.wait_ge(b_rstd, RSTEPS)
            units(g, normed(x1, None, rstd1, None, b_xs, b_xsT), 0)

            c_normed = normed(x2, mean2, rstd2, c_xc, c_xs, c_xsT)

            def c_step(t, p):
                p1 = 1 - p
                c_normed(t + 3, p1)
                if is_unit(t + 1):
                    u = t + 1
                    g.wait_ge(c_qmax, u + 1)
                    wait(g, c_qe, u - 1)
                    q.tensor_tensor(qs[p1][:, :, :, :], qvb[p1][:, :, 0:D].rearrange("p u (h d) -> p u h d", d=DH),
                                    qmax[p1][:, :, :].unsqueeze(3).to_broadcast([128, UNIT, H, DH]), ALU.subtract).then_inc(c_qs, 1)
                if is_unit(t):
                    g.wait_ge(c_qrec, t + 1)
                    wait(g, c_qxTp, t - 1)
                    q.tensor_tensor(qx[p][:, :, :, :], qe[p][:, :, :, :],
                                    qrec[p][:, :, :].unsqueeze(3).to_broadcast([128, UNIT, H, DH]), ALU.mult).then_inc(c_qx, 1)
            g.wait_ge(c_rstd, LSTEPS)
            units(g, c_step, 3)

            g.wait_ge(d_rstd, LSTEPS)
            units(g, normed(y, mean3, rstd3, d_xc, d_xs, d_xsT), 0)

        def blocks_scalar(a):
            q = nc.scalar

            def modulated(u, p, sm):
                for j in range(UNIT):
                    last = q.activation(hT2[p][:, j, :], bank[0][:, j * T:(j + 1) * T], ACT.Identity,
                                        bias=column(u, j, S2 if sm is b_hT else S3), scale=column(u, j, A2 if sm is b_hT else A3))
                last.then_inc(sm, 1)

            def b_step(t, p):
                def tanh(c):
                    u = t + 1
                    if is_unit(u):
                        a.wait_ge(b_gu, FC * u + c + 1)
                        wait(a, b_y, FC * (u - 1) + c + 1)
                        q.activation(th[c][:, :], bank[1 + c][:, 0:UNIT * T], ACT.Tanh, scale=0.5).then_inc(b_th, 1)
                if is_unit(t + 2):
                    a.wait_ge(b_xsT, t + 3)
                    wait(a, b_gu, FC * (t + 1))
                tanh(0)
                if is_unit(t + 2):
                    modulated(t + 2, p, b_hT)
                tanh(1)
                tanh(2)
            units(a, b_step, 2)

            def c_step(t, p):
                p1 = 1 - p
                if is_unit(t + 1):
                    u = t + 1
                    a.wait_ge(c_nb, u + 1)
                    wait(a, c_kxTp, u - 1)
                    wait(a, c_krec, u - 1)
                    for j in range(UNIT):
                        last = q.activation(kx[p1][:, j, :], bank[1][:, j * T:(j + 1) * T], ACT.Exp,
                                            bias=knb[p1][:, j:j + 1], accum_out=ksum[p1][:, j:j + 1])
                    last.then_inc(c_kx, 1)
                    a.wait_ge(c_qs, u + 1)
                    wait(a, c_qx, u - 1)
                    q.activation(qe[p1][:, :, :, :].rearrange("p u h d -> p (u h d)"),
                                 qs[p1][:, :, :, :].rearrange("p u h d -> p (u h d)"), ACT.Exp).then_inc(c_qe, 1)
                if is_unit(t):
                    a.wait_ge(c_qxTp, t + 1)
                    wait(a, c_yp, t - 1)
                    q.activation(flat(qxT[p]), bank[6][:, 0:UNIT * D], ACT.Copy).then_inc(c_qxT, 1)
                if is_unit(t + 1):
                    u = t + 1
                    a.wait_ge(c_kxTp, u + 1)
                    wait(a, c_ctx, u - 1)
                    q.activation(flat(kxT[p1]), bank[4][:, 0:UNIT * D], ACT.Copy).then_inc(c_kxT, 1)
                if is_unit(t):
                    a.wait_ge(c_yp, t + 1)
                if is_unit(t + 3):
                    u = t + 3
                    a.wait_ge(c_xsT, u + 1)
                    wait(a, c_k, u - 1)
                    q.activation(flat(hT2[p1]), bank[0][:, 0:UNIT * T], ACT.Copy).then_inc(c_hT, 1)
                if is_unit(t):
                    q.activation(y[:, pair(t), :], bank[7][:, 0:UNIT * D].rearrange("p (u f) -> p u f", f=D), ACT.Copy).then_inc(c_y, 1)
            units(a, c_step, 3)

            def d_step(t, p):
                p1 = 1 - p
                if is_unit(t):
                    a.wait_ge(d_op, t + 1)
                    wait(a, d_hgT, t - 1)
                if is_unit(t + 2):
                    a.wait_ge(d_xsT, t + 3)
                    wait(a, d_hs, t + 1)
                if is_unit(t + 1):
                    a.wait_ge(d_hT, t + 2)
                    q.activation(th[p1][:, :], flat(hT2[p1]), ACT.Tanh, scale=0.5).then_inc(d_th, 1)
                if is_unit(t):
                    for j in range(UNIT):
                        last = q.activation(hg[p][:, j, :], bank[1][:, j * T:(j + 1) * T], ACT.Identity,
                                            bias=column(t, j, GO), scale=column(t, j, GATE))
                    last.then_inc(d_hg, 1)
                if is_unit(t + 2):
                    modulated(t + 2, p, d_hT)
            units(a, d_step, 2)

        def blocks_vector(v):
            q = nc.vector
            me, mo, de, do = bn[:, :, 1], bn[:, :, 4], bn[:, :, 2], bn[:, :, 5]

            v.wait_ge(s_bn, B)
            q.tensor_tensor(rt[:, :], me, me, ALU.mult)
            q.tensor_tensor(ry[:, :], mo, mo, ALU.mult)
            q.tensor_tensor(ms[:, :], de, do, ALU.add).then_inc(b_rstd, 1)
            v.wait_ge(b_rstd, 1)
            q.tensor_tensor(rt[:, :], rt[:, :], ry[:, :], ALU.add)
            q.tensor_scalar(ms[:, :], ms[:, :], 1.0 / D, EPS0, ALU.mult, ALU.add).then_inc(b_rstd, 1)
            v.wait_ge(b_rstd, 2)
            q.scalar_tensor_tensor(ms[:, :], rt[:, :], 0.5, ms[:, :], ALU.mult, ALU.add).then_inc(b_rstd, 1)
            v.wait_ge(b_rstd, 3)
            assert rsqrt(v, b_rstd, 3, rstd1[:, :], ms[:, :], rt[:, :]) == RSTEPS

            def std(mean, rstd, sm):
                q.tensor_tensor(mean[:, :], me, mo, ALU.add)
                q.tensor_tensor(rt[:, :], me, mo, ALU.subtract)
                q.tensor_tensor(ms[:, :], de, do, ALU.add).then_inc(sm, 1)
                v.wait_ge(sm, 1)
                q.tensor_scalar(mean[:, :], mean[:, :], 0.5, None, ALU.mult)
                q.tensor_scalar(ms[:, :], ms[:, :], 1.0 / D, EPS1, ALU.mult, ALU.add)
                q.scalar_tensor_tensor(rt[:, :], rt[:, :], 0.25, rt[:, :], ALU.mult, ALU.mult).then_inc(sm, 1)
                v.wait_ge(sm, 2)
                q.tensor_tensor(ms[:, :], ms[:, :], rt[:, :], ALU.add).then_inc(sm, 1)
                v.wait_ge(sm, 3)
                assert rsqrt(v, sm, 3, rstd[:, :], ms[:, :], rt[:, :]) == LSTEPS

            def moments(u, src, sm):
                for j in range(UNIT):
                    last = q.bn_stats(bn[:, bass.ds(u * UNIT + j, 1), :].rearrange("p a s -> p (a s)"), src(j))
                last.then_inc(sm, 1)

            def b_step(t, p):
                def gate(c):
                    u = t + 1
                    if is_unit(u):
                        v.wait_ge(b_th, FC * u + c + 1)
                        q.scalar_tensor_tensor(yg[c][:, :], th[c][:, :], 1.0, bank[1 + c][:, 0:UNIT * T], ALU.add,
                                               ALU.mult).then_inc(b_y, 1)

                def gated(c):
                    u = t + 1
                    if is_unit(u):
                        v.wait_ge(b_y, FC * u + c + 1)
                        wait(v, b_fm, u)
                        q.tensor_tensor(ff[c][:, :], bank[1 + c][:, UNIT * T:], yg[c][:, :], ALU.mult).then_inc(b_ff, 1)
                if is_unit(t):
                    v.wait_ge(b_fm, t + 1)
                    wait(v, b_fgT, t)
                    q.tensor_tensor(fg[:, :, :], bank[4][:, 0:UNIT * T].rearrange("p (u t) -> p u t", t=T),
                                    mods[:, pair(t), G2:G2 + 1].to_broadcast([128, UNIT, T]), ALU.mult).then_inc(b_fg, 1)
                gate(0)
                gated(0)
                gate(1)
                gated(1)
                gate(2)
                if is_unit(t):
                    v.wait_ge(b_fgT, t + 1)
                    q.tensor_tensor(x2[:, pair(t), :], bank[5][:, 0:UNIT * D].rearrange("p (u f) -> p u f", f=D),
                                    x1[:, pair(t), :], ALU.add).then_inc(b_x2, 1)
                    v.wait_ge(b_x2, t + 1)
                gated(2)
                if is_unit(t):
                    moments(t, lambda j: x2[:, bass.ds(t * UNIT + j, 1), :].rearrange("p a f -> p (a f)"), b_bn)
            units(v, b_step, 2)
            v.wait_ge(b_bn, U)
            std(mean2, rstd2, c_rstd)

            def y_moments(u):
                moments(u, lambda j: y[:, bass.ds(u * UNIT + j, 1), :].rearrange("p a f -> p (a f)"), c_bn)

            def c_step(t, p):
                p1 = 1 - p
                if is_unit(t - 1):
                    v.wait_ge(c_y, t)
                if is_unit(t):
                    v.wait_ge(c_ctx, t + 1)
                    v.wait_ge(c_krec, t + 1)
                    wait(v, c_yp, t - 1)
                    for j in range(UNIT):
                        last = q.scalar_tensor_tensor(cx[p][:, j, :], bank[5][:, j * D:(j + 1) * D], krec[p][:, j:j + 1],
                                                      blocks[:, :], ALU.mult, ALU.mult)
                    last.then_inc(c_cx, 1)
                if is_unit(t - 1):
                    y_moments(t - 1)
                if is_unit(t + 2):
                    u = t + 2
                    v.wait_ge(c_qv, u + 1)
                    wait(v, c_ctx, u - 1)
                    wait(v, c_qs, u - 1)
                    q.tensor_tensor(qvb[p][:, :, :], bank[2 + p][:, :].rearrange("p (u f) -> p u f", f=2 * D),
                                    bias_qv[:, :].unsqueeze(1).to_broadcast([128, UNIT, 2 * D]), ALU.add).then_inc(c_qvb, 1)
                if is_unit(t + 1):
                    v.wait_ge(c_qe, t + 2)
                    q.tensor_reduce(qsum[:, :, :], qe[p1][:, :, :, :], X_AXIS, ALU.add).then_inc(c_qsum, 1)
                if is_unit(t + 2):
                    u = t + 2
                    v.wait_ge(c_qvb, u + 1)
                    q.tensor_reduce(qmax[p][:, :, :], qvb[p][:, :, 0:D].rearrange("p u (h d) -> p u h d", d=DH),
                                    X_AXIS, ALU.max).then_inc(c_qmax, 1)
                    v.wait_ge(c_k, u + 1)
                    q.tensor_reduce(kmax[:, :], bank[1][:, 0:UNIT * T].rearrange("p (u t) -> p u t", t=T),
                                    X_AXIS, ALU.max, negate=True).then_inc(c_km, 1)
                if is_unit(t + 1):
                    u = t + 1
                    v.wait_ge(c_qsum, u + 1)
                    wait(v, c_qx, u - 1)
                    q.reciprocal(qrec[p1][:, :, :].rearrange("p u h -> p (u h)"),
                                 qsum[:, :, :].rearrange("p u h -> p (u h)")).then_inc(c_qrec, 1)
                    v.wait_ge(c_kx, u + 1)
                    q.reciprocal(krec[p1][:, :], ksum[p1][:, :]).then_inc(c_krec, 1)
                if is_unit(t + 2):
                    u = t + 2
                    v.wait_ge(c_km, u + 1)
                    wait(v, c_kx, u - 1)
                    q.tensor_scalar(knb[p][:, :], kmax[:, :], bias_k[:, 0:1], bias_k[:, 0:1], ALU.subtract, ALU.add).then_inc(c_nb, 1)
            units(v, c_step, 3)
            v.wait_ge(c_y, U)
            y_moments(U - 1)
            v.wait_ge(c_bn, U)
            std(mean3, rstd3, d_rstd)

            def d_step(t, p):
                p1 = 1 - p
                if is_unit(t + 1):
                    u = t + 1
                    v.wait_ge(d_th, u + 1)
                    wait(v, d_op, u - 1)
                    q.scalar_tensor_tensor(hs[p1][:, :], th[p1][:, :], 1.0, flat(hT2[p1]), ALU.add, ALU.mult).then_inc(d_hs, 1)
                if is_unit(t):
                    v.wait_ge(d_hgT, t + 1)
                    q.tensor_tensor(res[:, pair(t), :], bank[2][:, 0:UNIT * D].rearrange("p (u f) -> p u f", f=D),
                                    x2[:, pair(t), :], ALU.add).then_inc(s_res, 1)
            units(v, d_step, 2)

        def blocks_tensor(e):
            q = nc.tensor

            def turned(dst, src, sm):
                for j in range(UNIT):
                    last = q.transpose(dst[:, j * 128:(j + 1) * 128], src(j), ident[:, :])
                last.then_inc(sm, 1)

            def b_step(t, p):
                def hidden(c):
                    u = t + 1
                    if is_unit(u):
                        if c == 0:
                            e.wait_ge(b_hT, u + 1)
                        wait(e, b_ff, FC * (u - 1) + c + 1)
                        q.matmul(bank[1 + c][:, 0:UNIT * T], w1T[:, c * 128:c * 128 + 128], flat(hT2[1 - p]), start=True, stop=True)
                        q.matmul(bank[1 + c][:, UNIT * T:], w3T[:, c * 128:c * 128 + 128], flat(hT2[1 - p]), start=True,
                                 stop=True).then_inc(b_gu, 1)

                def back(c):
                    if is_unit(t):
                        e.wait_ge(b_ff, FC * t + c + 1)
                        if c == 0:
                            wait(e, b_fg, t)
                        last = q.matmul(bank[4][:, 0:UNIT * T], w2T[:, c, :], ff[c][:, :], start=c == 0, stop=c == FC - 1)
                        if c == FC - 1:
                            last.then_inc(b_fm, 1)
                back(0)
                hidden(0)
                if is_unit(t + 2):
                    e.wait_ge(b_xs, t + 3)
                    wait(e, b_hT, t + 2)
                    turned(bank[0], lambda j: xs2[p][:, j, :], b_xsT)
                back(1)
                back(2)
                hidden(1)
                hidden(2)
                if is_unit(t):
                    e.wait_ge(b_fg, t + 1)
                    wait(e, b_x2, t)
                    turned(bank[5], lambda j: fg[:, j, :], b_fgT)
            e.wait_ge(s_x1, B)
            units(e, b_step, 2)

            def c_step(t, p):
                p1 = 1 - p
                if is_unit(t):
                    e.wait_ge(c_kxT, t + 1)
                    e.wait_ge(c_qvb, t + 1)
                    wait(e, c_cx, t)
                    for j in range(UNIT):
                        last = q.matmul(bank[5][:, j * D:(j + 1) * D], kxT[p][:, j, :], qvb[p][:, j, D:2 * D], start=True, stop=True)
                    last.then_inc(c_ctx, 1)
                if is_unit(t + 2):
                    u = t + 2
                    e.wait_ge(c_hT, u + 1)
                    wait(e, c_qvb, u - 1)
                    for j in range(UNIT):
                        last = q.matmul(bank[2 + p][:, j * 2 * D:(j + 1) * 2 * D], hT2[p][:, j, :],
                                        lin[:, 0:2, :].rearrange("p c f -> p (c f)"), start=True, stop=True)
                    last.then_inc(c_qv, 1)
                if is_unit(t + 3):
                    u = t + 3
                    e.wait_ge(c_xs, u + 1)
                    wait(e, c_hT, u)
                    turned(bank[0], lambda j: xs2[p1][:, j, :], c_xsT)
                if is_unit(t):
                    e.wait_ge(c_qx, t + 1)
                    wait(e, c_qxT, t)
                    turned(bank[6], lambda j: qx[p][:, j, :, :].rearrange("p h d -> p (h d)"), c_qxTp)
                if is_unit(t + 1):
                    u = t + 1
                    e.wait_ge(c_kx, u + 1)
                    wait(e, c_kxT, u)
                    turned(bank[4], lambda j: kx[p1][:, j, :], c_kxTp)
                if is_unit(t + 2):
                    u = t + 2
                    wait(e, c_kx, u)
                    q.matmul(bank[1][:, 0:UNIT * T], lin[:, 2, :], flat(hT2[p]), start=True, stop=True).then_inc(c_k, 1)
                if is_unit(t):
                    e.wait_ge(c_qxT, t + 1)
                    e.wait_ge(c_cx, t + 1)
                    wait(e, c_y, t)
                    for j in range(UNIT):
                        last = q.matmul(bank[7][:, j * D:(j + 1) * D], qxT[p][:, j, :], cx[p][:, j, :], start=True, stop=True)
                    last.then_inc(c_yp, 1)
            e.wait_ge(b_x2, U)
            units(e, c_step, 3)

            def d_step(t, p):
                p1 = 1 - p
                if is_unit(t + 2):
                    e.wait_ge(d_xs, t + 3)
                    wait(e, d_hT, t + 2)
                    turned(bank[0], lambda j: xs2[p][:, j, :], d_xsT)
                if is_unit(t + 1):
                    u = t + 1
                    e.wait_ge(d_hs, u + 1)
                    wait(e, d_hg, u)
                    q.matmul(bank[1][:, 0:UNIT * T], outw[:, :], hs[p1][:, :], start=True, stop=True).then_inc(d_op, 1)
                if is_unit(t):
                    e.wait_ge(d_hg, t + 1)
                    wait(e, s_res, t)
                    turned(bank[2], lambda j: hg[p][:, j, :], d_hgT)
            e.wait_ge(c_y, U)
            e.wait_ge(c_bn, U)
            units(e, d_step, 2)

        @block.sync
        def _(sp):
            sp.dma_start(cond_n[:, :], cond).then_inc(ld_small, 16)
            for row, v, n in ((R_ADA, ada_b, 6), (R_N1, norm1_w, 1), (R_PB, proj_b, 1), (R_N2, norm2_w, 1),
                              (R_NG, norm_g, 1), (R_NB, norm_b, 1), (R_BK, bk, 1), (R_EB, emb_b, 2),
                              (R_SG, sn_g, 1), (R_SB, sn_b, 1), (R_OB, out_b, 1)):
                sp.dma_start(params_n[row:row + n, :], v.rearrange("(a n) -> a n", a=n)).then_inc(ld_small, 16)
            sp.dma_start(qkv_n[:, :, :], qkv_w.rearrange("(c p) f -> p c f", p=128)).then_inc(ld_qkv, 16)
            wait(sp, padded, 3)
            for w, wn in ((w1, w1_n), (w3, w3_n)):
                sp.dma_start(wn[:, 0:FC - 1, :], w[0:(FC - 1) * 128, :].rearrange("(c p) f -> p c f", p=128)).then_inc(ld_rest, 16)
                sp.dma_start(wn[0:LAST, FC - 1, :], w[(FC - 1) * 128:FFN, :]).then_inc(ld_rest, 16)
            sp.dma_start(w2_n[:, 0:FFN], w2).then_inc(ld_rest, 16)
            sp.dma_start(emb_n[:, :], emb_W).then_inc(ld_rest, 16)
            for i, w in enumerate((Wq, Wv, Wk)):
                sp.dma_start(lin_n[:, i, :], w).then_inc(ld_rest, 16)
            sp.dma_start(outw_n[:, :], out_W).then_inc(ld_rest, 16)
            sp.dma_start(bqv[:, 0:D], bq.rearrange("(a n) -> a n", a=1)).then_inc(ld_rest, 16)
            sp.dma_start(bqv[:, D:2 * D], bv.rearrange("(a n) -> a n", a=1)).then_inc(ld_rest, 16)
            with sp.Fori(0, NG) as g:
                sp.wait_ge(s_res, (g + 1) * (GRP // UNIT))
                sp.dma_start(out[bass.ds(g * GRP, GRP), :, :].rearrange("b t f -> t b f"),
                             res[:, bass.ds(g * GRP, GRP), :]).then_inc(stored, 16)
            sp.wait_ge(stored, 16 * NG)


        @block.gpsimd
        def _(g):
            q = nc.gpsimd
            q.memset(w1_n[:, FC - 1, :], 0.0).then_inc(padded, 1)
            q.memset(w3_n[:, FC - 1, :], 0.0).then_inc(padded, 1)
            q.memset(w2_n[:, FFN:], 0.0).then_inc(padded, 1)
            q.memset(ident[:, :], 0.0).then_inc(consts, 1)
            q.memset(identb[:, :], 0.0).then_inc(consts, 1)
            q.memset(sel[:, :, :], 0.0).then_inc(consts, 1)
            q.memset(blocks[:, :], 1.0).then_inc(consts, 1)
            q.memset(ones[:, :], 1.0)
            q.memset(three_halves[:, :], 1.5).then_inc(consts, 1)
            g.wait_ge(consts, 5)
            for m in (ident, identb):
                q.affine_select(out=m[:, :], in_=m[:, :], compare_op=ALU.not_equal, fill=1.0, base=0,
                                pattern=[[-1, 128]], channel_multiplier=1).then_inc(consts, 1)
            for k in (0, 1):
                q.affine_select(out=sel[:, :, :], in_=sel[:, :, :], compare_op=ALU.not_equal, fill=1.0,
                                base=-H * k, pattern=[[-1, H], [0, 128]], channel_multiplier=1).then_inc(consts, 1)
                g.wait_ge(consts, 8 + k)
            bl = blocks[:, :].rearrange("p (a b) -> p a b", b=DH)
            q.affine_select(out=bl, in_=bl, compare_op=ALU.is_ge, fill=0.0, base=0,
                            pattern=[[-DH, H], [0, DH]], channel_multiplier=1).then_inc(consts, 1)
            g.wait_ge(consts, 10)
            q.affine_select(out=bl, in_=bl, compare_op=ALU.is_ge, fill=0.0, base=DH - 1,
                            pattern=[[DH, H], [0, DH]], channel_multiplier=-1).then_inc(consts, 1)
            g.wait_ge(pv_a, N_SIN)
            g.wait_ge(ld_pos, 48)
            q.tensor_scalar(nsin[:, :, :], sincos[:, 0, :, :], -1.0, 1.0, ALU.mult, ALU.mult).then_inc(pv_g, 1)
            g.wait_ge(pv_g, 1)
            for s in range(2):
                for e in range(2):
                    own, other = s * DH, 2 * DH + s * DH
                    w_e = qkw[:, s:s + 1, e:ROPE:2].to_broadcast([128, B, AXES])
                    w_o = qkw[:, s:s + 1, 1 - e:ROPE:2].to_broadcast([128, B, AXES])
                    q.tensor_tensor(rope[:, :, own + e:own + ROPE:2], sincos[:, 1, :, :], w_e, ALU.mult).then_inc(pv_g, 1)
                    sn = sincos[:, 0, :, :] if e else nsin[:, :, :]
                    q.tensor_tensor(rope[:, :, other + e:other + ROPE:2], sn, w_o, ALU.mult).then_inc(pv_g, 1)
                q.tensor_copy(rope[:, :, own + ROPE:own + DH],
                              qkw[:, s:s + 1, ROPE:DH].to_broadcast([128, B, DH - ROPE])).then_inc(pv_g, 1)
                q.memset(rope[:, :, other + ROPE:other + DH], 0.0).then_inc(pv_g, 1)

            def step(t, p):
                b = t + 4
                if not is_seq(b):
                    return
                wait(g, s_parts, PARTS * (b - 2) + PARTS)
                g.wait_ge(s_qk, b + 1)
                f4 = rope[:, bass.ds(b, 1), :].rearrange("p a (u s d) -> p (a u) s d", u=2, s=2)
                qk4 = qk[p][:, :, :].rearrange("p (s h) d -> p s h d", s=2)
                rot4 = rot[p][:, :, :].rearrange("p (s h) d -> p s h d", s=2)
                pa4 = partner[:, :, :].rearrange("p (s h) d -> p s h d", s=2)
                q.tensor_tensor(rot4, qk4, f4[:, 0, :, :].unsqueeze(2).to_broadcast([128, 2, H, DH]), ALU.mult)
                for e in range(2):
                    last = q.tensor_tensor(pa4[:, :, :, e::2], qk4[:, :, :, 1 - e:ROPE:2],
                                           f4[:, 1, :, e:ROPE:2].unsqueeze(2).to_broadcast([128, 2, H, AXES]), ALU.mult)
                last.then_inc(s_rot, 1)
                g.wait_ge(s_rot, ROT * b + 1)
                q.tensor_tensor(rot[p][:, :, 0:ROPE], rot[p][:, :, 0:ROPE], partner[:, :, :], ALU.add).then_inc(s_rot, 1)
                g.wait_ge(s_ss, SEED * b + SEED)
                y_, s_, t_ = qv_y[p][:, :], qv_s[p][:, :], qv_t[:, :]
                for k in range(3):
                    q.tensor_tensor(t_, y_, y_, ALU.mult).then_inc(s_newton, 1)
                    g.wait_ge(s_newton, NEWT * b + 4 * k + 1)
                    q.tensor_tensor(t_, t_, s_, ALU.mult).then_inc(s_newton, 1)
                    g.wait_ge(s_newton, NEWT * b + 4 * k + 2)
                    q.tensor_tensor(t_, three_halves[:, :], t_, ALU.subtract).then_inc(s_newton, 1)
                    g.wait_ge(s_newton, NEWT * b + 4 * k + 3)
                    q.tensor_tensor(y_, y_, t_, ALU.mult).then_inc(s_newton, 1)
                    g.wait_ge(s_newton, NEWT * b + 4 * k + 4)
                g.wait_ge(s_rot, ROT * b + 2)
                q.tensor_tensor(rot[p][:, :, :], rot[p][:, :, :],
                                qv_y[p][:, :].unsqueeze(2).to_broadcast([128, 2 * H, DH]), ALU.mult).then_inc(s_rot, 1)

            g.wait_ge(pv_g, 13)
            steps(g, step)
            blocks_gpsimd(g)


        @block.scalar
        def _(a):
            q = nc.scalar
            for i in range(4):
                a.dma_start(xin[:, 4 * i:4 * i + 4, :], x[4 * i:4 * i + 4, :, :].rearrange("b t f -> t b f")).then_inc(ld_x, 16)
            a.dma_start(ada_n[:, :, :], ada_w.rearrange("(c p) f -> p c f", p=128)).then_inc(ld_ada, 16)
            a.dma_start(posn[:, :].rearrange("p (b c) -> p b c", c=AXES), pos.rearrange("b t c -> t b c")).then_inc(ld_pos, 16)
            for s, w in enumerate((q_norm_w, k_norm_w)):
                a.dma_start(qkw[:, s, :], w.partition_broadcast(128)).then_inc(ld_pos, 16)
            a.dma_start(proj_n[:, :], proj_w).then_inc(ld_ada, 16)
            a.wait_ge(pv_v, V_ANG)
            q.activation(sincos[:, :, :, :].rearrange("p s b c -> p (s b c)"),
                         ang[:, :, :].rearrange("p s n -> p (s n)"), ACT.Sin).then_inc(pv_a, 1)
            a.wait_ge(ld_x, 64)
            q.activation(big[:, :, :], xin[:, :, :], ACT.Square).then_inc(pv_a, 1)
            a.wait_ge(pt, P_ADA)
            q.activation(adaT[:, 0:512], bank[1][:, :], ACT.Copy).then_inc(pv_a, 1)
            q.activation(adaT[:, 512:768], bank[2][:, 0:256], ACT.Copy).then_inc(pv_a, 1)
            q.activation(projT[:, :], bank[2][:, 256:384], ACT.Copy).then_inc(pv_a, 1)
            a.wait_ge(pv_v, V_COND)
            q.activation(ctanh[:, :], condT[:, :], ACT.Tanh, scale=0.5).then_inc(pv_a, 1)
            a.wait_ge(pt, P_W1)
            q.activation(w1T[:, :], bank[5][:, 0:FC * 128], ACT.Copy).then_inc(pv_a, 1)
            a.wait_ge(pt, P_W3)
            q.activation(w3T[:, :], bank[6][:, 0:FC * 128], ACT.Copy).then_inc(pv_a, 1)
            a.wait_ge(pt, P_W2)
            q.activation(w2T[:, :, :].rearrange("p c f -> p (c f)"), bank[7][:, 0:FC * 128], ACT.Copy, scale=0.5).then_inc(pv_a, 1)
            q.activation(outw[:, :], outw_n[:, :], ACT.Copy, scale=0.5).then_inc(pv_a, 1)
            a.wait_ge(seeded, 5)
            a.wait_ge(pv_v, N_DONE)

            def step(t, p):
                q1, q0 = (p + 1) % 2, p

                def exp(c):
                    if is_seq(t):
                        a.wait_ge(s_e, NC * t + c + 1)
                        wait(a, s_o, NC * (t - 1) + c + 1)
                        q.activation(probs[c][:, :, :].rearrange("p h t -> p (h t)"), bank[E_BANK[c % 2]][:, :],
                                     ACT.Exp, scale=SCALE).then_inc(s_p, 1)

                def stacked(k):
                    if not is_seq(t + 1):
                        return
                    b = t + 1
                    sb_ = bank[STACK_BANK][:, :].bitcast(BF16).rearrange("p (s j t) -> p s j t", s=2, t=T)
                    js = slice(PAIRS // 2, PAIRS)
                    if k == 0:
                        a.wait_ge(s_st, 2 * b + 2)
                        wait(a, s_e, NC * (b - 2) + NC)
                        q.activation(qT[q1][:, js, :], sb_[:, 0, :, :], ACT.Copy)
                    elif k == 1:
                        q.activation(kT[q1][0:64, js, 0, :], sb_[0:64, 1, :, :], ACT.Copy)
                    else:
                        q.activation(kT[q1][64:128, js, 1, :], sb_[64:128, 1, :, :], ACT.Copy).then_inc(s_st1, 1)

                def high(s):
                    if not is_seq(t + 3):
                        return
                    b = t + 3
                    if s == 0:
                        a.wait_ge(s_rot, ROT * b + ROT)
                        wait(a, s_st, 2 * (b - 2) + 2)
                    slots = parts[q1][:, s, :, :].rearrange("p h (k d) -> p h k d", d=DH)[:, :, 2 * s:2 * s + 3, :]
                    last = q.activation(slots, rot[q1][:, s * H:(s + 1) * H, :].unsqueeze(2).to_broadcast([128, H, 3, DH]), ACT.Copy)
                    if s == 1:
                        last.then_inc(s_hi, 1)

                if is_seq(t + 4):
                    a.wait_ge(s_xsT, t + 5)
                    wait(a, s_qkv, t + 3)
                stacked(0)
                if is_seq(t + 4):
                    b = t + 4
                    q.activation(hT[q0][:, :], bank[W_BANK][:, 0:T], ACT.Identity,
                                 bias=mods[:, bass.ds(b, 1), S1:S1 + 1].rearrange("p a f -> p (a f)"),
                                 scale=mods[:, bass.ds(b, 1), A1:A1 + 1].rearrange("p a f -> p (a f)")).then_inc(s_hT, 1)
                if is_seq(t):
                    a.wait_ge(s_mTp, t + 1)
                    wait(a, s_e, NC * (t - 2) + NC)
                    q.activation(mT[q0][:, :], bank[E_BANK[0]][:, 0:T // 2].bitcast(BF16), ACT.Copy).then_inc(s_mT, 1)
                stacked(1)
                stacked(2)
                if is_seq(t + 4):
                    b = t + 4
                    a.wait_ge(s_qkv, b + 1)
                    wait(a, s_ss, SEED * (b - 2) + 1)
                    q.activation(qk2[q0][:, :, :].rearrange("p h d -> p (h d)"), bank[W_BANK][:, 0:2 * D], ACT.Square).then_inc(s_sq, 1)
                if is_seq(t - 1):
                    b = t - 1
                    a.wait_ge(s_oTp, b + 1)
                    wait(a, s_proj, b)
                    q.activation(oT[:, :], bank[P_BANK][:, 0:T], ACT.Copy).then_inc(s_oT, 1)
                exp(0)
                if is_seq(t + 4):
                    b = t + 4
                    wait(a, s_rot, ROT * (b - 2) + 1)
                    q.activation(qk[q0][:, :, :].rearrange("p h d -> p (h d)"), bank[W_BANK][:, 0:2 * D], ACT.Copy).then_inc(s_qk, 1)
                exp(1)
                if is_seq(t - 1):
                    a.wait_ge(s_proj, t)
                    wait(a, s_prT, t - 1)
                exp(2)
                if is_seq(t - 1):
                    b = t - 1
                    q.activation(pr[:, :], bank[P_BANK][:, 0:T], ACT.Identity,
                                 bias=mods[:, bass.ds(b, 1), GB1:GB1 + 1].rearrange("p a f -> p (a f)"),
                                 scale=mods[:, bass.ds(b, 1), G1:G1 + 1].rearrange("p a f -> p (a f)")).then_inc(s_pr, 1)
                if is_seq(t + 4):
                    b = t + 4
                    q.activation(vall[:, bass.ds(b, 1), :].rearrange("p a f -> p (a f)"), bank[W_BANK][:, 2 * D:3 * D],
                                 ACT.Copy).then_inc(s_vall, 1)
                exp(3)
                high(0)
                high(1)
                if is_seq(t):
                    b = t
                    a.wait_ge(s_o, NC * b + NC)
                    wait(a, s_oq, b)
                    q.activation(oT4[:, :], bank[O_BANK][:, :], ACT.Copy).then_inc(s_oT4, 1)

            steps(a, step)
            blocks_scalar(a)


        @block.vector
        def _(v):
            q = nc.vector
            n = 0

            def did(ins):
                nonlocal n
                n += 1
                ins.then_inc(pv_v, 1)
                v.wait_ge(pv_v, n)

            for p in range(2):
                q.memset(parts[p][:, :, :, :].rearrange("p s h d -> p (s h d)").bitcast(F32), 0.0)
                q.memset(kT[p][:, :, :, :].rearrange("p j s t -> p (j s t)").bitcast(F32), 0.0)
                q.memset(vpad[p][:, :, :], 0.0).then_inc(seeded, 1)
            q.memset(mparts[:, :].bitcast(F32), 0.0).then_inc(seeded, 1)
            v.wait_ge(seeded, 3)
            for p in range(2):
                q.memset(vpad[p][:, :, DH:DH + 1], 1.0).then_inc(seeded, 1)
            v.wait_ge(ld_pos, 48)
            r0, r1 = ang[:, 0, :], ang[:, 1, :]
            did(q.tensor_scalar(turns[:, :], posn[:, :], 1.0 / (2 * math.pi), ROUND, ALU.mult, ALU.add))
            did(q.tensor_scalar(turns[:, :], turns[:, :], -ROUND, None, ALU.add))
            did(q.scalar_tensor_tensor(r0, turns[:, :], -TWO_PI_A, posn[:, :], ALU.mult, ALU.add))
            did(q.scalar_tensor_tensor(r0, turns[:, :], -TWO_PI_B, r0, ALU.mult, ALU.add))
            did(q.scalar_tensor_tensor(r0, turns[:, :], -TWO_PI_C, r0, ALU.mult, ALU.add))
            did(q.scalar_tensor_tensor(r1, r0, -1.0, r0, ALU.mult, ALU.max))
            did(q.tensor_scalar(r1, r1, -1.0, math.pi / 2, ALU.mult, ALU.add))
            did(q.tensor_scalar(r0, r0, PI_BELOW, -PI_BELOW, ALU.min, ALU.max))
            assert n == V_ANG
            v.wait_ge(pt, P_COND)
            did(q.tensor_copy(par[:, :], bank[0][:, 0:NROW]))
            did(q.tensor_copy(condT[:, :], bank[0][:, 32:32 + B]))
            assert n == V_COND
            v.wait_ge(pv_a, 2)
            did(q.tensor_reduce(ms[:, :], big[:, :, :], X_AXIS, ALU.add))
            did(q.tensor_scalar(ms[:, :], ms[:, :], 1.0 / D, EPS0, ALU.mult, ALU.add))
            n = rsqrt(v, pv_v, n, rstd_x[:, :], ms[:, :], rt[:, :])
            v.wait_ge(pt, P_QKV)
            did(q.tensor_copy(qkvT[:, :], bank[3][:, 0:3 * D]))
            v.wait_ge(pt, P_MOD)
            did(q.tensor_tensor(modr[:, :, :], bank[4][:, 0:6 * B].rearrange("p (c b) -> p c b", b=B),
                                par[:, R_ADA:R_ADA + 6].unsqueeze(2).to_broadcast([128, 6, B]), ALU.add))
            did(q.tensor_scalar(mods[:, :, A1], modr[:, 1, :], 1.0, par[:, R_N1:R_N1 + 1], ALU.add, ALU.mult))
            did(q.tensor_copy(mods[:, :, S1], modr[:, 0, :]))
            did(q.tensor_copy(mods[:, :, G1], modr[:, 2, :]))
            did(q.tensor_scalar(mods[:, :, GB1], modr[:, 2, :], par[:, R_PB:R_PB + 1], None, ALU.mult))
            did(q.tensor_scalar(mods[:, :, A2], modr[:, 4, :], 1.0, par[:, R_N2:R_N2 + 1], ALU.add, ALU.mult))
            did(q.tensor_copy(mods[:, :, S2], modr[:, 3, :]))
            did(q.tensor_copy(mods[:, :, G2], modr[:, 5, :]))
            did(q.tensor_copy(mods[:, :, GATE], condT[:, :]))
            did(q.tensor_scalar(mods[:, :, GO], condT[:, :], par[:, R_OB:R_OB + 1], None, ALU.mult))
            v.wait_ge(pv_a, 6)
            did(q.scalar_tensor_tensor(csilu[:, :], ctanh[:, :], 1.0, condT[:, :], ALU.add, ALU.mult))
            did(q.tensor_scalar(csilu[:, :], csilu[:, :], 0.5, None, ALU.mult))
            assert n == N_CSILU
            did(q.tensor_scalar(nbb[:, :], par[:, R_NB:R_NB + 1].to_broadcast([128, 128]), 1.0, None, ALU.mult))
            assert n == N_NBB
            v.wait_ge(ld_rest, N_REST)
            did(q.tensor_scalar(lin[:, :, :], lin_n[:, :, :], par[:, R_NG:R_NG + 1], None, ALU.mult))
            v.wait_ge(pt, P_BIAS)
            did(q.tensor_copy(bias_qv[:, :], bank[3][:, 0:2 * D]))
            did(q.tensor_tensor(bias_k[:, :], bank[3][:, 2 * D:2 * D + 1], par[:, R_BK:R_BK + 1], ALU.add))
            v.wait_ge(pt, P_EMB)
            did(q.tensor_tensor(embr[:, :, :], bank[4][:, 0:2 * B].rearrange("p (c b) -> p c b", b=B),
                                par[:, R_EB:R_EB + 2].unsqueeze(2).to_broadcast([128, 2, B]), ALU.add))
            did(q.tensor_scalar(mods[:, :, A3], embr[:, 0, :], 1.0, par[:, R_SG:R_SG + 1], ALU.add, ALU.mult))
            did(q.tensor_scalar(mods[:, :, S3], embr[:, 0, :], 1.0, par[:, R_SB:R_SB + 1], ALU.add, ALU.mult))
            did(q.tensor_tensor(mods[:, :, S3], mods[:, :, S3], embr[:, 1, :], ALU.add))
            assert n == N_DONE
            v.wait_ge(pv_g, 13)

            def step(t, p):
                q0, q1 = p, (p + 1) % 2
                def rowmax(c):
                    if is_seq(t + 1):
                        b = t + 1
                        v.wait_ge(s_s, NC * b + c + 1)
                        if c == 0:
                            wait(v, s_mp, b - 1)
                        q.tensor_reduce(nmax[q1][:, c * HPC:(c + 1) * HPC],
                                        bank[S_BANK[c % 2]][:, :].rearrange("p (h t) -> p h t", t=T),
                                        X_AXIS, ALU.max, negate=True).then_inc(s_max, 1)
                def cut(k):
                    b = t + 2
                    if not is_seq(b):
                        return
                    both = parts[q0][:, :, :, :].rearrange("p s h (k d) -> p (s h) k d", d=DH)
                    pq = parts[q0][:, 0, :, :].rearrange("p h (k d) -> p h k d", d=DH)
                    pk = parts[q0][:, 1, :, :].rearrange("p h (k d) -> p h k d", d=DH)
                    if k == 0:
                        v.wait_ge(s_hi, b + 1)
                        q.tensor_tensor(rest[:, :, :], rot[q0][:, :, :], both[:, :, 2, :], ALU.subtract).then_inc(s_parts, 1)
                    if k == 1:
                        v.wait_ge(s_parts, PARTS * b + 1)
                        q.tensor_copy(both[:, :, 5, :], rest[:, :, :]).then_inc(s_parts, 1)
                    if k == 2:
                        v.wait_ge(s_parts, PARTS * b + 2)
                        q.tensor_tensor(pq[:, :, 4, :], rest[:, 0:H, :], pq[:, :, 5, :], ALU.subtract).then_inc(s_parts, 1)
                        q.tensor_tensor(pk[:, :, 1, :], rest[:, H:, :], pk[:, :, 5, :], ALU.subtract).then_inc(s_parts, 1)
                        q.tensor_copy(pq[:, :, 3, :], pq[:, :, 5, :]).then_inc(s_parts, 1)
                        q.tensor_copy(pk[:, :, 0, :], pk[:, :, 5, :]).then_inc(s_parts, 1)

                def seed(k):
                    b = t + 4
                    if not is_seq(b):
                        return
                    if k == 0:
                        v.wait_ge(s_sq, b + 1)
                        wait(v, s_newton, NEWT * (b - 2) + NEWT)
                        q.tensor_reduce(qv_ms[q0][:, :], qk2[q0][:, :, :], X_AXIS, ALU.add).then_inc(s_ss, 1)
                    else:
                        v.wait_ge(s_ss, SEED * b + k)
                    if k == 1:
                        q.tensor_scalar(qv_s[q0][:, :], qv_ms[q0][:, :], 0.5 / DH, 0.5 * EPS0, ALU.mult, ALU.add).then_inc(s_ss, 1)
                    if k == 2:
                        q.tensor_scalar(qv_ms[q0][:, :].bitcast(I32), qv_s[q0][:, :].bitcast(I32), 1, None,
                                        ALU.logical_shift_right).then_inc(s_ss, 1)
                    if k == 3:
                        wait(v, s_rot, ROT * (b - 2) + ROT)
                        q.tensor_scalar(qv_y[q0][:, :].bitcast(I32), qv_ms[q0][:, :].bitcast(I32), -1.0,
                                        float(MAGIC - 2 ** 22), ALU.mult, ALU.add).then_inc(s_ss, 1)

                rowmax(0)
                cut(0)
                cut(1)
                if is_seq(t - 1):
                    b = t - 1
                    v.wait_ge(s_oq, b + 1)
                    oq = bank[O_BANK][:, :].rearrange("p (h w) -> p h w", w=VW)
                    q.reciprocal(rsum[:, :], oq[:, :, DH:DH + 1].rearrange("p h a -> p (h a)")).then_inc(s_rec, 1)
                if is_seq(t + 5):
                    b = t + 5
                    wait(v, s_xsT, b - 1)
                    q.tensor_scalar(xs[q1][:, :], xin[:, bass.ds(b, 1), :].rearrange("p a f -> p (a f)"),
                                    rstd_x[:, bass.ds(b, 1)], None, ALU.mult).then_inc(s_xs, 1)
                if is_seq(t - 1):
                    b = t - 1
                    v.wait_ge(s_rec, b + 1)
                    wait(v, s_oTp, b)
                    q.tensor_tensor(o[:, :, :], bank[O_BANK][:, :].rearrange("p (h w) -> p h w", w=VW)[:, :, 0:DH],
                                    rsum[:, :].unsqueeze(2).to_broadcast([128, H, DH]), ALU.mult).then_inc(s_on, 1)
                cut(2)
                rowmax(1)
                seed(0)
                rowmax(2)
                if is_seq(t + 2):
                    b = t + 2
                    v.wait_ge(s_st, 2 * b + 1)
                    wait(v, s_e, NC * (b - 2) + NC // 2)
                    sb_ = bank[STACK_BANK][:, :].bitcast(BF16).rearrange("p (s j t) -> p s j t", s=2, t=T)
                    js = slice(0, PAIRS // 2)
                    q.tensor_copy(qT[q0][:, js, :], sb_[:, 0, :, :])
                    q.tensor_copy(kT[q0][0:64, js, 0, :], sb_[0:64, 1, :, :])
                    q.tensor_copy(kT[q0][64:128, js, 1, :], sb_[64:128, 1, :, :]).then_inc(s_st0, 1)
                if is_seq(t + 1):
                    b = t + 1
                    v.wait_ge(s_vall, b + 1)
                    wait(v, s_o, NC * (b - 2) + NC)
                    q.tensor_scalar(vpad[q1][:, :, 0:DH], vall[:, bass.ds(b, 1), :].rearrange("p a (h d) -> p (a h) d", d=DH),
                                    1.0, None, ALU.mult).then_inc(s_vpad, 1)
                if is_seq(t - 1):
                    b = t - 1
                    v.wait_ge(s_prT, b + 1)
                    q.tensor_tensor(x1[:, bass.ds(b, 1), :].rearrange("p a f -> p (a f)"), bank[P_BANK][:, 0:D],
                                    xin[:, bass.ds(b, 1), :].rearrange("p a f -> p (a f)"), ALU.add).then_inc(s_x1, 1)
                if is_seq(t - 1):
                    v.wait_ge(s_x1, t)
                seed(1)
                if is_seq(t - 1):
                    q.bn_stats(bn[:, bass.ds(t - 1, 1), :].rearrange("p a s -> p (a s)"),
                               x1[:, bass.ds(t - 1, 1), :].rearrange("p a f -> p (a f)")).then_inc(s_bn, 1)
                rowmax(3)
                seed(2)
                if is_seq(t + 1):
                    b = t + 1
                    v.wait_ge(s_max, NC * b + NC)
                    wait(v, s_mTp, b)
                    q.tensor_copy(mparts[:, 0:H], nmax[q1][:, :]).then_inc(s_mh, 1)
                    v.wait_ge(s_mh, b + 1)
                    q.tensor_tensor(mparts[:, H:2 * H], nmax[q1][:, :], mparts[:, 0:H], ALU.subtract).then_inc(s_mp, 1)
                seed(3)

            steps(v, step)
            blocks_vector(v)

        @block.tensor
        def _(e):
            q = nc.tensor
            e.wait_ge(consts, 11)
            e.wait_ge(ld_small, N_SMALL)
            q.transpose(bank[0][:, 0:NROW], params_n[:, :], ident[0:NROW, 0:NROW])
            q.transpose(bank[0][:, 32:32 + B], cond_n[:, :], ident[0:B, 0:B]).then_inc(pt, 1)
            e.wait_ge(ld_ada, 32)
            for c in range(6):
                q.transpose(bank[1 + c // 4][:, c % 4 * 128:c % 4 * 128 + 128], ada_n[:, c, :], ident[:, :])
            q.transpose(bank[2][:, 256:384], proj_n[:, :], ident[:, :]).then_inc(pt, 1)
            e.wait_ge(ld_qkv, 16)
            for c in range(3):
                last = q.transpose(bank[3][:, c * 128:c * 128 + 128], qkv_n[:, c, :], ident[:, :])
            last.then_inc(pt, 1)
            e.wait_ge(pv_v, V_COND)
            e.wait_ge(pv_a, 4)
            for c in range(6):
                last = q.matmul(bank[4][:, c * B:(c + 1) * B], adaT[:, c * 128:c * 128 + 128], condT[:, :], start=True, stop=True)
            last.then_inc(pt, 1)
            e.wait_ge(ld_rest, N_REST)
            for k, src in ((5, w1_n), (6, w3_n)):
                for c in range(FC):
                    last = q.transpose(bank[k][:, c * 128:c * 128 + 128], src[:, c, :], ident[:, :])
                last.then_inc(pt, 1)
            for c in range(FC):
                last = q.transpose(bank[7][:, c * 128:c * 128 + 128], w2_n[:, c * 128:c * 128 + 128], ident[:, :])
            last.then_inc(pt, 1)
            e.wait_ge(pv_v, N_NBB)
            q.matmul(bank[3][:, 0:2 * D], nbb[:, :], lin_n[:, 0:2, :].rearrange("p c f -> p (c f)"), start=True, stop=False)
            q.matmul(bank[3][:, 0:2 * D], ones[:, :], bqv[:, :], start=False, stop=True)
            q.matmul(bank[3][:, 2 * D:2 * D + 1], lin_n[:, 2, :], nbb[:, 0:1], start=True, stop=True).then_inc(pt, 1)
            for c in range(2):
                last = q.matmul(bank[4][:, c * B:(c + 1) * B], emb_n[:, c * 128:c * 128 + 128], csilu[:, :], start=True, stop=True)
            last.then_inc(pt, 1)
            e.wait_ge(pv_v, N_DONE)
            e.wait_ge(pv_a, 10)
            e.wait_ge(seeded, 5)

            def step(t, p):
                q0, q1 = p, (p + 1) % 2

                def weighted(c):
                    if not is_seq(t):
                        return
                    if c == 0:
                        e.wait_ge(s_mT, t + 1)
                    wait(e, s_p, NC * t + c - 1)
                    for i in range(HPC):
                        h = c * HPC + i
                        dst = bank[E_BANK[c % 2]][:, i * T:(i + 1) * T]
                        q.matmul(dst, kT[q0][:, h // 2, h % 2, :], qT[q0][:, h // 2, :], start=True, stop=False)
                        last = q.matmul(dst, sel[:, h, :], mT[q0][:, :], start=False, stop=True)
                    last.then_inc(s_e, 1)

                def scores(c):
                    if not is_seq(t + 1):
                        return
                    b = t + 1
                    if c == 0:
                        e.wait_ge(s_st0, b + 1)
                    if c == NC // 2:
                        e.wait_ge(s_st1, b + 1)
                    wait(e, s_max, NC * b + c - 1)
                    for i in range(HPC // 2):
                        j = c * (HPC // 2) + i
                        last = q.matmul(bank[S_BANK[c % 2]][:, i * 2 * T:(i + 1) * 2 * T], qT[q1][:, j, :],
                                        kT[q1][:, j, :, :].rearrange("p s t -> p (s t)"), start=True, stop=True)
                    last.then_inc(s_s, 1)

                def values(c):
                    if not is_seq(t):
                        return
                    if c == 0:
                        e.wait_ge(s_vpad, t + 1)
                        wait(e, s_on, t)
                    e.wait_ge(s_p, NC * t + c + 1)
                    for i in range(HPC):
                        last = q.matmul(bank[O_BANK][VW * i:VW * (i + 1), c * T:(c + 1) * T], vpad[q0][:, c * HPC + i, :],
                                        probs[c][:, i, :], start=True, stop=True)
                    last.then_inc(s_o, 1)

                def stack(half):
                    b = t + 2 - half
                    if not is_seq(b):
                        return
                    if half == 0:
                        e.wait_ge(s_parts, PARTS * b + PARTS)
                        wait(e, s_st1, b)
                    else:
                        e.wait_ge(s_st0, b + 1)
                    src = parts[q0 if half == 0 else q1]
                    for s in range(2):
                        for j in range(PAIRS // 2):
                            h = half * (H // 2) + 2 * j
                            at = (s * PAIRS // 2 + j) * T // 2
                            last = q.transpose(bank[STACK_BANK][:, at:at + T // 2].bitcast(BF16),
                                               src[:, s, h:h + 2, :].rearrange("p h k -> p (h k)"), identb[:, :])
                    last.then_inc(s_st, 1)

                scores(0)
                if is_seq(t + 4):
                    b = t + 4
                    e.wait_ge(s_xs, b + 1)
                    wait(e, s_vall, b)
                    q.transpose(bank[W_BANK][:, 0:T], xs[q0][:, :], ident[:, :]).then_inc(s_xsT, 1)
                stack(1)
                scores(1)
                if is_seq(t):
                    e.wait_ge(s_mp, t + 1)
                    wait(e, s_p, NC * t - 1)
                    q.transpose(bank[E_BANK[0]][:, 0:T // 2].bitcast(BF16), mparts[:, :], identb[:, :]).then_inc(s_mTp, 1)
                if is_seq(t - 1):
                    b = t - 1
                    e.wait_ge(s_oT4, b + 1)
                    for i in range(NC):
                        last = q.transpose(bank[O_BANK][:, i * T:(i + 1) * T], oT4[:, i * T:(i + 1) * T], ident[:, :])
                    last.then_inc(s_oq, 1)
                if is_seq(t + 4):
                    b = t + 4
                    e.wait_ge(s_hT, b + 1)
                    q.matmul(bank[W_BANK][:, 0:3 * D], hT[q0][:, :], qkvT[:, :], start=True, stop=True).then_inc(s_qkv, 1)
                weighted(0)
                if is_seq(t - 1):
                    b = t - 1
                    e.wait_ge(s_on, b + 1)
                    wait(e, s_x1, b)
                    q.transpose(bank[P_BANK][:, 0:T], o[:, :, :].rearrange("p h d -> p (h d)"), ident[:, :]).then_inc(s_oTp, 1)
                weighted(1)
                scores(2)
                stack(0)
                if is_seq(t - 1):
                    b = t - 1
                    e.wait_ge(s_oT, b + 1)
                    q.matmul(bank[P_BANK][:, 0:T], projT[:, :], oT[:, :], start=True, stop=True).then_inc(s_proj, 1)
                weighted(2)
                scores(3)
                weighted(3)
                if is_seq(t - 1):
                    b = t - 1
                    e.wait_ge(s_pr, b + 1)
                    q.transpose(bank[P_BANK][:, 0:D], pr[:, :], ident[:, :]).then_inc(s_prT, 1)
                values(0)
                values(1)
                values(2)
                values(3)

            steps(e, step)
            blocks_tensor(e)


_INS = ['x', 'cond_1024', 'fside_BxSx3_0', 'L0_cond_norm1_w', 'L0_cond_qkv_w', 'L0_cond_q_norm_w', 'L0_cond_k_norm_w',
        'L0_cond_proj_w', 'L0_cond_proj_b', 'L0_cond_norm2_w', 'L0_cond_w1', 'L0_cond_w3', 'L0_cond_w2', 'L0_cond_ada_w',
        'L0_cond_ada_b', 'L1_cond_norm_g', 'L1_cond_norm_b', 'L1_cond_Wq', 'L1_cond_bq', 'L1_cond_Wk', 'L1_cond_bk',
        'L1_cond_Wv', 'L1_cond_bv', 'L1_cond_emb_W', 'L1_cond_emb_b', 'L1_cond_sn_g', 'L1_cond_sn_b', 'L1_cond_out_W',
        'L1_cond_out_b']


def kernel(**inputs):
    import numpy as _np
    import concourse.bacc as _bacc
    from concourse import mybir as _mybir
    from concourse.bass_utils import run_bass_kernel_spmd as _run

    nc = _bacc.Bacc("TRN2", target_bir_lowering=False, num_devices=1)
    arrays, args = {}, []
    for name in _INS:
        a = _np.ascontiguousarray(inputs[name])
        arrays[f"in_{name}_dram"] = a
        args.append(nc.dram_tensor(f"in_{name}_dram", a.shape, _mybir.dt.from_np(a.dtype), kind="ExternalInput").ap())
    args.append(nc.dram_tensor("out_0_dram", (B, T, D), _mybir.dt.float32, kind="ExternalOutput").ap())
    dit_then_linear_attention(nc, *args)
    r = _run(nc, [arrays], core_ids=[0])
    return r.results[0]["out_0_dram"]
```

```python
import math

import numpy as np
import concourse.bass as bass
from concourse import mybir
from concourse.alu_op_type import AluOpType as ALU
from contextlib import ExitStack

F32 = mybir.dt.float32
BF16 = mybir.dt.bfloat16
I32 = mybir.dt.int32
ACT = mybir.ActivationFunctionType
X_AXIS = mybir.AxisListType.X

B, T, D = 16, 128, 128
H = 16
DH = D // H
ROPE = DH // 6 * 6
AXES = ROPE // 2
FFN = int(2 * (4 * D) / 3)
FC = -(-FFN // 128)
LAST = FFN - (FC - 1) * 128
UNIT = 2
U = B // UNIT
EARLY = B // 2
EARLY_U = EARLY // UNIT
NG = 4
GRP = B // NG
SLOT = 64
HPC = 4
NC = H // HPC
PAIRS = H // 2
VW = 32
EPS0, EPS1 = 1e-6, 1e-5
SCALE = DH ** -0.5
MAGIC = 0x5F3759DF
ROUND = 1.5 * 2.0 ** 23
TWO_PI_A = 6.28125
TWO_PI_B = float(np.float32(round((2 * math.pi - TWO_PI_A) * 2 ** 21) / 2 ** 21))
TWO_PI_C = 2 * math.pi - TWO_PI_A - TWO_PI_B
PI_BELOW = 3.1415925

A1, S1, G1, GB1, A2, S2, G2, A3, S3, GATE, GO, NMOD = range(12)
R_ADA, R_N1, R_PB, R_N2, R_NG, R_NB, R_BK, R_EB, R_SG, R_SB, R_OB, NROW = 0, 6, 7, 8, 9, 10, 11, 12, 14, 15, 16, 17
FIRST_ROWS = 7
HEAD_B = 4
TBL = 4 * DH

LEAD = 5
POOL_NORMS = HEAD_B - LEAD


def is_seq(b):
    return not isinstance(b, int) or 0 <= b < B


def wait(eng, sem, value):
    if not isinstance(value, int) or value > 0:
        eng.wait_ge(sem, value)


def pipeline(eng, body, first, last, end, start):
    last = first + (last - first) // 2 * 2
    for t in range(start, first):
        body(t, t % 2)
    with eng.Fori(first, last - 1, 2) as t:
        body(t, first % 2)
        body(t + 1, (first + 1) % 2)
    for t in range(last, end):
        body(t, t % 2)


def steps(eng, body, next_body=None):
    pipeline(eng, body, 3, B - LEAD, B - 2, -LEAD)
    for t in (B - 2, B - 1, B):
        if next_body is not None:
            next_body(t - B, (t - B) % 2)
        body(t, t % 2)


def at(t, k):
    return isinstance(t, int) and t == k


def before(t, k):
    return isinstance(t, int) and t < k


def is_unit(u):
    return not isinstance(u, int) or 0 <= u < U


def units(eng, body, lead, start=None):
    pipeline(eng, body, 2, U - lead, U, -lead if start is None else start)


def dit_then_linear_attention(nc, x, cond, pos, norm1_w, qkv_w, q_norm_w, k_norm_w, proj_w, proj_b,
                              norm2_w, w1, w3, w2, ada_w, ada_b, norm_g, norm_b, Wq, bq, Wk, bk, Wv,
                              bv, emb_W, emb_b, sn_g, sn_b, out_W, out_b, out):
    ctx = ExitStack()
    with ctx:
        def sb(name, shape, dt=F32):
            return ctx.enter_context(nc.sbuf_tensor(name, shape, dt))

        def sem(name):
            return ctx.enter_context(nc.semaphore(name))

        ident = sb("ident", [128, 128])
        identb = sb("identb", [128, 128], BF16)
        ones = sb("ones", [1, 128])
        blocks = sb("blocks", [128, 128])
        sel = sb("sel", [128, H, 128], BF16)
        xin = sb("xin", [128, B, D])
        cond_n = sb("cond_n", [B, D])
        params_a = sb("params_a", [FIRST_ROWS, D])
        params_b = sb("params_b", [NROW - FIRST_ROWS, D])
        bqv = sb("bqv", [1, 2 * D])
        posn = sb("posn", [128, B * AXES])
        qkw = sb("qkw", [128, 2, DH])
        qkv_n = sb("qkv_n", [128, 3, D])
        proj_n = sb("proj_n", [128, D])
        w1_n = sb("w1_n", [128, FC, D])
        w3_n = sb("w3_n", [128, FC, D])
        w2_n = sb("w2_n", [128, FC * 128])
        ada_n = sb("ada_n", [128, 6, D])
        emb_n = sb("emb_n", [128, 2 * D])
        lin_n = sb("lin_n", [128, 3, D])
        outw_n = sb("outw_n", [128, D])
        adaT = sb("adaT", [128, 6 * D])
        qkvT = sb("qkvT", [128, 3 * D])
        projT = sb("projT", [128, D])
        w1T = sb("w1T", [128, FC * 128])
        w3T = sb("w3T", [128, FC * 128])
        w2T = sb("w2T", [128, FC, D])
        lin = sb("lin", [128, 3, D])
        outw = sb("outw", [128, D])
        nbb = sb("nbb", [128, 128])
        bias_qv = sb("bias_qv", [128, 2 * D])
        bias_k = sb("bias_k", [128, 1])
        par = sb("par", [128, NROW])
        condT = sb("condT", [128, B])
        csilu = sb("csilu", [128, B])
        ctanh = sb("ctanh", [128, B])
        modr = sb("modr", [128, 6, B])
        embr = sb("embr", [128, 2, B])
        mods = sb("mods", [128, B, NMOD])
        ang = sb("ang", [128, 2, B * AXES])
        sincos = sb("sincos", [128, 2, B, AXES])
        nsin = sb("nsin", [128, B, AXES])
        turns = sb("turns", [128, B * AXES])
        rope = sb("rope", [128, B, TBL])
        big = sb("big", [128, B, D])
        ms = sb("ms", [128, B])
        ry = sb("ry", [128, B])
        rt = sb("rt", [128, B])
        rstd_x = sb("rstd_x", [128, B])
        xs = [sb(f"xs{p}", [128, D]) for p in range(2)]
        hT = [sb(f"hT{p}", [128, T]) for p in range(2)]
        qk = [sb(f"qk{p}", [128, 2 * H, DH]) for p in range(2)]
        qk2 = [sb(f"qk2{p}", [128, 2 * H, DH]) for p in range(2)]
        qv_ms = [sb(f"qv_ms{p}", [128, 2 * H]) for p in range(2)]
        qv_s = [sb(f"qv_s{p}", [128, 2 * H]) for p in range(2)]
        qv_y = [sb(f"qv_y{p}", [128, 2 * H]) for p in range(2)]
        qv_t = sb("qv_t", [128, 2 * H])
        three_halves = sb("three_halves", [128, 2 * H])
        partner = sb("partner", [128, 2 * H, ROPE])
        rot = [sb(f"rot{p}", [128, 2 * H, DH]) for p in range(2)]
        rest = sb("rest", [128, 2 * H, DH])
        parts = [sb(f"parts{p}", [128, 2, H, SLOT], BF16) for p in range(2)]
        qT = [sb(f"qT{p}", [128, PAIRS, T], BF16) for p in range(2)]
        kT = [sb(f"kT{p}", [128, PAIRS, 2, T], BF16) for p in range(2)]
        nmax = [sb(f"nmax{p}", [128, H]) for p in range(2)]
        mparts = sb("mparts", [128, 128], BF16)
        mT = [sb(f"mT{p}", [128, T], BF16) for p in range(2)]
        probs = [sb(f"probs{c}", [128, HPC, T]) for c in range(NC)]
        vall = sb("vall", [128, B, D])
        vpad = [sb(f"vpad{p}", [128, H, VW]) for p in range(2)]
        oT4 = sb("oT4", [128, NC * T])
        rsum = sb("rsum", [128, H])
        o = sb("o", [128, H, DH])
        oT = sb("oT", [128, T])
        pr = sb("pr", [128, T])
        x1 = sb("x1", [128, B, D])
        def two(name, *shape):
            return [sb(f"{name}{p}", [128, *shape]) for p in range(2)]
        rstd1 = sb("rstd1", [128, B])
        xs2 = two("xs2", UNIT, D)
        hT2 = two("hT2", UNIT, T)
        th = [sb(f"th{c}", [128, UNIT * T]) for c in range(FC)]
        yg = [sb(f"yg{c}", [128, UNIT * T]) for c in range(FC)]
        ff = [sb(f"ff{c}", [128, UNIT * T]) for c in range(FC)]
        fg = sb("fg", [128, UNIT, T])
        x2 = sb("x2", [128, B, D])
        bn = sb("bn", [128, B, 6])
        mean2 = sb("mean2", [128, B])
        rstd2 = sb("rstd2", [128, B])
        kmax = sb("kmax", [128, UNIT])
        knb = two("knb", UNIT)
        kx = two("kx", UNIT, T)
        ksum = two("ksum", UNIT)
        krec = two("krec", UNIT)
        kxT = two("kxT", UNIT, D)
        qvb = two("qvb", UNIT, 2 * D)
        qmax = two("qmax", UNIT, H)
        qs = two("qs", UNIT, H, DH)
        qe = two("qe", UNIT, H, DH)
        qsum = sb("qsum", [128, UNIT, H])
        qrec = two("qrec", UNIT, H)
        qx = two("qx", UNIT, H, DH)
        qxT = two("qxT", UNIT, T)
        cx = two("cx", UNIT, D)
        y = sb("y", [128, B, D])
        mean3 = sb("mean3", [128, B])
        rstd3 = sb("rstd3", [128, B])
        hs = two("hs", UNIT * T)
        hg = two("hg", UNIT, T)
        res = sb("res", [128, B, D])

        bank = [ctx.enter_context(nc.psum_tensor(f"bank{i}", [128, 512], F32)) for i in range(8)]
        S_BANK, E_BANK, STACK_BANK, P_BANK, O_BANK, W_BANK = (0, 1), (2, 3), 4, 5, 6, 7
        GU_BANK, F_BANK, FT_BANK, X_BANK = (0, 1, 4), 2, 3, 7

        ld_head = sem("ld_head")
        ld_x = sem("ld_x")
        ld_first = sem("ld_first")
        ld_small = sem("ld_small")
        ld_ada = sem("ld_ada")
        ld_proj = sem("ld_proj")
        ld_qkv = sem("ld_qkv")
        ld_pos = sem("ld_pos")
        ld_rest = sem("ld_rest")
        consts = sem("consts")
        padded = sem("padded")
        seeded = sem("seeded")
        stored = sem("stored")
        pt = sem("pt")
        pv_v = sem("pv_v")
        pv_a = sem("pv_a")
        pv_g = sem("pv_g")
        s_xs = sem("s_xs")
        s_xsT = sem("s_xsT")
        s_hT = sem("s_hT")
        s_qkv = sem("s_qkv")
        s_sq = sem("s_sq")
        s_qk = sem("s_qk")
        s_vall = sem("s_vall")
        s_ss = sem("s_ss")
        s_newton = sem("s_newton")
        s_rot = sem("s_rot")
        s_hi = sem("s_hi")
        s_parts = sem("s_parts")
        s_st = sem("s_st")
        s_st0 = sem("s_st0")
        s_st1 = sem("s_st1")
        s_s = sem("s_s")
        s_max = sem("s_max")
        s_mh = sem("s_mh")
        s_mp = sem("s_mp")
        s_mTp = sem("s_mTp")
        s_mT = sem("s_mT")
        s_e = sem("s_e")
        s_p = sem("s_p")
        s_vpad = sem("s_vpad")
        s_o = sem("s_o")
        s_oT4 = sem("s_oT4")
        s_oq = sem("s_oq")
        s_rec = sem("s_rec")
        s_on = sem("s_on")
        s_oTp = sem("s_oTp")
        s_oT = sem("s_oT")
        s_proj = sem("s_proj")
        s_pr = sem("s_pr")
        s_prT = sem("s_prT")
        s_x1 = sem("s_x1")
        s_bn = sem("s_bn")
        s_res = sem("s_res")

        b_bn = sem("b_bn")
        b_ff = sem("b_ff")
        b_fg = sem("b_fg")
        b_fgT = sem("b_fgT")
        b_fm = sem("b_fm")
        b_gu = sem("b_gu")
        b_hT = sem("b_hT")
        b_rstd = sem("b_rstd")
        b_late = sem("b_late")
        b_th = sem("b_th")
        b_x2 = sem("b_x2")
        b_xs = sem("b_xs")
        b_xsT = sem("b_xsT")
        b_y = sem("b_y")
        c_bn = sem("c_bn")
        c_ctx = sem("c_ctx")
        c_cx = sem("c_cx")
        c_hT = sem("c_hT")
        c_k = sem("c_k")
        c_km = sem("c_km")
        c_krec = sem("c_krec")
        c_kx = sem("c_kx")
        c_kxT = sem("c_kxT")
        c_kxTp = sem("c_kxTp")
        c_nb = sem("c_nb")
        c_qe = sem("c_qe")
        c_qmax = sem("c_qmax")
        c_qrec = sem("c_qrec")
        c_qs = sem("c_qs")
        c_qsum = sem("c_qsum")
        c_qv = sem("c_qv")
        c_qvb = sem("c_qvb")
        c_qx = sem("c_qx")
        c_qxT = sem("c_qxT")
        c_qxTp = sem("c_qxTp")
        c_rstd = sem("c_rstd")
        c_late = sem("c_late")
        c_xc = sem("c_xc")
        c_xs = sem("c_xs")
        c_xsT = sem("c_xsT")
        c_y = sem("c_y")
        c_yp = sem("c_yp")
        d_hT = sem("d_hT")
        d_hg = sem("d_hg")
        d_hgT = sem("d_hgT")
        d_hs = sem("d_hs")
        d_op = sem("d_op")
        d_rstd = sem("d_rstd")
        d_late = sem("d_late")
        d_th = sem("d_th")
        d_xc = sem("d_xc")
        d_xs = sem("d_xs")
        d_xsT = sem("d_xsT")

        NEWT, ROT, PARTS, SEED = 12, 3, 6, 4
        RSTEPS, LSTEPS = 14, 14
        N_FIRST, N_SMALL, N_REST = 16 * 3, 16 * 9, 16 * 12
        P_COND, P_ADA, P_QKV, P_MOD, P_MODS, P_PAR, P_W1, P_W3, P_W2, P_BIAS = range(1, 11)
        A_SQUARE, A_SIN, A_QKV, A_SQUARES, A_TANH, A_DONE = 1, 2, 3, 4, 5, 10
        V_COND, V_ADA, V_ANG, V_MOD, V_RSTD, V_RSTDS, V_MODS, V_LIN, V_DONE = 2, 4, 12, 15, 28, 41, 50, 54, 60

        block = ctx.enter_context(nc.Block())

        def rsqrt(v, sm, base, y_, s_, t_):
            n = base

            def did(ins):
                nonlocal n
                n += 1
                ins.then_inc(sm, 1)
                v.wait_ge(sm, n)
            did(nc.vector.tensor_scalar(t_.bitcast(I32), s_.bitcast(I32), 1, None, ALU.logical_shift_right))
            did(nc.vector.tensor_scalar(y_.bitcast(I32), t_.bitcast(I32), -1.0, float(MAGIC), ALU.mult, ALU.add))
            for _ in range(3):
                did(nc.vector.tensor_tensor(t_, y_, y_, ALU.mult))
                did(nc.vector.scalar_tensor_tensor(t_, t_, -0.5, s_, ALU.mult, ALU.mult))
                did(nc.vector.scalar_tensor_tensor(y_, t_, 1.5, y_, ALU.add, ALU.mult))
            return n

        def pair(u):
            return bass.ds(u * UNIT, UNIT)

        def flat(t_):
            return t_[:, :, :].rearrange("p u t -> p (u t)")

        def column(u, j, col):
            return mods[:, bass.ds(u * UNIT + j, 1), col:col + 1].rearrange("p a f -> p (a f)")

        def blocks_gpsimd(g):
            q = nc.gpsimd

            def normed(src, mean, rstd, centred, made, used):
                def step(t, p):
                    u, xs_ = t, xs2[p]
                    if not is_unit(u):
                        return
                    wait(g, used, u - 1)
                    x_ = src[:, pair(u), :]
                    if mean is not None:
                        q.tensor_tensor(xs_[:, :, :], x_, mean[:, pair(u)].unsqueeze(2).to_broadcast([128, UNIT, D]),
                                        ALU.subtract).then_inc(centred, 1)
                        g.wait_ge(centred, u + 1)
                        x_ = xs_[:, :, :]
                    q.tensor_tensor(xs_[:, :, :], x_, rstd[:, pair(u)].unsqueeze(2).to_broadcast([128, UNIT, D]),
                                    ALU.mult).then_inc(made, 1)
                return step

            def newton(sm, rstd, k):
                y_, s_, t_ = rstd[:, 0:EARLY], ms[:, 0:EARLY], rt[:, 0:EARLY]
                n = 6 + 4 * k
                g.wait_ge(sm, n)
                q.tensor_tensor(t_, y_, y_, ALU.mult).then_inc(sm, 1)
                g.wait_ge(sm, n + 1)
                q.tensor_tensor(t_, t_, s_, ALU.mult).then_inc(sm, 1)
                g.wait_ge(sm, n + 2)
                q.tensor_tensor(t_, three_halves[:, 0:EARLY], t_, ALU.subtract).then_inc(sm, 1)
                g.wait_ge(sm, n + 3)
                q.tensor_tensor(y_, y_, t_, ALU.mult).then_inc(sm, 1)

            def half_square(sm, mean, eps):
                cols = slice(0, EARLY)
                me, mo, de, do = bn[:, cols, 1], bn[:, cols, 4], bn[:, cols, 2], bn[:, cols, 5]
                m_, r_, y_ = ms[:, cols], rt[:, cols], ry[:, cols]
                if mean is None:
                    q.tensor_tensor(r_, me, me, ALU.mult)
                    q.tensor_tensor(y_, mo, mo, ALU.mult)
                else:
                    q.tensor_tensor(mean[:, cols], me, mo, ALU.add)
                    q.tensor_tensor(r_, me, mo, ALU.subtract)
                q.tensor_tensor(m_, de, do, ALU.add).then_inc(sm, 1)
                g.wait_ge(sm, 1)
                q.tensor_scalar(m_, m_, 0.5 / D, 0.5 * eps, ALU.mult, ALU.add)
                if mean is None:
                    q.tensor_tensor(r_, r_, y_, ALU.add).then_inc(sm, 1)
                else:
                    q.tensor_scalar(mean[:, cols], mean[:, cols], 0.5, 0.0, ALU.mult, ALU.add)
                    q.tensor_tensor(r_, r_, r_, ALU.mult).then_inc(sm, 1)
                g.wait_ge(sm, 2)
                q.tensor_scalar(r_, r_, 0.25 if mean is None else 0.125, 0.0, ALU.mult, ALU.add).then_inc(sm, 1)
                g.wait_ge(sm, 3)
                q.tensor_tensor(m_, m_, r_, ALU.add).then_inc(sm, 1)

            g.wait_ge(s_bn, EARLY)
            half_square(b_rstd, None, EPS0)
            for k in range(3):
                newton(b_rstd, rstd1, k)
            g.wait_ge(b_rstd, 18)
            b_normed = normed(x1, None, rstd1, None, b_xs, b_xsT)

            def b_step(t, p):
                if at(t, EARLY_U):
                    g.wait_ge(b_late, RSTEPS)
                b_normed(t, p)
            pipeline(g, b_step, 2, EARLY_U, U, 0)

            g.wait_ge(b_bn, EARLY_U)
            half_square(c_rstd, mean2, EPS1)
            for k in range(3):
                newton(c_rstd, rstd2, k)
            g.wait_ge(c_rstd, 18)
            c_normed = normed(x2, mean2, rstd2, c_xc, c_xs, c_xsT)

            def c_step(t, p):
                p1 = 1 - p
                if at(t + 3, EARLY_U):
                    g.wait_ge(c_late, LSTEPS)
                c_normed(t + 3, p1)
                if is_unit(t + 1):
                    u = t + 1
                    g.wait_ge(c_qmax, u + 1)
                    wait(g, c_qe, u - 1)
                    q.tensor_tensor(qs[p1][:, :, :, :], qvb[p1][:, :, 0:D].rearrange("p u (h d) -> p u h d", d=DH),
                                    qmax[p1][:, :, :].unsqueeze(3).to_broadcast([128, UNIT, H, DH]), ALU.subtract).then_inc(c_qs, 1)
                if is_unit(t):
                    g.wait_ge(c_qrec, t + 1)
                    wait(g, c_qxTp, t - 1)
                    q.tensor_tensor(qx[p][:, :, :, :], qe[p][:, :, :, :],
                                    qrec[p][:, :, :].unsqueeze(3).to_broadcast([128, UNIT, H, DH]), ALU.mult).then_inc(c_qx, 1)
                if at(t, EARLY_U):
                    g.wait_ge(c_bn, EARLY_U)
                    half_square(d_rstd, mean3, EPS1)
                for k in range(3):
                    if at(t, EARLY_U + 1 + k):
                        newton(d_rstd, rstd3, k)
            units(g, c_step, 3)

            g.wait_ge(d_rstd, 18)
            d_normed = normed(y, mean3, rstd3, d_xc, d_xs, d_xsT)

            def d_step(t, p):
                if at(t, EARLY_U):
                    g.wait_ge(d_late, LSTEPS)
                d_normed(t, p)
            pipeline(g, d_step, 2, EARLY_U, U, 0)

        def blocks_scalar(a, start=None):
            q = nc.scalar

            def modulated(u, p, sm, src):
                for j in range(UNIT):
                    last = q.activation(hT2[p][:, j, :], src[:, j * T:(j + 1) * T], ACT.Identity,
                                        bias=column(u, j, S2 if sm is b_hT else S3), scale=column(u, j, A2 if sm is b_hT else A3))
                last.then_inc(sm, 1)

            def b_step(t, p):
                def tanh(c):
                    u = t + 1
                    if is_unit(u):
                        a.wait_ge(b_gu, FC * u + c + 1)
                        wait(a, b_y, FC * (u - 1) + c + 1)
                        q.activation(th[c][:, :], bank[GU_BANK[c]][:, 0:UNIT * T], ACT.Tanh, scale=0.5).then_inc(b_th, 1)
                if is_unit(t + 2):
                    a.wait_ge(b_xsT, t + 3)
                    wait(a, b_gu, FC * (t + 1))
                tanh(0)
                if is_unit(t + 2):
                    modulated(t + 2, p, b_hT, bank[X_BANK])
                tanh(1)
                tanh(2)
            if start is None:
                return b_step
            units(a, b_step, 2, start)

            def c_step(t, p):
                p1 = 1 - p
                if is_unit(t + 1):
                    u = t + 1
                    a.wait_ge(c_nb, u + 1)
                    wait(a, c_kxTp, u - 1)
                    wait(a, c_krec, u - 1)
                    for j in range(UNIT):
                        last = q.activation(kx[p1][:, j, :], bank[1][:, j * T:(j + 1) * T], ACT.Exp,
                                            bias=knb[p1][:, j:j + 1], accum_out=ksum[p1][:, j:j + 1])
                    last.then_inc(c_kx, 1)
                    a.wait_ge(c_qs, u + 1)
                    wait(a, c_qx, u - 1)
                    q.activation(qe[p1][:, :, :, :].rearrange("p u h d -> p (u h d)"),
                                 qs[p1][:, :, :, :].rearrange("p u h d -> p (u h d)"), ACT.Exp).then_inc(c_qe, 1)
                if is_unit(t):
                    a.wait_ge(c_qxTp, t + 1)
                    wait(a, c_yp, t - 1)
                    q.activation(flat(qxT[p]), bank[6][:, 0:UNIT * D], ACT.Copy).then_inc(c_qxT, 1)
                if is_unit(t + 1):
                    u = t + 1
                    a.wait_ge(c_kxTp, u + 1)
                    wait(a, c_ctx, u - 1)
                    q.activation(flat(kxT[p1]), bank[4][:, 0:UNIT * D], ACT.Copy).then_inc(c_kxT, 1)
                if is_unit(t):
                    a.wait_ge(c_yp, t + 1)
                if is_unit(t + 3):
                    u = t + 3
                    a.wait_ge(c_xsT, u + 1)
                    wait(a, c_k, u - 1)
                    q.activation(flat(hT2[p1]), bank[0][:, 0:UNIT * T], ACT.Copy).then_inc(c_hT, 1)
                if is_unit(t):
                    q.activation(y[:, pair(t), :], bank[7][:, 0:UNIT * D].rearrange("p (u f) -> p u f", f=D), ACT.Copy).then_inc(c_y, 1)
            units(a, c_step, 3)

            def d_step(t, p):
                p1 = 1 - p
                if is_unit(t):
                    a.wait_ge(d_op, t + 1)
                    wait(a, d_hgT, t - 1)
                if is_unit(t + 2):
                    a.wait_ge(d_xsT, t + 3)
                    wait(a, d_hs, t + 1)
                if is_unit(t + 1):
                    a.wait_ge(d_hT, t + 2)
                    q.activation(th[p1][:, :], flat(hT2[p1]), ACT.Tanh, scale=0.5).then_inc(d_th, 1)
                if is_unit(t):
                    for j in range(UNIT):
                        last = q.activation(hg[p][:, j, :], bank[2 + p][:, j * T:(j + 1) * T], ACT.Identity,
                                            bias=column(t, j, GO), scale=column(t, j, GATE))
                    last.then_inc(d_hg, 1)
                if is_unit(t + 2):
                    modulated(t + 2, p, d_hT, bank[0 + p])
            units(a, d_step, 2)

        def early_seed(v, sm, rstd):
            v.wait_ge(sm, 4)
            nc.vector.tensor_scalar(rt[:, 0:EARLY].bitcast(I32), ms[:, 0:EARLY].bitcast(I32), 1, None,
                                    ALU.logical_shift_right).then_inc(sm, 1)
            v.wait_ge(sm, 5)
            nc.vector.tensor_scalar(rstd[:, 0:EARLY].bitcast(I32), rt[:, 0:EARLY].bitcast(I32), -1.0,
                                    float(MAGIC - 2 ** 22), ALU.mult, ALU.add).then_inc(sm, 1)

        def blocks_vector(v, start=None):
            q = nc.vector
            late = slice(EARLY, B)
            me, mo, de, do = bn[:, late, 1], bn[:, late, 4], bn[:, late, 2], bn[:, late, 5]
            m_, r_, y_ = ms[:, late], rt[:, late], ry[:, late]

            def late_rms():
                v.wait_ge(s_bn, B)
                q.tensor_tensor(r_, me, me, ALU.mult)
                q.tensor_tensor(y_, mo, mo, ALU.mult)
                q.tensor_tensor(m_, de, do, ALU.add).then_inc(b_late, 1)
                v.wait_ge(b_late, 1)
                q.tensor_tensor(r_, r_, y_, ALU.add)
                q.tensor_scalar(m_, m_, 1.0 / D, EPS0, ALU.mult, ALU.add).then_inc(b_late, 1)
                v.wait_ge(b_late, 2)
                q.scalar_tensor_tensor(m_, r_, 0.5, m_, ALU.mult, ALU.add).then_inc(b_late, 1)
                v.wait_ge(b_late, 3)
                assert rsqrt(v, b_late, 3, rstd1[:, late], m_, r_) == RSTEPS

            def late_std(mean, rstd, sm):
                q.tensor_tensor(mean[:, late], me, mo, ALU.add)
                q.tensor_tensor(r_, me, mo, ALU.subtract)
                q.tensor_tensor(m_, de, do, ALU.add).then_inc(sm, 1)
                v.wait_ge(sm, 1)
                q.tensor_scalar(mean[:, late], mean[:, late], 0.5, None, ALU.mult)
                q.tensor_scalar(m_, m_, 1.0 / D, EPS1, ALU.mult, ALU.add)
                q.scalar_tensor_tensor(r_, r_, 0.25, r_, ALU.mult, ALU.mult).then_inc(sm, 1)
                v.wait_ge(sm, 2)
                q.tensor_tensor(m_, m_, r_, ALU.add).then_inc(sm, 1)
                v.wait_ge(sm, 3)
                assert rsqrt(v, sm, 3, rstd[:, late], m_, r_) == LSTEPS

            def moments(u, src, sm):
                for j in range(UNIT):
                    last = q.bn_stats(bn[:, bass.ds(u * UNIT + j, 1), :].rearrange("p a s -> p (a s)"), src(j))
                last.then_inc(sm, 1)

            def b_step(t, p):
                def gate(c):
                    u = t + 1
                    if is_unit(u):
                        v.wait_ge(b_th, FC * u + c + 1)
                        q.scalar_tensor_tensor(yg[c][:, :], th[c][:, :], 1.0, bank[GU_BANK[c]][:, 0:UNIT * T], ALU.add,
                                               ALU.mult).then_inc(b_y, 1)

                def gated(c):
                    u = t + 1
                    if is_unit(u):
                        v.wait_ge(b_y, FC * u + c + 1)
                        wait(v, b_fm, u)
                        q.tensor_tensor(ff[c][:, :], bank[GU_BANK[c]][:, UNIT * T:], yg[c][:, :], ALU.mult).then_inc(b_ff, 1)
                if is_unit(t):
                    v.wait_ge(b_fm, t + 1)
                    wait(v, b_fgT, t)
                    q.tensor_tensor(fg[:, :, :], bank[F_BANK][:, 0:UNIT * T].rearrange("p (u t) -> p u t", t=T),
                                    mods[:, pair(t), G2:G2 + 1].to_broadcast([128, UNIT, T]), ALU.mult).then_inc(b_fg, 1)
                gate(0)
                gated(0)
                gate(1)
                gated(1)
                if at(t, EARLY_U + 2):
                    early_seed(v, c_rstd, rstd2)
                gate(2)
                if is_unit(t):
                    v.wait_ge(b_fgT, t + 1)
                    q.tensor_tensor(x2[:, pair(t), :], bank[FT_BANK][:, 0:UNIT * D].rearrange("p (u f) -> p u f", f=D),
                                    x1[:, pair(t), :], ALU.add).then_inc(b_x2, 1)
                    v.wait_ge(b_x2, t + 1)
                gated(2)
                if is_unit(t):
                    moments(t, lambda j: x2[:, bass.ds(t * UNIT + j, 1), :].rearrange("p a f -> p (a f)"), b_bn)
            if start is None:
                return b_step
            late_rms()
            units(v, b_step, 2, start)
            v.wait_ge(b_bn, U)
            late_std(mean2, rstd2, c_late)

            def y_moments(u):
                moments(u, lambda j: y[:, bass.ds(u * UNIT + j, 1), :].rearrange("p a f -> p (a f)"), c_bn)

            def c_step(t, p):
                p1 = 1 - p
                if at(t, EARLY_U + 1):
                    early_seed(v, d_rstd, rstd3)
                if is_unit(t - 1):
                    v.wait_ge(c_y, t)
                if is_unit(t):
                    v.wait_ge(c_ctx, t + 1)
                    v.wait_ge(c_krec, t + 1)
                    wait(v, c_yp, t - 1)
                    for j in range(UNIT):
                        last = q.scalar_tensor_tensor(cx[p][:, j, :], bank[5][:, j * D:(j + 1) * D], krec[p][:, j:j + 1],
                                                      blocks[:, :], ALU.mult, ALU.mult)
                    last.then_inc(c_cx, 1)
                if is_unit(t - 1):
                    y_moments(t - 1)
                if is_unit(t + 2):
                    u = t + 2
                    v.wait_ge(c_qv, u + 1)
                    wait(v, c_ctx, u - 1)
                    wait(v, c_qs, u - 1)
                    q.tensor_tensor(qvb[p][:, :, :], bank[2 + p][:, :].rearrange("p (u f) -> p u f", f=2 * D),
                                    bias_qv[:, :].unsqueeze(1).to_broadcast([128, UNIT, 2 * D]), ALU.add).then_inc(c_qvb, 1)
                if is_unit(t + 1):
                    v.wait_ge(c_qe, t + 2)
                    q.tensor_reduce(qsum[:, :, :], qe[p1][:, :, :, :], X_AXIS, ALU.add).then_inc(c_qsum, 1)
                if is_unit(t + 2):
                    u = t + 2
                    v.wait_ge(c_qvb, u + 1)
                    q.tensor_reduce(qmax[p][:, :, :], qvb[p][:, :, 0:D].rearrange("p u (h d) -> p u h d", d=DH),
                                    X_AXIS, ALU.max).then_inc(c_qmax, 1)
                    v.wait_ge(c_k, u + 1)
                    q.tensor_reduce(kmax[:, :], bank[1][:, 0:UNIT * T].rearrange("p (u t) -> p u t", t=T),
                                    X_AXIS, ALU.max, negate=True).then_inc(c_km, 1)
                if is_unit(t + 1):
                    u = t + 1
                    v.wait_ge(c_qsum, u + 1)
                    wait(v, c_qx, u - 1)
                    q.reciprocal(qrec[p1][:, :, :].rearrange("p u h -> p (u h)"),
                                 qsum[:, :, :].rearrange("p u h -> p (u h)")).then_inc(c_qrec, 1)
                    v.wait_ge(c_kx, u + 1)
                    q.reciprocal(krec[p1][:, :], ksum[p1][:, :]).then_inc(c_krec, 1)
                if is_unit(t + 2):
                    u = t + 2
                    v.wait_ge(c_km, u + 1)
                    wait(v, c_kx, u - 1)
                    q.tensor_scalar(knb[p][:, :], kmax[:, :], bias_k[:, 0:1], bias_k[:, 0:1], ALU.subtract, ALU.add).then_inc(c_nb, 1)
            units(v, c_step, 3)
            v.wait_ge(c_y, U)
            y_moments(U - 1)
            v.wait_ge(c_bn, U)

            def d_step(t, p):
                p1 = 1 - p
                if at(t, 0):
                    late_std(mean3, rstd3, d_late)
                if is_unit(t + 1):
                    u = t + 1
                    v.wait_ge(d_th, u + 1)
                    wait(v, d_op, u - 1)
                    q.scalar_tensor_tensor(hs[p1][:, :], th[p1][:, :], 1.0, flat(hT2[p1]), ALU.add, ALU.mult).then_inc(d_hs, 1)
                if is_unit(t):
                    v.wait_ge(d_hgT, t + 1)
                    q.tensor_tensor(res[:, pair(t), :], bank[4 + p][:, 0:UNIT * D].rearrange("p (u f) -> p u f", f=D),
                                    x2[:, pair(t), :], ALU.add).then_inc(s_res, 1)
            units(v, d_step, 2)

        def blocks_tensor(e, start=None):
            q = nc.tensor

            def turned(dst, src, sm):
                for j in range(UNIT):
                    last = q.transpose(dst[:, j * 128:(j + 1) * 128], src(j), ident[:, :])
                last.then_inc(sm, 1)

            def b_step(t, p):
                def hidden(c):
                    u = t + 1
                    if is_unit(u):
                        if c == 0:
                            e.wait_ge(b_hT, u + 1)
                            if at(u, 0):
                                e.wait_ge(s_max, NC * B)
                                e.wait_ge(s_st1, B)
                        wait(e, b_ff, FC * (u - 1) + c + 1)
                        q.matmul(bank[GU_BANK[c]][:, 0:UNIT * T], w1T[:, c * 128:c * 128 + 128], flat(hT2[1 - p]), start=True, stop=True)
                        q.matmul(bank[GU_BANK[c]][:, UNIT * T:], w3T[:, c * 128:c * 128 + 128], flat(hT2[1 - p]), start=True,
                                 stop=True).then_inc(b_gu, 1)

                def back(c):
                    if is_unit(t):
                        e.wait_ge(b_ff, FC * t + c + 1)
                        if c == 0:
                            wait(e, b_fg, t)
                            if at(t, 0):
                                e.wait_ge(s_p, NC * B)
                        last = q.matmul(bank[F_BANK][:, 0:UNIT * T], w2T[:, c, :], ff[c][:, :], start=c == 0, stop=c == FC - 1)
                        if c == FC - 1:
                            last.then_inc(b_fm, 1)
                back(0)
                hidden(0)
                if is_unit(t + 2):
                    e.wait_ge(b_xs, t + 3)
                    wait(e, b_hT, t + 2)
                    turned(bank[X_BANK], lambda j: xs2[p][:, j, :], b_xsT)
                back(1)
                back(2)
                hidden(1)
                hidden(2)
                if is_unit(t):
                    e.wait_ge(b_fg, t + 1)
                    wait(e, b_x2, t)
                    turned(bank[FT_BANK], lambda j: fg[:, j, :], b_fgT)
            if start is None:
                return b_step
            units(e, b_step, 2, start)

            def c_step(t, p):
                p1 = 1 - p
                if is_unit(t):
                    e.wait_ge(c_kxT, t + 1)
                    e.wait_ge(c_qvb, t + 1)
                    wait(e, c_cx, t)
                    for j in range(UNIT):
                        last = q.matmul(bank[5][:, j * D:(j + 1) * D], kxT[p][:, j, :], qvb[p][:, j, D:2 * D], start=True, stop=True)
                    last.then_inc(c_ctx, 1)
                if is_unit(t + 2):
                    u = t + 2
                    e.wait_ge(c_hT, u + 1)
                    wait(e, c_qvb, u - 1)
                    for j in range(UNIT):
                        last = q.matmul(bank[2 + p][:, j * 2 * D:(j + 1) * 2 * D], hT2[p][:, j, :],
                                        lin[:, 0:2, :].rearrange("p c f -> p (c f)"), start=True, stop=True)
                    last.then_inc(c_qv, 1)
                if is_unit(t + 3):
                    u = t + 3
                    e.wait_ge(c_xs, u + 1)
                    wait(e, c_hT, u)
                    turned(bank[0], lambda j: xs2[p1][:, j, :], c_xsT)
                if is_unit(t):
                    e.wait_ge(c_qx, t + 1)
                    wait(e, c_qxT, t)
                    turned(bank[6], lambda j: qx[p][:, j, :, :].rearrange("p h d -> p (h d)"), c_qxTp)
                if is_unit(t + 1):
                    u = t + 1
                    e.wait_ge(c_kx, u + 1)
                    wait(e, c_kxT, u)
                    turned(bank[4], lambda j: kx[p1][:, j, :], c_kxTp)
                if is_unit(t + 2):
                    u = t + 2
                    wait(e, c_kx, u)
                    q.matmul(bank[1][:, 0:UNIT * T], lin[:, 2, :], flat(hT2[p]), start=True, stop=True).then_inc(c_k, 1)
                if is_unit(t):
                    e.wait_ge(c_qxT, t + 1)
                    e.wait_ge(c_cx, t + 1)
                    wait(e, c_y, t)
                    for j in range(UNIT):
                        last = q.matmul(bank[7][:, j * D:(j + 1) * D], qxT[p][:, j, :], cx[p][:, j, :], start=True, stop=True)
                    last.then_inc(c_yp, 1)
            e.wait_ge(b_x2, U)
            units(e, c_step, 3)

            def d_step(t, p):
                p1 = 1 - p
                if is_unit(t + 3):
                    e.wait_ge(d_xs, t + 4)
                    wait(e, d_hT, t + 2)
                    turned(bank[0 + p1], lambda j: xs2[p1][:, j, :], d_xsT)
                if is_unit(t + 1):
                    u = t + 1
                    e.wait_ge(d_hs, u + 1)
                    wait(e, d_hg, u - 1)
                    q.matmul(bank[2 + p1][:, 0:UNIT * T], outw[:, :], hs[p1][:, :], start=True, stop=True).then_inc(d_op, 1)
                if is_unit(t):
                    e.wait_ge(d_hg, t + 1)
                    wait(e, s_res, t - 1)
                    turned(bank[4 + p], lambda j: hg[p][:, j, :], d_hgT)
            e.wait_ge(c_y, U)
            units(e, d_step, 3)

        @block.sync
        def _(sp):
            sp.dma_start(cond_n[:, :], cond).then_inc(ld_first, 16)
            for row, v, n in ((R_ADA, ada_b, 6), (R_N1, norm1_w, 1)):
                sp.dma_start(params_a[row:row + n, :], v.rearrange("(a n) -> a n", a=n)).then_inc(ld_first, 16)
            sp.dma_start(qkv_n[:, :, :], qkv_w.rearrange("(c p) f -> p c f", p=128)).then_inc(ld_qkv, 16)
            for row, v, n in ((R_PB, proj_b, 1), (R_N2, norm2_w, 1), (R_NG, norm_g, 1), (R_NB, norm_b, 1),
                              (R_BK, bk, 1), (R_EB, emb_b, 2), (R_SG, sn_g, 1), (R_SB, sn_b, 1), (R_OB, out_b, 1)):
                row -= FIRST_ROWS
                sp.dma_start(params_b[row:row + n, :], v.rearrange("(a n) -> a n", a=n)).then_inc(ld_small, 16)
            wait(sp, padded, 3)
            for w, wn in ((w1, w1_n), (w3, w3_n)):
                sp.dma_start(wn[:, 0:FC - 1, :], w[0:(FC - 1) * 128, :].rearrange("(c p) f -> p c f", p=128)).then_inc(ld_rest, 16)
                sp.dma_start(wn[0:LAST, FC - 1, :], w[(FC - 1) * 128:FFN, :]).then_inc(ld_rest, 16)
            sp.dma_start(w2_n[:, 0:FFN], w2).then_inc(ld_rest, 16)
            sp.dma_start(emb_n[:, :], emb_W).then_inc(ld_rest, 16)
            for i, w in enumerate((Wq, Wv, Wk)):
                sp.dma_start(lin_n[:, i, :], w).then_inc(ld_rest, 16)
            sp.dma_start(outw_n[:, :], out_W).then_inc(ld_rest, 16)
            sp.dma_start(bqv[:, 0:D], bq.rearrange("(a n) -> a n", a=1)).then_inc(ld_rest, 16)
            sp.dma_start(bqv[:, D:2 * D], bv.rearrange("(a n) -> a n", a=1)).then_inc(ld_rest, 16)
            with sp.Fori(0, NG) as g:
                sp.wait_ge(s_res, (g + 1) * (GRP // UNIT))
                sp.dma_start(out[bass.ds(g * GRP, GRP), :, :].rearrange("b t f -> t b f"),
                             res[:, bass.ds(g * GRP, GRP), :]).then_inc(stored, 16)
            sp.wait_ge(stored, 16 * NG)


        @block.gpsimd
        def _(g):
            q = nc.gpsimd
            q.memset(ident[:, :], 0.0).then_inc(consts, 1)
            g.wait_ge(consts, 1)
            q.affine_select(out=ident[:, :], in_=ident[:, :], compare_op=ALU.not_equal, fill=1.0, base=0,
                            pattern=[[-1, 128]], channel_multiplier=1).then_inc(consts, 1)
            q.memset(w1_n[:, FC - 1, :], 0.0).then_inc(padded, 1)
            q.memset(w3_n[:, FC - 1, :], 0.0).then_inc(padded, 1)
            q.memset(w2_n[:, FFN:], 0.0).then_inc(padded, 1)
            q.memset(identb[:, :], 0.0)
            q.memset(sel[:, :, :], 0.0)
            q.memset(blocks[:, :], 1.0)
            q.memset(ones[:, :], 1.0)
            q.memset(three_halves[:, :], 1.5).then_inc(consts, 1)
            g.wait_ge(consts, 3)
            q.affine_select(out=identb[:, :], in_=identb[:, :], compare_op=ALU.not_equal, fill=1.0, base=0,
                            pattern=[[-1, 128]], channel_multiplier=1)
            bl = blocks[:, :].rearrange("p (a b) -> p a b", b=DH)
            q.affine_select(out=bl, in_=bl, compare_op=ALU.is_ge, fill=0.0, base=0,
                            pattern=[[-DH, H], [0, DH]], channel_multiplier=1).then_inc(consts, 1)
            g.wait_ge(consts, 4)
            q.affine_select(out=bl, in_=bl, compare_op=ALU.is_ge, fill=0.0, base=DH - 1,
                            pattern=[[DH, H], [0, DH]], channel_multiplier=-1).then_inc(consts, 1)

            g.wait_ge(ld_pos, 48)
            for s in range(2):
                own, other = s * DH, 2 * DH + s * DH
                q.tensor_copy(rope[:, :, own + ROPE:own + DH],
                              qkw[:, s:s + 1, ROPE:DH].to_broadcast([128, B, DH - ROPE])).then_inc(pv_g, 1)
                q.memset(rope[:, :, other + ROPE:other + DH], 0.0).then_inc(pv_g, 1)
            g.wait_ge(pv_a, A_SIN)
            q.tensor_scalar(nsin[:, :, :], sincos[:, 0, :, :], -1.0, 1.0, ALU.mult, ALU.mult).then_inc(pv_g, 1)
            g.wait_ge(pv_g, 5)
            for s in range(2):
                for e in range(2):
                    own, other = s * DH, 2 * DH + s * DH
                    w_e = qkw[:, s:s + 1, e:ROPE:2].to_broadcast([128, B, AXES])
                    w_o = qkw[:, s:s + 1, 1 - e:ROPE:2].to_broadcast([128, B, AXES])
                    q.tensor_tensor(rope[:, :, own + e:own + ROPE:2], sincos[:, 1, :, :], w_e, ALU.mult).then_inc(pv_g, 1)
                    sn = sincos[:, 0, :, :] if e else nsin[:, :, :]
                    q.tensor_tensor(rope[:, :, other + e:other + ROPE:2], sn, w_o, ALU.mult).then_inc(pv_g, 1)
            def input_normed(t, p):
                b = t + 5
                if is_seq(b) and not before(t, POOL_NORMS):
                    if at(t, POOL_NORMS):
                        g.wait_ge(s_xs, b)
                    wait(g, s_xsT, b - 1)
                    q.tensor_tensor(xs[1 - p][:, :], xin[:, bass.ds(b, 1), :].rearrange("p a f -> p (a f)"),
                                    rstd_x[:, bass.ds(b, 1)].to_broadcast([128, D]), ALU.mult).then_inc(s_xs, 1)

            for k in range(2):
                g.wait_ge(consts, 5 + k)
                q.affine_select(out=sel[:, :, :], in_=sel[:, :, :], compare_op=ALU.not_equal, fill=1.0,
                                base=-H * k, pattern=[[-1, H], [0, 128]], channel_multiplier=1).then_inc(consts, 1)

            def step(t, p):
                if at(t, POOL_NORMS):
                    g.wait_ge(pv_v, V_RSTDS)
                input_normed(t, p)
                b = t + 4
                if not is_seq(b):
                    return
                wait(g, s_parts, PARTS * (b - 2) + PARTS)
                g.wait_ge(s_qk, b + 1)
                f4 = rope[:, bass.ds(b, 1), :].rearrange("p a (u s d) -> p (a u) s d", u=2, s=2)
                qk4 = qk[p][:, :, :].rearrange("p (s h) d -> p s h d", s=2)
                rot4 = rot[p][:, :, :].rearrange("p (s h) d -> p s h d", s=2)
                pa4 = partner[:, :, :].rearrange("p (s h) d -> p s h d", s=2)
                q.tensor_tensor(rot4, qk4, f4[:, 0, :, :].unsqueeze(2).to_broadcast([128, 2, H, DH]), ALU.mult)
                for e in range(2):
                    last = q.tensor_tensor(pa4[:, :, :, e::2], qk4[:, :, :, 1 - e:ROPE:2],
                                           f4[:, 1, :, e:ROPE:2].unsqueeze(2).to_broadcast([128, 2, H, AXES]), ALU.mult)
                last.then_inc(s_rot, 1)
                g.wait_ge(s_rot, ROT * b + 1)
                q.tensor_tensor(rot[p][:, :, 0:ROPE], rot[p][:, :, 0:ROPE], partner[:, :, :], ALU.add).then_inc(s_rot, 1)
                g.wait_ge(s_ss, SEED * b + SEED)
                y_, s_, t_ = qv_y[p][:, :], qv_s[p][:, :], qv_t[:, :]
                for k in range(3):
                    q.tensor_tensor(t_, y_, y_, ALU.mult).then_inc(s_newton, 1)
                    g.wait_ge(s_newton, NEWT * b + 4 * k + 1)
                    q.tensor_tensor(t_, t_, s_, ALU.mult).then_inc(s_newton, 1)
                    g.wait_ge(s_newton, NEWT * b + 4 * k + 2)
                    q.tensor_tensor(t_, three_halves[:, :], t_, ALU.subtract).then_inc(s_newton, 1)
                    g.wait_ge(s_newton, NEWT * b + 4 * k + 3)
                    q.tensor_tensor(y_, y_, t_, ALU.mult).then_inc(s_newton, 1)
                    g.wait_ge(s_newton, NEWT * b + 4 * k + 4)
                g.wait_ge(s_rot, ROT * b + 2)
                q.tensor_tensor(rot[p][:, :, :], rot[p][:, :, :],
                                qv_y[p][:, :].unsqueeze(2).to_broadcast([128, 2 * H, DH]), ALU.mult).then_inc(s_rot, 1)

            g.wait_ge(pv_g, 13)
            steps(g, step)
            blocks_gpsimd(g)


        @block.scalar
        def _(a):
            q = nc.scalar
            a.dma_start(ada_n[:, :, :], ada_w.rearrange("(c p) f -> p c f", p=128)).then_inc(ld_ada, 16)
            rows = slice(0, HEAD_B)
            a.dma_start(xin[:, rows, :], x[rows, :, :].rearrange("b t f -> t b f")).then_inc(ld_head, 16)
            a.dma_start(posn[:, :].rearrange("p (b c) -> p b c", c=AXES), pos.rearrange("b t c -> t b c")).then_inc(ld_pos, 16)
            for s, w in enumerate((q_norm_w, k_norm_w)):
                a.dma_start(qkw[:, s, :], w.partition_broadcast(128)).then_inc(ld_pos, 16)
            rows = slice(HEAD_B, B)
            a.dma_start(xin[:, rows, :], x[rows, :, :].rearrange("b t f -> t b f")).then_inc(ld_x, 16)
            a.dma_start(proj_n[:, :], proj_w).then_inc(ld_proj, 16)
            a.wait_ge(ld_head, 16)
            q.activation(big[:, 0:HEAD_B, :], xin[:, 0:HEAD_B, :], ACT.Square).then_inc(pv_a, 1)
            a.wait_ge(pv_v, V_ANG)
            q.activation(sincos[:, :, :, :].rearrange("p s b c -> p (s b c)"),
                         ang[:, :, :].rearrange("p s n -> p (s n)"), ACT.Sin).then_inc(pv_a, 1)
            a.wait_ge(pt, P_QKV)
            q.activation(qkvT[:, :], bank[3][:, 0:3 * D], ACT.Copy).then_inc(pv_a, 1)
            a.wait_ge(ld_x, 16)
            q.activation(big[:, HEAD_B:, :], xin[:, HEAD_B:, :], ACT.Square).then_inc(pv_a, 1)

            def prepare_weights():
                a.wait_ge(pv_v, V_COND)
                q.activation(ctanh[:, :], condT[:, :], ACT.Tanh, scale=0.5).then_inc(pv_a, 1)
                a.wait_ge(pt, P_W1)
                q.activation(w1T[:, :], bank[5][:, 0:FC * 128], ACT.Copy).then_inc(pv_a, 1)
                a.wait_ge(pt, P_W3)
                q.activation(w3T[:, :], bank[6][:, 0:FC * 128], ACT.Copy).then_inc(pv_a, 1)
                a.wait_ge(pt, P_W2)
                q.activation(w2T[:, :, :].rearrange("p c f -> p (c f)"), bank[2][:, 0:FC * 128], ACT.Copy, scale=0.5).then_inc(pv_a, 1)
                q.activation(projT[:, :], bank[2][:, FC * 128:FC * 128 + 128], ACT.Copy).then_inc(pv_a, 1)
                q.activation(outw[:, :], outw_n[:, :], ACT.Copy, scale=0.5).then_inc(pv_a, 1)
                a.wait_ge(seeded, 5)
            a.wait_ge(pv_v, V_MOD)

            def step(t, p):
                q1, q0 = (p + 1) % 2, p

                def exp(c):
                    if is_seq(t):
                        a.wait_ge(s_e, NC * t + c + 1)
                        wait(a, s_o, NC * (t - 1) + c + 1)
                        q.activation(probs[c][:, :, :].rearrange("p h t -> p (h t)"), bank[E_BANK[c % 2]][:, :],
                                     ACT.Exp, scale=SCALE).then_inc(s_p, 1)

                def stacked(k):
                    if not is_seq(t + 1):
                        return
                    b = t + 1
                    sb_ = bank[STACK_BANK][:, :].bitcast(BF16).rearrange("p (s j t) -> p s j t", s=2, t=T)
                    js = slice(PAIRS // 2, PAIRS)
                    if k == 0:
                        a.wait_ge(s_st, 2 * b + 2)
                        wait(a, s_e, NC * (b - 2) + NC)
                        q.activation(qT[q1][:, js, :], sb_[:, 0, :, :], ACT.Copy)
                    elif k == 1:
                        q.activation(kT[q1][0:64, js, 0, :], sb_[0:64, 1, :, :], ACT.Copy)
                    else:
                        q.activation(kT[q1][64:128, js, 1, :], sb_[64:128, 1, :, :], ACT.Copy).then_inc(s_st1, 1)

                def high(s):
                    if not is_seq(t + 3):
                        return
                    b = t + 3
                    if s == 0:
                        a.wait_ge(s_rot, ROT * b + ROT)
                        wait(a, s_st, 2 * (b - 2) + 2)
                    slots = parts[q1][:, s, :, :].rearrange("p h (k d) -> p h k d", d=DH)[:, :, 2 * s:2 * s + 3, :]
                    last = q.activation(slots, rot[q1][:, s * H:(s + 1) * H, :].unsqueeze(2).to_broadcast([128, H, 3, DH]), ACT.Copy)
                    if s == 1:
                        last.then_inc(s_hi, 1)

                if is_seq(t):
                    a.wait_ge(s_mTp, t + 1)
                    wait(a, s_e, NC * (t - 2) + NC)
                    q.activation(mT[q0][:, :], bank[E_BANK[0]][:, 0:T // 2].bitcast(BF16), ACT.Copy).then_inc(s_mT, 1)
                if is_seq(t + 4):
                    a.wait_ge(s_xsT, t + 5)
                    wait(a, s_qkv, t + 3)
                stacked(0)
                if is_seq(t + 4):
                    b = t + 4
                    q.activation(hT[q0][:, :], bank[W_BANK][:, 0:T], ACT.Identity,
                                 bias=mods[:, bass.ds(b, 1), S1:S1 + 1].rearrange("p a f -> p (a f)"),
                                 scale=mods[:, bass.ds(b, 1), A1:A1 + 1].rearrange("p a f -> p (a f)")).then_inc(s_hT, 1)
                stacked(1)
                exp(0)
                stacked(2)
                if is_seq(t - 1):
                    b = t - 1
                    a.wait_ge(s_oTp, b + 1)
                    wait(a, s_proj, b)
                    q.activation(oT[:, :], bank[P_BANK][:, 0:T], ACT.Copy).then_inc(s_oT, 1)
                exp(1)
                if is_seq(t + 4):
                    b = t + 4
                    a.wait_ge(s_qkv, b + 1)
                    wait(a, s_ss, SEED * (b - 2) + 1)
                    q.activation(qk2[q0][:, :, :].rearrange("p h d -> p (h d)"), bank[W_BANK][:, 0:2 * D], ACT.Square).then_inc(s_sq, 1)
                if is_seq(t + 4):
                    b = t + 4
                    wait(a, s_rot, ROT * (b - 2) + 1)
                    q.activation(qk[q0][:, :, :].rearrange("p h d -> p (h d)"), bank[W_BANK][:, 0:2 * D], ACT.Copy).then_inc(s_qk, 1)
                if is_seq(t + 4):
                    b = t + 4
                    q.activation(vall[:, bass.ds(b, 1), :].rearrange("p a f -> p (a f)"), bank[W_BANK][:, 2 * D:3 * D],
                                 ACT.Copy).then_inc(s_vall, 1)
                exp(2)
                if is_seq(t - 1):
                    a.wait_ge(s_proj, t)
                    wait(a, s_prT, t - 1)
                exp(3)
                if is_seq(t - 1):
                    b = t - 1
                    q.activation(pr[:, :], bank[P_BANK][:, 0:T], ACT.Identity,
                                 bias=mods[:, bass.ds(b, 1), GB1:GB1 + 1].rearrange("p a f -> p (a f)"),
                                 scale=mods[:, bass.ds(b, 1), G1:G1 + 1].rearrange("p a f -> p (a f)")).then_inc(s_pr, 1)
                high(0)
                if is_seq(t):
                    b = t
                    a.wait_ge(s_o, NC * b + NC)
                    wait(a, s_oq, b)
                    q.activation(oT4[:, :], bank[O_BANK][:, :], ACT.Copy).then_inc(s_oT4, 1)
                high(1)

            def step_with_preparation(t, p):
                step(t, p)
                if at(t, -4):
                    prepare_weights()
                if at(t, 0):
                    a.wait_ge(pv_v, V_MODS)
            steps(a, step_with_preparation, blocks_scalar(a))
            blocks_scalar(a, 1)


        @block.vector
        def _(v):
            q = nc.vector
            n = 0

            def count(ins):
                nonlocal n
                n += 1
                ins.then_inc(pv_v, 1)

            def did(ins):
                count(ins)
                v.wait_ge(pv_v, n)

            for p in range(2):
                q.memset(parts[p][:, :, :, :].rearrange("p s h d -> p (s h d)").bitcast(F32), 0.0)
                q.memset(kT[p][:, :, :, :].rearrange("p j s t -> p (j s t)").bitcast(F32), 0.0)
                q.memset(vpad[p][:, :, :], 0.0).then_inc(seeded, 1)
            q.memset(mparts[:, :].bitcast(F32), 0.0).then_inc(seeded, 1)
            v.wait_ge(seeded, 3)
            for p in range(2):
                q.memset(vpad[p][:, :, DH:DH + 1], 1.0).then_inc(seeded, 1)

            v.wait_ge(pt, P_COND)
            count(q.tensor_copy(par[:, 0:FIRST_ROWS], bank[0][:, 0:FIRST_ROWS]))
            count(q.tensor_copy(condT[:, :], bank[0][:, 32:32 + B]))
            assert n == V_COND
            v.wait_ge(pt, P_ADA)
            count(q.tensor_copy(adaT[:, 0:512], bank[1][:, :]))
            count(q.tensor_copy(adaT[:, 512:768], bank[2][:, 0:256]))
            assert n == V_ADA
            v.wait_ge(ld_pos, 48)
            r0, r1 = ang[:, 0, :], ang[:, 1, :]
            did(q.tensor_scalar(turns[:, :], posn[:, :], 1.0 / (2 * math.pi), ROUND, ALU.mult, ALU.add))
            did(q.tensor_scalar(turns[:, :], turns[:, :], -ROUND, None, ALU.add))
            did(q.scalar_tensor_tensor(r0, turns[:, :], -TWO_PI_A, posn[:, :], ALU.mult, ALU.add))
            did(q.scalar_tensor_tensor(r0, turns[:, :], -TWO_PI_B, r0, ALU.mult, ALU.add))
            did(q.scalar_tensor_tensor(r0, turns[:, :], -TWO_PI_C, r0, ALU.mult, ALU.add))
            did(q.scalar_tensor_tensor(r1, r0, -1.0, r0, ALU.mult, ALU.max))
            did(q.tensor_scalar(r1, r1, -1.0, math.pi / 2, ALU.mult, ALU.add))
            did(q.tensor_scalar(r0, r0, PI_BELOW, -PI_BELOW, ALU.min, ALU.max))
            assert n == V_ANG
            v.wait_ge(pt, P_MOD)
            did(q.tensor_tensor(modr[:, 0:2, :], bank[4][:, 0:2 * B].rearrange("p (c b) -> p c b", b=B),
                                par[:, R_ADA:R_ADA + 2].unsqueeze(2).to_broadcast([128, 2, B]), ALU.add))
            count(q.tensor_scalar(mods[:, :, A1], modr[:, 1, :], 1.0, par[:, R_N1:R_N1 + 1], ALU.add, ALU.mult))
            count(q.tensor_copy(mods[:, :, S1], modr[:, 0, :]))
            assert n == V_MOD

            def input_rstd(rows):
                nonlocal n
                did(q.tensor_reduce(ms[:, rows], big[:, rows, :], X_AXIS, ALU.add))
                did(q.tensor_scalar(ms[:, rows], ms[:, rows], 1.0 / D, EPS0, ALU.mult, ALU.add))
                n = rsqrt(v, pv_v, n, rstd_x[:, rows], ms[:, rows], rt[:, rows])

            v.wait_ge(pv_a, A_SQUARE)
            input_rstd(slice(0, HEAD_B))
            assert n == V_RSTD

            def other_rstd():
                v.wait_ge(pv_a, A_SQUARES)
                input_rstd(slice(HEAD_B, B))
                assert n == V_RSTDS

            def other_modulations():
                v.wait_ge(pt, P_PAR)
                count(q.tensor_copy(par[:, FIRST_ROWS:], bank[3][:, 0:NROW - FIRST_ROWS]))
                did(q.tensor_tensor(modr[:, 2:6, :], bank[0][:, 2 * B:6 * B].rearrange("p (c b) -> p c b", b=B),
                                    par[:, R_ADA + 2:R_ADA + 6].unsqueeze(2).to_broadcast([128, 4, B]), ALU.add))
                count(q.tensor_copy(mods[:, :, G1], modr[:, 2, :]))
                count(q.tensor_scalar(mods[:, :, GB1], modr[:, 2, :], par[:, R_PB:R_PB + 1], None, ALU.mult))
                count(q.tensor_scalar(mods[:, :, A2], modr[:, 4, :], 1.0, par[:, R_N2:R_N2 + 1], ALU.add, ALU.mult))
                count(q.tensor_copy(mods[:, :, S2], modr[:, 3, :]))
                count(q.tensor_copy(mods[:, :, G2], modr[:, 5, :]))
                count(q.tensor_copy(mods[:, :, GATE], condT[:, :]))
                count(q.tensor_scalar(mods[:, :, GO], condT[:, :], par[:, R_OB:R_OB + 1], None, ALU.mult))
                assert n == V_MODS

            def style():
                v.wait_ge(pv_a, A_TANH)
                did(q.scalar_tensor_tensor(csilu[:, :], ctanh[:, :], 1.0, condT[:, :], ALU.add, ALU.mult))
                did(q.tensor_scalar(csilu[:, :], csilu[:, :], 0.5, None, ALU.mult))
                count(q.tensor_scalar(nbb[:, :], par[:, R_NB:R_NB + 1].to_broadcast([128, 128]), 1.0, None, ALU.mult))
                v.wait_ge(ld_rest, N_REST)
                count(q.tensor_scalar(lin[:, :, :], lin_n[:, :, :], par[:, R_NG:R_NG + 1], None, ALU.mult))
                assert n == V_LIN

            def biases():
                v.wait_ge(pt, P_BIAS)
                count(q.tensor_copy(bias_qv[:, :], bank[3][:, 0:2 * D]))
                count(q.tensor_tensor(bias_k[:, :], bank[3][:, 2 * D:2 * D + 1], par[:, R_BK:R_BK + 1], ALU.add))
                did(q.tensor_tensor(embr[:, :, :], bank[3][:, 3 * D:3 * D + 2 * B].rearrange("p (c b) -> p c b", b=B),
                                    par[:, R_EB:R_EB + 2].unsqueeze(2).to_broadcast([128, 2, B]), ALU.add))
                count(q.tensor_scalar(mods[:, :, A3], embr[:, 0, :], 1.0, par[:, R_SG:R_SG + 1], ALU.add, ALU.mult))
                did(q.tensor_scalar(mods[:, :, S3], embr[:, 0, :], 1.0, par[:, R_SB:R_SB + 1], ALU.add, ALU.mult))
                did(q.tensor_tensor(mods[:, :, S3], mods[:, :, S3], embr[:, 1, :], ALU.add))
                assert n == V_DONE

            def step(t, p):
                q0, q1 = p, (p + 1) % 2
                def rowmax(c):
                    if is_seq(t + 1):
                        b = t + 1
                        v.wait_ge(s_s, NC * b + c + 1)
                        if c == 0:
                            wait(v, s_mp, b - 1)
                        q.tensor_reduce(nmax[q1][:, c * HPC:(c + 1) * HPC],
                                        bank[S_BANK[c % 2]][:, :].rearrange("p (h t) -> p h t", t=T),
                                        X_AXIS, ALU.max, negate=True).then_inc(s_max, 1)
                def cut(k):
                    b = t + 2
                    if not is_seq(b):
                        return
                    both = parts[q0][:, :, :, :].rearrange("p s h (k d) -> p (s h) k d", d=DH)
                    pq = parts[q0][:, 0, :, :].rearrange("p h (k d) -> p h k d", d=DH)
                    pk = parts[q0][:, 1, :, :].rearrange("p h (k d) -> p h k d", d=DH)
                    if k == 0:
                        v.wait_ge(s_hi, b + 1)
                        q.tensor_tensor(rest[:, :, :], rot[q0][:, :, :], both[:, :, 2, :], ALU.subtract).then_inc(s_parts, 1)
                    if k == 1:
                        v.wait_ge(s_parts, PARTS * b + 1)
                        q.tensor_copy(both[:, :, 5, :], rest[:, :, :]).then_inc(s_parts, 1)
                    if k == 2:
                        v.wait_ge(s_parts, PARTS * b + 2)
                        q.tensor_tensor(pq[:, :, 4, :], rest[:, 0:H, :], pq[:, :, 5, :], ALU.subtract).then_inc(s_parts, 1)
                        q.tensor_tensor(pk[:, :, 1, :], rest[:, H:, :], pk[:, :, 5, :], ALU.subtract).then_inc(s_parts, 1)
                        q.tensor_copy(pq[:, :, 3, :], pq[:, :, 5, :]).then_inc(s_parts, 1)
                        q.tensor_copy(pk[:, :, 0, :], pk[:, :, 5, :]).then_inc(s_parts, 1)

                def seed(k):
                    b = t + 4
                    if not is_seq(b):
                        return
                    if k == 0:
                        v.wait_ge(s_sq, b + 1)
                        wait(v, s_newton, NEWT * (b - 2) + NEWT)
                        q.tensor_reduce(qv_ms[q0][:, :], qk2[q0][:, :, :], X_AXIS, ALU.add).then_inc(s_ss, 1)
                    else:
                        v.wait_ge(s_ss, SEED * b + k)
                    if k == 1:
                        q.tensor_scalar(qv_s[q0][:, :], qv_ms[q0][:, :], 0.5 / DH, 0.5 * EPS0, ALU.mult, ALU.add).then_inc(s_ss, 1)
                    if k == 2:
                        q.tensor_scalar(qv_ms[q0][:, :].bitcast(I32), qv_s[q0][:, :].bitcast(I32), 1, None,
                                        ALU.logical_shift_right).then_inc(s_ss, 1)
                    if k == 3:
                        wait(v, s_rot, ROT * (b - 2) + ROT)
                        q.tensor_scalar(qv_y[q0][:, :].bitcast(I32), qv_ms[q0][:, :].bitcast(I32), -1.0,
                                        float(MAGIC - 2 ** 22), ALU.mult, ALU.add).then_inc(s_ss, 1)

                cut(0)
                if is_seq(t):
                    b = t
                    v.wait_ge(s_vall, b + 1)
                    wait(v, s_o, NC * (b - 2) + NC)
                    q.tensor_scalar(vpad[q0][:, :, 0:DH], vall[:, bass.ds(b, 1), :].rearrange("p a (h d) -> p (a h) d", d=DH),
                                    1.0, None, ALU.mult).then_inc(s_vpad, 1)
                if is_seq(t - 1):
                    b = t - 1
                    v.wait_ge(s_oq, b + 1)
                    oq = bank[O_BANK][:, :].rearrange("p (h w) -> p h w", w=VW)
                    q.reciprocal(rsum[:, :], oq[:, :, DH:DH + 1].rearrange("p h a -> p (h a)")).then_inc(s_rec, 1)
                cut(1)
                if is_seq(t - 1):
                    b = t - 1
                    v.wait_ge(s_rec, b + 1)
                    wait(v, s_oTp, b)
                    q.tensor_tensor(o[:, :, :], bank[O_BANK][:, :].rearrange("p (h w) -> p h w", w=VW)[:, :, 0:DH],
                                    rsum[:, :].unsqueeze(2).to_broadcast([128, H, DH]), ALU.mult).then_inc(s_on, 1)
                if is_seq(t + 5) and before(t, POOL_NORMS):
                    b = t + 5
                    wait(v, s_xsT, b - 1)
                    q.tensor_scalar(xs[q1][:, :], xin[:, bass.ds(b, 1), :].rearrange("p a f -> p (a f)"),
                                    rstd_x[:, bass.ds(b, 1)], None, ALU.mult).then_inc(s_xs, 1)
                rowmax(0)
                cut(2)
                rowmax(1)
                rowmax(2)
                if is_seq(t + 2):
                    b = t + 2
                    v.wait_ge(s_st, 2 * b + 1)
                    wait(v, s_e, NC * (b - 2) + NC // 2)
                    sb_ = bank[STACK_BANK][:, :].bitcast(BF16).rearrange("p (s j t) -> p s j t", s=2, t=T)
                    js = slice(0, PAIRS // 2)
                    q.tensor_copy(qT[q0][:, js, :], sb_[:, 0, :, :])
                    q.tensor_copy(kT[q0][0:64, js, 0, :], sb_[0:64, 1, :, :])
                    q.tensor_copy(kT[q0][64:128, js, 1, :], sb_[64:128, 1, :, :]).then_inc(s_st0, 1)
                rowmax(3)
                seed(0)
                if is_seq(t + 1):
                    b = t + 1
                    v.wait_ge(s_max, NC * b + NC)
                    wait(v, s_mTp, b)
                    q.tensor_copy(mparts[:, 0:H], nmax[q1][:, :]).then_inc(s_mh, 1)
                seed(1)
                if is_seq(t + 1):
                    b = t + 1
                    v.wait_ge(s_mh, b + 1)
                    q.tensor_tensor(mparts[:, H:2 * H], nmax[q1][:, :], mparts[:, 0:H], ALU.subtract).then_inc(s_mp, 1)
                if is_seq(t - 1):
                    b = t - 1
                    v.wait_ge(s_prT, b + 1)
                    q.tensor_tensor(x1[:, bass.ds(b, 1), :].rearrange("p a f -> p (a f)"), bank[P_BANK][:, 0:D],
                                    xin[:, bass.ds(b, 1), :].rearrange("p a f -> p (a f)"), ALU.add).then_inc(s_x1, 1)
                seed(2)
                if is_seq(t - 1):
                    v.wait_ge(s_x1, t)
                seed(3)
                if is_seq(t - 1):
                    q.bn_stats(bn[:, bass.ds(t - 1, 1), :].rearrange("p a s -> p (a s)"),
                               x1[:, bass.ds(t - 1, 1), :].rearrange("p a f -> p (a f)")).then_inc(s_bn, 1)
                if at(t, B - LEAD + 1):
                    early_seed(v, b_rstd, rstd1)

            def step_with_preparation(t, p):
                step(t, p)
                for k, prepare in ((-4, other_rstd), (-4, other_modulations),
                                   (-4, style), (-2, biases)):
                    if at(t, k):
                        prepare()
            steps(v, step_with_preparation, blocks_vector(v))
            blocks_vector(v, 1)

        @block.tensor
        def _(e):
            q = nc.tensor
            e.wait_ge(consts, 2)
            e.wait_ge(ld_first, N_FIRST)
            q.transpose(bank[0][:, 0:FIRST_ROWS], params_a[:, :], ident[0:FIRST_ROWS, 0:FIRST_ROWS])
            q.transpose(bank[0][:, 32:32 + B], cond_n[:, :], ident[0:B, 0:B]).then_inc(pt, 1)
            e.wait_ge(ld_ada, 16)
            for c in range(6):
                last = q.transpose(bank[1 + c // 4][:, c % 4 * 128:c % 4 * 128 + 128], ada_n[:, c, :], ident[:, :])
            last.then_inc(pt, 1)
            e.wait_ge(ld_qkv, 16)
            for c in range(3):
                last = q.transpose(bank[3][:, c * 128:c * 128 + 128], qkv_n[:, c, :], ident[:, :])
            last.then_inc(pt, 1)
            e.wait_ge(pv_v, V_ADA)
            for cs, dst in (((0, 1), bank[4]), ((2, 3, 4, 5), bank[0])):
                for c in cs:
                    last = q.matmul(dst[:, c * B:(c + 1) * B], adaT[:, c * 128:c * 128 + 128], condT[:, :], start=True, stop=True)
                last.then_inc(pt, 1)
            e.wait_ge(pv_a, A_QKV)

            def prepare_weights():
                e.wait_ge(ld_small, N_SMALL)
                q.transpose(bank[3][:, 0:NROW - FIRST_ROWS], params_b[:, :],
                            ident[0:NROW - FIRST_ROWS, 0:NROW - FIRST_ROWS]).then_inc(pt, 1)
                e.wait_ge(ld_rest, N_REST)
                for k, src in ((5, w1_n), (6, w3_n)):
                    for c in range(FC):
                        last = q.transpose(bank[k][:, c * 128:c * 128 + 128], src[:, c, :], ident[:, :])
                    last.then_inc(pt, 1)
                for c in range(FC):
                    q.transpose(bank[2][:, c * 128:c * 128 + 128], w2_n[:, c * 128:c * 128 + 128], ident[:, :])
                e.wait_ge(ld_proj, 16)
                q.transpose(bank[2][:, FC * 128:FC * 128 + 128], proj_n[:, :], ident[:, :]).then_inc(pt, 1)
                e.wait_ge(seeded, 5)
                e.wait_ge(consts, 4)
                e.wait_ge(pv_v, V_MOD)

            def prepare_biases():
                e.wait_ge(pv_v, V_LIN)
                q.matmul(bank[3][:, 0:2 * D], nbb[:, :], lin_n[:, 0:2, :].rearrange("p c f -> p (c f)"), start=True, stop=False)
                q.matmul(bank[3][:, 0:2 * D], ones[:, :], bqv[:, :], start=False, stop=True)
                q.matmul(bank[3][:, 2 * D:2 * D + 1], lin_n[:, 2, :], nbb[:, 0:1], start=True, stop=True)
                for c in range(2):
                    last = q.matmul(bank[3][:, 3 * D + c * B:3 * D + (c + 1) * B], emb_n[:, c * 128:c * 128 + 128], csilu[:, :],
                                    start=True, stop=True)
                last.then_inc(pt, 1)

            def step(t, p):
                q0, q1 = p, (p + 1) % 2

                def weighted(c):
                    if not is_seq(t):
                        return
                    if c == 0:
                        e.wait_ge(s_mT, t + 1)
                    wait(e, s_p, NC * t + c - 1)
                    for i in range(HPC):
                        h = c * HPC + i
                        dst = bank[E_BANK[c % 2]][:, i * T:(i + 1) * T]
                        q.matmul(dst, kT[q0][:, h // 2, h % 2, :], qT[q0][:, h // 2, :], start=True, stop=False)
                        last = q.matmul(dst, sel[:, h, :], mT[q0][:, :], start=False, stop=True)
                    last.then_inc(s_e, 1)

                def scores(c):
                    if not is_seq(t + 1):
                        return
                    b = t + 1
                    if c == 0:
                        e.wait_ge(s_st0, b + 1)
                    if c == NC // 2:
                        e.wait_ge(s_st1, b + 1)
                    wait(e, s_max, NC * b + c - 1)
                    for i in range(HPC // 2):
                        j = c * (HPC // 2) + i
                        last = q.matmul(bank[S_BANK[c % 2]][:, i * 2 * T:(i + 1) * 2 * T], qT[q1][:, j, :],
                                        kT[q1][:, j, :, :].rearrange("p s t -> p (s t)"), start=True, stop=True)
                    last.then_inc(s_s, 1)

                def values(c):
                    if not is_seq(t):
                        return
                    if c == 0:
                        e.wait_ge(s_vpad, t + 1)
                        wait(e, s_on, t)
                    e.wait_ge(s_p, NC * t + c + 1)
                    for i in range(HPC):
                        last = q.matmul(bank[O_BANK][VW * i:VW * (i + 1), c * T:(c + 1) * T], vpad[q0][:, c * HPC + i, :],
                                        probs[c][:, i, :], start=True, stop=True)
                    last.then_inc(s_o, 1)

                def stack(half):
                    b = t + 2 - half
                    if not is_seq(b):
                        return
                    if half == 0:
                        e.wait_ge(s_parts, PARTS * b + PARTS)
                        wait(e, s_st1, b)
                    else:
                        e.wait_ge(s_st0, b + 1)
                    src = parts[q0 if half == 0 else q1]
                    for s in range(2):
                        for j in range(PAIRS // 2):
                            h = half * (H // 2) + 2 * j
                            at = (s * PAIRS // 2 + j) * T // 2
                            last = q.transpose(bank[STACK_BANK][:, at:at + T // 2].bitcast(BF16),
                                               src[:, s, h:h + 2, :].rearrange("p h k -> p (h k)"), identb[:, :])
                    last.then_inc(s_st, 1)

                stack(1)
                scores(0)
                if is_seq(t):
                    e.wait_ge(s_mp, t + 1)
                    wait(e, s_p, NC * t - 1)
                    q.transpose(bank[E_BANK[0]][:, 0:T // 2].bitcast(BF16), mparts[:, :], identb[:, :]).then_inc(s_mTp, 1)
                if is_seq(t + 4):
                    b = t + 4
                    e.wait_ge(s_xs, b + 1)
                    wait(e, s_vall, b)
                    q.transpose(bank[W_BANK][:, 0:T], xs[q0][:, :], ident[:, :]).then_inc(s_xsT, 1)
                if is_seq(t - 1):
                    b = t - 1
                    e.wait_ge(s_oT4, b + 1)
                    for i in range(NC):
                        last = q.transpose(bank[O_BANK][:, i * T:(i + 1) * T], oT4[:, i * T:(i + 1) * T], ident[:, :])
                    last.then_inc(s_oq, 1)
                weighted(0)
                weighted(1)
                scores(1)
                if is_seq(t - 1):
                    b = t - 1
                    e.wait_ge(s_on, b + 1)
                    wait(e, s_x1, b)
                    q.transpose(bank[P_BANK][:, 0:T], o[:, :, :].rearrange("p h d -> p (h d)"), ident[:, :]).then_inc(s_oTp, 1)
                if is_seq(t + 4):
                    b = t + 4
                    e.wait_ge(s_hT, b + 1)
                    q.matmul(bank[W_BANK][:, 0:3 * D], hT[q0][:, :], qkvT[:, :], start=True, stop=True).then_inc(s_qkv, 1)
                weighted(2)
                scores(2)
                stack(0)
                if is_seq(t - 1):
                    b = t - 1
                    e.wait_ge(s_oT, b + 1)
                    q.matmul(bank[P_BANK][:, 0:T], projT[:, :], oT[:, :], start=True, stop=True).then_inc(s_proj, 1)
                weighted(3)
                scores(3)
                values(0)
                values(1)
                values(2)
                values(3)
                if is_seq(t - 1):
                    b = t - 1
                    e.wait_ge(s_pr, b + 1)
                    q.transpose(bank[P_BANK][:, 0:D], pr[:, :], ident[:, :]).then_inc(s_prT, 1)

            def step_with_preparation(t, p):
                step(t, p)
                if at(t, -4):
                    prepare_weights()
                if at(t, -2):
                    prepare_biases()
                if at(t, -2):
                    e.wait_ge(pv_v, V_MODS)
                if at(t, -1):
                    e.wait_ge(pv_v, V_DONE)
                    e.wait_ge(pv_a, A_DONE)
                    e.wait_ge(consts, 7)
            steps(e, step_with_preparation, blocks_tensor(e))
            blocks_tensor(e, 1)


_INS = ['x', 'cond_1024', 'fside_BxSx3_0', 'L0_cond_norm1_w', 'L0_cond_qkv_w', 'L0_cond_q_norm_w', 'L0_cond_k_norm_w',
        'L0_cond_proj_w', 'L0_cond_proj_b', 'L0_cond_norm2_w', 'L0_cond_w1', 'L0_cond_w3', 'L0_cond_w2', 'L0_cond_ada_w',
        'L0_cond_ada_b', 'L1_cond_norm_g', 'L1_cond_norm_b', 'L1_cond_Wq', 'L1_cond_bq', 'L1_cond_Wk', 'L1_cond_bk',
        'L1_cond_Wv', 'L1_cond_bv', 'L1_cond_emb_W', 'L1_cond_emb_b', 'L1_cond_sn_g', 'L1_cond_sn_b', 'L1_cond_out_W',
        'L1_cond_out_b']


def kernel(**inputs):
    import numpy as _np
    import concourse.bacc as _bacc
    from concourse import mybir as _mybir
    from concourse.bass_utils import run_bass_kernel_spmd as _run

    nc = _bacc.Bacc("TRN2", target_bir_lowering=False, num_devices=1)
    arrays, args = {}, []
    for name in _INS:
        a = _np.ascontiguousarray(inputs[name])
        arrays[f"in_{name}_dram"] = a
        args.append(nc.dram_tensor(f"in_{name}_dram", a.shape, _mybir.dt.from_np(a.dtype), kind="ExternalInput").ap())
    args.append(nc.dram_tensor("out_0_dram", (B, T, D), _mybir.dt.float32, kind="ExternalOutput").ap())
    dit_then_linear_attention(nc, *args)
    r = _run(nc, [arrays], core_ids=[0])
    return r.results[0]["out_0_dram"]
```
